# Optimizing a Trainium2 kernel written in Bass

```python
import numpy as np
import jax
import jax.numpy as jnp

def _softmax(x, axis=-1):
    return jax.nn.softmax(x, axis=axis)

def _gelu(x):
    return jax.nn.gelu(x, approximate=True)

def _silu(x):
    return jax.nn.silu(x)

def _sigmoid(x):
    return jax.nn.sigmoid(x)

def _layernorm(x, axis=-1, eps=1e-05):
    m = jnp.mean(x, axis=axis, keepdims=True)
    v = jnp.var(x, axis=axis, keepdims=True)
    return (x - m) / jnp.sqrt(v + eps)

def _scatter_add(tgt, idx, src, axis=0):
    return tgt.at[idx].add(src)

def _segment_sum(src, seg, n):
    return jax.ops.segment_sum(src, seg, n)
kernel_name = 'mk_gnn_preln_d4_gnn_r32_319666'

def setup_inputs(seed: int=0):
    np.random.seed(seed)
    _w = jnp.asarray

    def _rec_inputs():
        import jax
        import jax.numpy as jnp
        _gk = jax.random.key(seed)
        x = -0.0009044 + 1 * jax.random.normal(jax.random.fold_in(_gk, 1), (3125, 16), jnp.float32)
        src = jax.random.randint(jax.random.fold_in(_gk, 2), (100000,), 0, 3125, jnp.int32)
        dst = jax.random.randint(jax.random.fold_in(_gk, 3), (100000,), 0, 3125, jnp.int32)
        _o = jnp.argsort(dst, stable=True)
        src = src[_o]
        dst = dst[_o]
        edge_attr_16 = -3.57403e-05 + 0.999761 * jax.random.normal(jax.random.fold_in(_gk, 12), (100000, 16), jnp.float32)
        return (x, src, dst, edge_attr_16)
    x, src, dst, edge_attr_16 = _rec_inputs()

    def _L0_gnn_setup():
        import jax, jax.numpy as jnp
        import numpy as np
        N_NODES = 3125
        N_EDGES = 50000

        def _sage_conv(x, edge_index, W_l, b, W_r, num_nodes):
            src, dst = (edge_index[0], edge_index[1])
            msg_sum = jax.ops.segment_sum(x[src], dst, num_segments=num_nodes)
            deg = jax.ops.segment_sum(jnp.ones((edge_index.shape[1],), x.dtype), dst, num_segments=num_nodes)
            agg = msg_sum / jnp.maximum(deg, 1.0)[:, None]
            return agg @ W_l + b + x @ W_r
        key = jax.random.key(seed)
        ks = jax.random.split(key, 8)
        x = jax.random.normal(ks[0], (N_NODES, 16), dtype=jnp.float32)
        edge_index = jax.random.randint(ks[1], (2, N_EDGES), 0, N_NODES, dtype=jnp.int64)
        s1 = 1.0 / np.sqrt(16.0)
        s2 = 1.0 / np.sqrt(32.0)
        W1_l = jax.random.normal(ks[2], (16, 32), dtype=jnp.float32) * s1
        b1 = jax.random.normal(ks[3], (32,), dtype=jnp.float32) * s1
        W1_r = jax.random.normal(ks[4], (16, 32), dtype=jnp.float32) * s1
        W2_l = jax.random.normal(ks[5], (32, 16), dtype=jnp.float32) * s2
        b2 = jax.random.normal(ks[6], (16,), dtype=jnp.float32) * s2
        W2_r = jax.random.normal(ks[7], (32, 16), dtype=jnp.float32) * s2
        return {'x': x, 'edge_index': edge_index, 'W1_l': W1_l, 'b1': b1, 'W1_r': W1_r, 'W2_l': W2_l, 'b2': b2, 'W2_r': W2_r}
    _L0_gnn_all = _L0_gnn_setup()
    _L0_gnn_in = {k: v for k, v in _L0_gnn_all.items() if k in ('W1_l', 'b1', 'W1_r', 'W2_l', 'b2', 'W2_r')}
    del _L0_gnn_all

    def _L1_gnn_setup():
        import jax, jax.numpy as jnp
        import numpy as np
        N_NODES = 50000
        N_EDGES = 25000
        D_IN = 16

        def gcn_conv(x, edge_index, W, b, n_nodes):
            h = x @ W
            src = jnp.concatenate([edge_index[0], jnp.arange(n_nodes)])
            dst = jnp.concatenate([edge_index[1], jnp.arange(n_nodes)])
            deg = jax.ops.segment_sum(jnp.ones_like(dst, dtype=h.dtype), dst, num_segments=n_nodes)
            deg_inv_sqrt = jnp.where(deg > 0, jax.lax.rsqrt(deg), 0.0)
            norm = deg_inv_sqrt[src] * deg_inv_sqrt[dst]
            msg = h[src] * norm[:, None]
            out = jax.ops.segment_sum(msg, dst, num_segments=n_nodes)
            return out + b
        key = jax.random.key(seed)
        ks = jax.random.split(key, 16)
        d = D_IN
        x = jax.random.normal(ks[0], (N_NODES, d), dtype=jnp.float32)
        edge_index = jax.random.randint(ks[1], (2, N_EDGES), 0, N_NODES, dtype=jnp.int64)

        def glorot(k, fan_in, fan_out):
            s = (6.0 / (fan_in + fan_out)) ** 0.5
            return jax.random.uniform(k, (fan_in, fan_out), jnp.float32, -s, s)
        return {'x': x, 'edge_index': edge_index, 'W1': glorot(ks[2], d, 2 * d), 'b1': jnp.zeros((2 * d,), jnp.float32), 'W2': glorot(ks[3], 2 * d, 4 * d), 'b2': jnp.zeros((4 * d,), jnp.float32), 'W3': glorot(ks[4], 4 * d, 8 * d), 'b3': jnp.zeros((8 * d,), jnp.float32), 'Wl1': glorot(ks[5], 8 * d, 4 * d), 'bl1': jnp.zeros((4 * d,), jnp.float32), 'Wl2': glorot(ks[6], 4 * d, 2 * d), 'bl2': jnp.zeros((2 * d,), jnp.float32), 'Wl3': glorot(ks[7], 2 * d, d), 'bl3': jnp.zeros((d,), jnp.float32)}
    _L1_gnn_all = _L1_gnn_setup()
    _L1_gnn_in = {k: v for k, v in _L1_gnn_all.items() if k in ('W1', 'b1', 'W2', 'b2', 'W3', 'b3', 'Wl1', 'bl1', 'Wl2', 'bl2', 'Wl3', 'bl3')}
    del _L1_gnn_all

    def _L2_gnn_setup():
        import jax, jax.numpy as jnp
        import numpy as np
        STALK_DIM = 16
        N_NODES = 50000
        N_EDGES = 12500
        HIDDEN = 64
        key = jax.random.key(seed)
        k1, k2, k3, k4 = jax.random.split(key, 4)
        d = STALK_DIM
        x = jax.random.normal(k1, (N_NODES, d), dtype=jnp.float32)
        edge_index = jax.random.randint(k2, (2, N_EDGES), 0, N_NODES, dtype=jnp.int64)
        W1 = jax.random.normal(k3, (HIDDEN, 2 * d), dtype=jnp.float32) * (1.0 / np.sqrt(2 * d))
        b1 = jnp.zeros((HIDDEN,), dtype=jnp.float32)
        W2 = jax.random.normal(k4, (d, HIDDEN), dtype=jnp.float32) * (1.0 / np.sqrt(HIDDEN))
        b2 = jnp.zeros((d,), dtype=jnp.float32)
        return {'x': x, 'edge_index': edge_index, 'W1': W1, 'b1': b1, 'W2': W2, 'b2': b2}
    _L2_gnn_all = _L2_gnn_setup()
    _L2_gnn_in = {k: v for k, v in _L2_gnn_all.items() if k in ('W1', 'b1', 'W2', 'b2')}
    del _L2_gnn_all

    def _L3_gnn_setup():
        import jax, jax.numpy as jnp
        import numpy as np
        N_NODES = 30000
        N_EDGES = 9375
        IN_FEATS = 16
        OUT_FEATS = 16
        EDGE_DIM = 16
        key = jax.random.key(seed)
        ks = jax.random.split(key, 8)
        feat = jax.random.normal(ks[0], (N_NODES, IN_FEATS), dtype=jnp.float32)
        efeat = jax.random.normal(ks[1], (N_EDGES, EDGE_DIM), dtype=jnp.float32)
        W_msg = jax.random.normal(ks[2], (EDGE_DIM, IN_FEATS * OUT_FEATS), dtype=jnp.float32) * 0.1
        b_msg = jnp.zeros((IN_FEATS * OUT_FEATS,), dtype=jnp.float32)
        W_attn = jax.random.normal(ks[3], (EDGE_DIM, IN_FEATS * OUT_FEATS), dtype=jnp.float32) * 0.1
        b_attn = jnp.zeros((IN_FEATS * OUT_FEATS,), dtype=jnp.float32)
        src = jax.random.randint(ks[4], (N_EDGES,), 0, N_NODES, dtype=jnp.int32)
        dst = jax.random.randint(ks[5], (N_EDGES,), 0, N_NODES, dtype=jnp.int32)
        return {'feat': feat, 'efeat': efeat, 'W_msg': W_msg, 'b_msg': b_msg, 'W_attn': W_attn, 'b_attn': b_attn, 'src': src, 'dst': dst}
    _L3_gnn_all = _L3_gnn_setup()
    _L3_gnn_in = {k: v for k, v in _L3_gnn_all.items() if k in ('W_msg', 'b_msg', 'W_attn', 'b_attn')}
    del _L3_gnn_all
    return {'x': x, 'src': src, 'dst': dst, 'edge_attr_16': edge_attr_16, 'L0_gnn_W1_l': _L0_gnn_in['W1_l'], 'L0_gnn_b1': _L0_gnn_in['b1'], 'L0_gnn_W1_r': _L0_gnn_in['W1_r'], 'L0_gnn_W2_l': _L0_gnn_in['W2_l'], 'L0_gnn_b2': _L0_gnn_in['b2'], 'L0_gnn_W2_r': _L0_gnn_in['W2_r'], 'L1_gnn_W1': _L1_gnn_in['W1'], 'L1_gnn_b1': _L1_gnn_in['b1'], 'L1_gnn_W2': _L1_gnn_in['W2'], 'L1_gnn_b2': _L1_gnn_in['b2'], 'L1_gnn_W3': _L1_gnn_in['W3'], 'L1_gnn_b3': _L1_gnn_in['b3'], 'L1_gnn_Wl1': _L1_gnn_in['Wl1'], 'L1_gnn_bl1': _L1_gnn_in['bl1'], 'L1_gnn_Wl2': _L1_gnn_in['Wl2'], 'L1_gnn_bl2': _L1_gnn_in['bl2'], 'L1_gnn_Wl3': _L1_gnn_in['Wl3'], 'L1_gnn_bl3': _L1_gnn_in['bl3'], 'L2_gnn_W1': _L2_gnn_in['W1'], 'L2_gnn_b1': _L2_gnn_in['b1'], 'L2_gnn_W2': _L2_gnn_in['W2'], 'L2_gnn_b2': _L2_gnn_in['b2'], 'L3_gnn_W_msg': _L3_gnn_in['W_msg'], 'L3_gnn_b_msg': _L3_gnn_in['b_msg'], 'L3_gnn_W_attn': _L3_gnn_in['W_attn'], 'L3_gnn_b_attn': _L3_gnn_in['b_attn']}

def reference(x, src, dst, edge_attr_16, L0_gnn_W1_l, L0_gnn_b1, L0_gnn_W1_r, L0_gnn_W2_l, L0_gnn_b2, L0_gnn_W2_r, L1_gnn_W1, L1_gnn_b1, L1_gnn_W2, L1_gnn_b2, L1_gnn_W3, L1_gnn_b3, L1_gnn_Wl1, L1_gnn_bl1, L1_gnn_Wl2, L1_gnn_bl2, L1_gnn_Wl3, L1_gnn_bl3, L2_gnn_W1, L2_gnn_b1, L2_gnn_W2, L2_gnn_b2, L3_gnn_W_msg, L3_gnn_b_msg, L3_gnn_W_attn, L3_gnn_b_attn):
    import jax
    import jax.numpy as jnp

    def _L0_gnn_ref(x, edge_index, W1_l, b1, W1_r, W2_l, b2, W2_r):
        import jax, jax.numpy as jnp
        import numpy as np
        N_NODES = 3125
        N_EDGES = 50000

        def _sage_conv(x, edge_index, W_l, b, W_r, num_nodes):
            src, dst = (edge_index[0], edge_index[1])
            msg_sum = jax.ops.segment_sum(x[src], dst, num_segments=num_nodes)
            deg = jax.ops.segment_sum(jnp.ones((edge_index.shape[1],), x.dtype), dst, num_segments=num_nodes)
            agg = msg_sum / jnp.maximum(deg, 1.0)[:, None]
            return agg @ W_l + b + x @ W_r
        n = x.shape[0]
        h = _sage_conv(x, edge_index, W1_l, b1, W1_r, n)
        h = jax.nn.relu(h)
        out = _sage_conv(h, edge_index, W2_l, b2, W2_r, n)
        return out

    def _L1_gnn_ref(x, edge_index, W1, b1, W2, b2, W3, b3, Wl1, bl1, Wl2, bl2, Wl3, bl3):
        import jax, jax.numpy as jnp
        import numpy as np
        N_NODES = 50000
        N_EDGES = 25000
        D_IN = 16

        def gcn_conv(x, edge_index, W, b, n_nodes):
            h = x @ W
            src = jnp.concatenate([edge_index[0], jnp.arange(n_nodes)])
            dst = jnp.concatenate([edge_index[1], jnp.arange(n_nodes)])
            deg = jax.ops.segment_sum(jnp.ones_like(dst, dtype=h.dtype), dst, num_segments=n_nodes)
            deg_inv_sqrt = jnp.where(deg > 0, jax.lax.rsqrt(deg), 0.0)
            norm = deg_inv_sqrt[src] * deg_inv_sqrt[dst]
            msg = h[src] * norm[:, None]
            out = jax.ops.segment_sum(msg, dst, num_segments=n_nodes)
            return out + b
        n = x.shape[0]
        out = jax.nn.relu(gcn_conv(x, edge_index, W1, b1, n))
        out = jax.nn.relu(gcn_conv(out, edge_index, W2, b2, n))
        out = jax.nn.relu(gcn_conv(out, edge_index, W3, b3, n))
        out = jax.nn.relu(out @ Wl1 + bl1)
        out = jax.nn.relu(out @ Wl2 + bl2)
        out = jax.nn.relu(out @ Wl3 + bl3)
        return out

    def _L2_gnn_ref(x, edge_index, W1, b1, W2, b2):
        import jax, jax.numpy as jnp
        import numpy as np
        STALK_DIM = 16
        N_NODES = 50000
        N_EDGES = 12500
        HIDDEN = 64
        d = x.shape[1]
        n = x.shape[0]
        src, dst = (edge_index[0], edge_index[1])
        xs, xd = (x[src], x[dst])

        def reflection(a, b):
            h = jax.nn.relu(jnp.concatenate([a, b], axis=1) @ W1.T + b1)
            return h @ W2.T + b2

        def householder(v):
            vn = v / jnp.maximum(jnp.linalg.norm(v, axis=1, keepdims=True), 1e-12)
            return jnp.eye(d, dtype=v.dtype)[None] - 2.0 * vn[:, :, None] * vn[:, None, :]
        F_s = householder(reflection(xs, xd))
        F_d = householder(reflection(xd, xs))
        L_sd = -jnp.einsum('eki,ekj->eij', F_s, F_d)
        ones_e = jnp.ones(src.shape[0], dtype=x.dtype)
        deg = jnp.zeros(n, dtype=x.dtype).at[src].add(ones_e).at[dst].add(ones_e)
        deg_inv_sqrt = 1.0 / jnp.sqrt(jnp.maximum(deg, 1e-05))
        coef = deg_inv_sqrt[src] * deg_inv_sqrt[dst]
        msg_s = coef[:, None] * jnp.einsum('eij,ej->ei', L_sd, xd)
        msg_d = coef[:, None] * jnp.einsum('eji,ej->ei', L_sd, xs)
        out = x - jnp.zeros_like(x).at[src].add(msg_s) - jnp.zeros_like(x).at[dst].add(msg_d)
        return jax.nn.relu(out)

    def _L3_gnn_ref(feat, efeat, W_msg, b_msg, W_attn, b_attn, src, dst):
        import jax, jax.numpy as jnp
        import numpy as np
        N_NODES = 30000
        N_EDGES = 9375
        IN_FEATS = 16
        OUT_FEATS = 16
        EDGE_DIM = 16
        N, in_f = feat.shape
        E = efeat.shape[0]
        w_m = (efeat @ W_msg + b_msg).reshape(E, in_f, -1)
        w_a = (efeat @ W_attn + b_attn).reshape(E, in_f, -1)
        h_src = feat[src][:, :, None]
        e1 = w_m * h_src
        e2 = w_a * h_src
        seg_max = jax.ops.segment_max(e2, dst, num_segments=N)
        ex = jnp.exp(e2 - seg_max[dst])
        denom = jax.ops.segment_sum(ex, dst, num_segments=N)
        attn = ex / denom[dst]
        ft = jax.ops.segment_sum(e1 * attn, dst, num_segments=N)
        return ft.sum(axis=1)
    edge_index = jnp.stack([src, dst])
    h = jnp.maximum(_layernorm(x, axis=-1), 0.0)
    x = x + _L0_gnn_ref(h, edge_index, L0_gnn_W1_l, L0_gnn_b1, L0_gnn_W1_r, L0_gnn_W2_l, L0_gnn_b2, L0_gnn_W2_r)
    h = jnp.maximum(_layernorm(x, axis=-1), 0.0)
    x = x + _L1_gnn_ref(h, edge_index, L1_gnn_W1, L1_gnn_b1, L1_gnn_W2, L1_gnn_b2, L1_gnn_W3, L1_gnn_b3, L1_gnn_Wl1, L1_gnn_bl1, L1_gnn_Wl2, L1_gnn_bl2, L1_gnn_Wl3, L1_gnn_bl3)
    h = jnp.maximum(_layernorm(x, axis=-1), 0.0)
    x = x + _L2_gnn_ref(h, edge_index, L2_gnn_W1, L2_gnn_b1, L2_gnn_W2, L2_gnn_b2)
    h = jnp.maximum(_layernorm(x, axis=-1), 0.0)
    x = x + _L3_gnn_ref(h, edge_attr_16, L3_gnn_W_msg, L3_gnn_b_msg, L3_gnn_W_attn, L3_gnn_b_attn, src, dst)
    return x

_drawn_inputs = setup_inputs


def setup_inputs(seed=0):
    import zlib

    import numpy as np

    out = dict(_drawn_inputs(seed))
    spreads = {'L1_gnn_b1': (0.0, 0.8),
     'L1_gnn_b2': (0.0, 0.559),
     'L1_gnn_b3': (0.0, 0.492),
     'L1_gnn_bl1': (0.0, 0.324),
     'L1_gnn_bl2': (0.0, 0.38),
     'L1_gnn_bl3': (0.0, 0.1),
     'L2_gnn_b1': (0.0, 2.0),
     'L2_gnn_b2': (0.0, 2.0),
     'L3_gnn_b_msg': (0.0, 0.1),
     'L3_gnn_b_attn': (0.0, 2.0)}
    factors = {'L1_gnn_W1': 8.0, 'L1_gnn_W2': 6.811, 'L2_gnn_W1': 4.852, 'L2_gnn_W2': 4.483}
    for name, (base, spread) in spreads.items():
        noise = np.random.default_rng([zlib.crc32(name.encode()), seed]).standard_normal(out[name].shape)
        drawn = base * np.exp(spread * noise) if base else spread * noise
        out[name] = jnp.asarray(drawn.astype(out[name].dtype))
    for name, factor in factors.items():
        out[name] = (out[name] * factor).astype(out[name].dtype)
    return out
```

```python
from contextlib import ExitStack

import numpy as np

import concourse.bass as bass
from concourse import mybir

F32 = mybir.dt.float32
BF16 = mybir.dt.bfloat16
I32 = mybir.dt.int32
ALU = mybir.AluOpType
ACT = mybir.ActivationFunctionType
AX = mybir.AxisListType

P = 128
N = 3125
E = 100000
D = 16
TILES = -(-N // P)
NP = TILES * P
LANE = 784
EP = P * LANE
PADID = NP - 1
BLOCKS = EP // P
WIN = 64
PAIRS = -(-TILES // 2)
NODES = 16
CHUNK = 8
HALF = CHUNK // 2
HID = 64
BATCH = 8
GROUPS = LANE // BATCH
SPLIT_LANE = E // P
SPLIT_AT = 71
SPLIT_STEPS = SPLIT_LANE // SPLIT_AT
TAIL = E - P * SPLIT_LANE
EA_ROWS = P * SPLIT_LANE + P
LN_EPS = 1e-5
LOWEST = -3.0e38
OFF_MAX = -1.0e30
OFF_EXP = -2.0e38

C_EYE, C_IOTA, C_NODE, C_PART, C_END = 0, 128, 256, 256 + TILES, 256 + TILES + 3


def constants():
    c = np.zeros((P, C_END), np.float32)
    c[:, C_EYE:C_EYE + P] = np.eye(P)
    c[:, C_IOTA:C_IOTA + P] = np.arange(P)[None, :]
    c[:, C_NODE:C_NODE + TILES] = np.arange(TILES)[None, :] * P + np.arange(P)[:, None]
    part = [0] * 16 + [1] * 16 + [2] * 16 + [0] * 16 + [1] * 16 + [0] * 16 + [0, 1, 2]
    for row, which in enumerate(part):
        c[row, C_PART + which] = 1.0
    return c


class Chain:

    def __init__(self, eng, sem, base=0):
        self.eng, self.sem, self.base, self.n = eng, sem, base, 0

    def __call__(self, ins):
        ins.then_inc(self.sem, 1)
        self.n += 1

    def sync(self):
        self.eng.wait_ge(self.sem, self.base + self.n)

    def step(self, ins):
        self(ins)
        self.sync()

    def publish(self, ins, sem, value):
        ins.then_inc(sem, 1)
        self.eng.wait_ge(sem, value)


def settled(eng, reg, sem, value):
    eng.reg_mov(reg, value)
    value = eng.snap(reg)
    eng.wait_ge(sem, 1)
    return value


class Scope:

    def __init__(self, nc, ctx, tag):
        self.nc, self.ctx, self.tag = nc, ctx, tag

    def sb(self, name, shape, dt=F32):
        return self.ctx.enter_context(self.nc.sbuf_tensor(f"{self.tag}_{name}", shape, dt))

    def ps(self, name, shape, dt=F32):
        return self.ctx.enter_context(self.nc.psum_tensor(f"{self.tag}_{name}", shape, dt))

    def sem(self, name):
        return self.ctx.enter_context(self.nc.semaphore(f"{self.tag}_{name}"))


def spread(ap, shape):
    while len(ap.shape) < len(shape):
        ap = ap.unsqueeze(len(ap.shape))
    return ap.broadcast_to(shape)


def stage_pad(nc, g, ins):
    with ExitStack() as ctx:
        s = Scope(nc, ctx, "pad")
        pad_ids = s.sb("pad_ids", [32, (EP - E) // 32], I32)
        loaded, pad_set, stored = s.sem("loaded"), s.sem("pad_set"), s.sem("stored")
        with nc.Block() as block:
            @block.gpsimd
            def _(pool):
                pool.memset(pad_ids[:], PADID).then_inc(pad_set, 1)

            @block.sync
            def _(sp):
                sp.dma_start(g.const[:], ins["constants"]).then_inc(loaded, 16)
                sp.dma_start(g.x[:, 0:TILES - 1, :],
                             ins["x"][0:(TILES - 1) * P, :].rearrange("(t p) d -> p t d", p=P)).then_inc(loaded, 16)
                for real, padded in ((ins["src"], g.src_d), (ins["dst"], g.dst_d)):
                    sp.dma_start(padded[0:E].rearrange("(a b) -> a b", a=32),
                                 real.rearrange("(a b) -> a b", a=32)).then_inc(stored, 16)
                sp.wait_ge(pad_set, 1)
                for padded in (g.src_d, g.dst_d):
                    sp.dma_start(padded[E:EP].rearrange("(a b) -> a b", a=32), pad_ids[:]).then_inc(stored, 16)
                sp.wait_ge(stored, 64)
                sp.wait_ge(loaded, 32)
            x_zeroed, x_tail = s.sem("x_zeroed"), s.sem("x_tail")

            @block.vector
            def _(dve):
                dve.memset(g.x[:, TILES - 1, :], 0.0).then_inc(x_zeroed, 1)
                dve.wait_ge(loaded, 32)
                dve.tensor_copy(g.eye_bf[:], g.const[:, C_EYE:C_EYE + P]).then_inc(x_zeroed, 1)
                dve.tensor_copy(g.iota_bf[:], g.const[:, C_IOTA:C_IOTA + P]).then_inc(x_zeroed, 1)

            @block.scalar
            def _(act):
                act.wait_ge(x_zeroed, 1)
                rest = N - (TILES - 1) * P
                act.dma_start(g.x[0:rest, TILES - 1, :], ins["x"][(TILES - 1) * P:N, :]).then_inc(x_tail, 16)
                act.wait_ge(x_tail, 16)


def stage_split(nc, g, ins):
    steps = SPLIT_STEPS + 1
    with ExitStack() as ctx:
        s = Scope(nc, ctx, "split")
        ea = [s.sb(f"ea{b}", [P, SPLIT_AT, D]) for b in range(2)]
        rest1 = [s.sb(f"rest1{b}", [P, SPLIT_AT, D]) for b in range(2)]
        rest2 = [s.sb(f"rest2{b}", [P, SPLIT_AT, D]) for b in range(2)]
        out = [s.sb(f"out{b}", [P, SPLIT_AT, P], BF16) for b in range(2)]
        loaded = [s.sem(f"loaded{b}") for b in range(2)]
        stored = [s.sem(f"stored{b}") for b in range(2)]
        set_up, part1, left1, part2, left2, part3 = map(s.sem, ("set_up", "part1", "left1", "part2", "left2", "part3"))
        tail_zeroed = s.sem("tail_zeroed")
        main = ins["edge_attr_16"][0:P * SPLIT_LANE, :].rearrange("(p t) d -> p t d", p=P)
        main_out = g.ea6_d[0:P * SPLIT_LANE, :].rearrange("(p t) k -> p t k", p=P)

        with nc.Block() as block:
            @block.sync
            def _(sp):
                for k in range(steps):
                    b = k % 2
                    if k >= 2:
                        sp.wait_ge(part2, k - 1)
                    if k < SPLIT_STEPS:
                        sp.dma_start(ea[b][:], main[:, k * SPLIT_AT:(k + 1) * SPLIT_AT, :]).then_inc(loaded[b], 16)
                    else:
                        sp.wait_ge(tail_zeroed, 1)
                        sp.dma_start(ea[b][0:TAIL, 0, :], ins["edge_attr_16"][P * SPLIT_LANE:E, :]).then_inc(loaded[b], 16)

            @block.gpsimd
            def _(pool):
                for b in range(2):
                    pool.memset(out[b][:, :, 6 * D:P], 0.0).then_inc(set_up, 1)
                pool.wait_ge(set_up, 2)
                for b in range(2):
                    pool.memset(out[b][:, :, 6 * D:6 * D + 3], 1.0).then_inc(set_up, 1)
                pool.wait_ge(set_up, 4)
                for k in range(steps):
                    b = k % 2
                    pool.wait_ge(part3, k + 1)
                    if k < SPLIT_STEPS:
                        pool.dma_start(main_out[:, k * SPLIT_AT:(k + 1) * SPLIT_AT, :], out[b][:]).then_inc(stored[b], 16)
                    else:
                        pool.dma_start(g.ea6_d[P * SPLIT_LANE:EA_ROWS, :], out[b][:, 0, :]).then_inc(stored[b], 16)
                for b in range(2):
                    pool.wait_ge(stored[b], 16 * len(range(b, steps, 2)))

            @block.scalar
            def _(act):
                for k in range(steps):
                    b, n = k % 2, SPLIT_AT if k < SPLIT_STEPS else 1
                    act.wait_ge(loaded[b], 16 * (k // 2 + 1))
                    if k >= 2:
                        act.wait_ge(stored[b], 16 * (k // 2))
                    rows = out[b][:, 0:n, :]
                    act.activation(rows[:, :, 0:3 * D].rearrange("p t (c d) -> p t c d", c=3),
                                   ea[b][:, 0:n, :].unsqueeze(2).broadcast_to([P, n, 3, D]), ACT.Copy).then_inc(part1, 1)
                    act.wait_ge(left1, k + 1)
                    act.activation(rows[:, :, 3 * D:5 * D].rearrange("p t (c d) -> p t c d", c=2),
                                   rest1[b][:, 0:n, :].unsqueeze(2).broadcast_to([P, n, 2, D]), ACT.Copy).then_inc(part2, 1)
                    act.wait_ge(left2, k + 1)
                    act.activation(rows[:, :, 5 * D:6 * D], rest2[b][:, 0:n, :], ACT.Copy).then_inc(part3, 1)

            @block.vector
            def _(dve):
                for k in range(steps):
                    b, n = k % 2, SPLIT_AT if k < SPLIT_STEPS else 1
                    if k >= 2:
                        dve.wait_ge(part3, k - 1)
                    dve.wait_ge(part1, k + 1)
                    dve.tensor_tensor(rest1[b][:, 0:n, :], ea[b][:, 0:n, :], out[b][:, 0:n, 0:D],
                                      ALU.subtract).then_inc(left1, 1)
                    dve.wait_ge(part2, k + 1)
                    dve.wait_ge(left1, k + 1)
                    dve.tensor_tensor(rest2[b][:, 0:n, :], rest1[b][:, 0:n, :], out[b][:, 0:n, 3 * D:4 * D],
                                      ALU.subtract).then_inc(left2, 1)
                    if k == SPLIT_STEPS - 2:
                        dve.wait_ge(left1, k + 1)
                        dve.memset(ea[SPLIT_STEPS % 2][:, 0, :], 0.0).then_inc(tail_zeroed, 1)


def stage_offsets(nc, g):
    with ExitStack() as ctx:
        s = Scope(nc, ctx, "off")
        lasts_i = s.sb("lasts_i", [1, BLOCKS], I32)
        lasts = s.sb("lasts", [1, BLOCKS])
        ones = s.sb("ones", [1, P])
        lasts_bc = s.sb("lasts_bc", [P, BLOCKS])
        junk = s.sb("junk", [P, BLOCKS])
        below = s.sb("below", [P, TILES])
        block_at = s.sb("block_at", [P, TILES], I32)
        window_i = s.sb("window_i", [P, TILES, P], I32)
        window = s.sb("window", [P, TILES, P])
        inside = s.sb("inside", [P, TILES])
        last_row = s.sb("last_row", [1, 1])
        most_t = s.sb("most_t", [TILES, 1])
        most_f = s.sb("most_f", [1, TILES])
        most_all = s.sb("most_all", [1, 2])
        counts = s.sb("counts", [1, TILES + 2], I32)
        bc_ps = [s.ps(f"bc{b}", [P, 512]) for b in range(2)]
        deg_ps = s.ps("deg_ps", [TILES, P])
        row_ps = s.ps("row_ps", [1, TILES])
        lasts_in, dve_n, spread_done, windows_in, firsts_out, next_in, pe_deg = map(
            s.sem, ("lasts_in", "dve_n", "spread_done", "windows_in", "firsts_out", "next_in", "pe_deg"))
        half = BLOCKS // 2

        with nc.Block() as block:
            @block.sync
            def _(sp):
                sp.dma_start(lasts_i[:], g.dst_d[:].rearrange("(b e) -> b e", e=P)[:, P - 1:P]
                             .rearrange("b e -> e b"), allow_slow_non_contiguous=True).then_inc(lasts_in, 16)
                sp.wait_ge(dve_n, SET + LASTS + COUNTED)
                sp.dma_start(g.first_d[0:NP].rearrange("(t p) -> p t", p=P), g.first[:],
                             allow_slow_non_contiguous=True).then_inc(firsts_out, 16)
                sp.dma_start(g.first_d[NP:NP + 1].rearrange("(a b) -> a b", a=1), last_row[:]).then_inc(firsts_out, 16)
                sp.wait_ge(firsts_out, 32)
                sp.dma_start(g.deg[:], g.first_d[1:NP + 1].rearrange("(t p) -> p t", p=P),
                             allow_slow_non_contiguous=True).then_inc(next_in, 16)
                sp.wait_ge(next_in, 16)

            @block.tensor
            def _(pe):
                pe.wait_ge(dve_n, SET + LASTS)
                for b in range(2):
                    pe.matmul(bc_ps[b][:, 0:half], ones[:], lasts[:, b * half:(b + 1) * half],
                              start=True, stop=True).then_inc(spread_done, 1)
                pe.wait_ge(dve_n, SET + LASTS + COUNTED + 1)
                pe.transpose(deg_ps[:], g.deg[:], g.const[:, C_EYE:C_EYE + P]).then_inc(pe_deg, 1)
                pe.wait_ge(dve_n, SET + LASTS + COUNTED + 2)
                pe.transpose(row_ps[:], most_t[:], g.const[0:TILES, C_EYE:C_EYE + TILES]).then_inc(pe_deg, 1)

            @block.gpsimd
            def _(pool):
                pool.wait_ge(dve_n, SET + LASTS + 2 + TILES + 1)
                for t in range(TILES):
                    pool.indirect_dma_start(window_i[:, t, :], None, g.dst_d[:].rearrange("(b e) -> b e", e=P),
                                            bass.IndirectOffsetOnAxis(block_at[:, t:t + 1], 0)).then_inc(windows_in, 16)
                pool.wait_ge(windows_in, 16 * TILES)

            @block.vector
            def _(dve):
                c = Chain(dve, dve_n)
                c(dve.memset(ones[:], 1.0))
                c(dve.memset(last_row[:], float(E)))
                dve.wait_ge(lasts_in, 16)
                c.step(dve.tensor_copy(lasts[:], lasts_i[:]))
                dve.wait_ge(spread_done, 2)
                for b in range(2):
                    c(dve.tensor_copy(lasts_bc[:, b * half:(b + 1) * half], bc_ps[b][:, 0:half]))
                c.sync()
                for t in range(TILES):
                    c.step(dve.tensor_scalar(junk[:], lasts_bc[:], g.const[:, C_NODE + t:C_NODE + t + 1], 0.0,
                                             ALU.is_lt, ALU.add, accum_out=below[:, t:t + 1]))
                c.step(dve.tensor_copy(block_at[:], below[:]))
                dve.wait_ge(windows_in, 16 * TILES)
                c.step(dve.tensor_copy(window[:], window_i[:]))
                for t in range(TILES):
                    c.step(dve.tensor_scalar(junk[:, 0:P], window[:, t, :], g.const[:, C_NODE + t:C_NODE + t + 1], 0.0,
                                             ALU.is_lt, ALU.add, accum_out=inside[:, t:t + 1]))
                c.step(dve.scalar_tensor_tensor(out=g.first[:], in0=below[:], scalar=float(P), in1=inside[:],
                                                op0=ALU.mult, op1=ALU.add))
                assert c.n == SET + LASTS + COUNTED
                dve.wait_ge(next_in, 16)
                c.step(dve.tensor_tensor(g.deg[:], g.deg[:], g.first[:], ALU.subtract))
                dve.wait_ge(pe_deg, 1)
                c.step(dve.tensor_reduce(most_t[:], deg_ps[:], AX.X, ALU.max))
                dve.wait_ge(pe_deg, 2)
                c.step(dve.tensor_copy(most_f[:], row_ps[:]))
                c.step(dve.tensor_reduce(most_all[:, 0:1], most_f[:], AX.X, ALU.max))
                c.step(dve.tensor_scalar(most_f[:], most_f[:], float(CHUNK + 1), float(CHUNK - 1), ALU.max, ALU.add))
                c.step(dve.tensor_scalar(most_all[:, 1:2], most_all[:, 0:1], 1.0, float(WIN - 1), ALU.max, ALU.add))
                c.step(dve.tensor_copy(counts[:, 0:TILES], most_f[:]))
                c.step(dve.tensor_copy(counts[:, TILES:TILES + 1], most_all[:, 1:2]))
                c.step(dve.tensor_scalar(g.loops[:, 0:TILES], counts[:, 0:TILES], CHUNK.bit_length() - 1, None,
                                         ALU.arith_shift_right))
                c.step(dve.tensor_scalar(g.loops[:, TILES:TILES + 1], counts[:, TILES:TILES + 1],
                                         WIN.bit_length() - 1, None, ALU.arith_shift_right))
                c.step(dve.tensor_copy(most_f[:], g.loops[:, 0:TILES]))
                c.step(dve.tensor_reduce(most_all[:, 0:1], most_f[:], AX.X, ALU.add))
                c.step(dve.tensor_scalar(most_all[:, 0:1], most_all[:, 0:1], -1.0, None, ALU.add))
                c.step(dve.tensor_copy(g.loops[:, TILES + 1:TILES + 2], most_all[:, 0:1]))


SET, LASTS = 2, 1
COUNTED = 2 + TILES + 1 + 1 + TILES + 1


def stage_adjacency(nc, g):
    with ExitStack() as ctx:
        s = Scope(nc, ctx, "adj")
        at = s.sb("at", [P, TILES])
        at_i = s.sb("at_i", [P, TILES], I32)
        left = s.sb("left", [P, 2 * PAIRS])
        ids = s.sb("ids", [P, 2 * PAIRS, WIN], I32)
        ids2 = s.sb("ids2", [P, 2 * PAIRS, WIN], I32)
        outside = s.sb("outside", [P, 2 * PAIRS, WIN], BF16)
        lo_rows = s.sb("lo_rows", [P, 2 * PAIRS, WIN], BF16)
        hi_rows = s.sb("hi_rows", [P, 2 * PAIRS, WIN], BF16)
        lo_t = s.sb("lo_t", [P, PAIRS * P], BF16)
        hi_t = s.sb("hi_t", [P, PAIRS * P], BF16)
        hot_lo = [s.sb(f"hot_lo{b}", [P, NODES, P], BF16) for b in range(2)]
        hot_hi = [s.sb(f"hot_hi{b}", [P, NODES, TILES], BF16) for b in range(2)]
        ps = [[s.ps(f"ps{b}{h}", [P, NODES * TILES]) for h in range(2)] for b in range(2)]
        ps_t = s.ps("ps_t", [P, 2, P], BF16)
        turns = P // NODES // 2

        prepared, windows_in, rows_ready, turned, copied, hot_lo_n = map(
            s.sem, ("prepared", "windows_in", "rows_ready", "turned", "copied", "hot_lo_n"))
        hot_ready = [s.sem(f"hot_ready{b}") for b in range(2)]
        column_ready = [s.sem(f"column_ready{b}") for b in range(2)]
        moved = [[s.sem(f"moved{b}{h}") for h in range(2)] for b in range(2)]

        def each_group(eng, body):
            with eng.Fori(0, TILES // 2) as q:
                with eng.Fori(0, turns) as j:
                    for b in range(2):
                        body(b, (0, 1), q * turns + j, q, j)
            q = TILES // 2
            with eng.Fori(0, turns) as j:
                for b in range(2):
                    body(b, (0,), j + q * turns, q, j)

        with nc.Block() as block:
            @block.gpsimd
            def _(pool):
                pool.wait_ge(prepared, 3)
                for t in range(TILES):
                    pool.indirect_dma_start(ids[:, t, :], None, g.src_d[:].rearrange("(e o) -> e o", o=1),
                                            bass.IndirectOffsetOnAxis(at_i[:, t:t + 1], 0)).then_inc(windows_in, 16)
                pool.wait_ge(windows_in, 16 * TILES)

            @block.vector
            def _(dve):
                c = Chain(dve, prepared)
                c(dve.memset(left[:], 0.0))
                c(dve.tensor_copy(at[:], g.first[:]))
                c.sync()
                c.step(dve.tensor_copy(at_i[:], at[:]))
                c(dve.tensor_copy(left[:, 0:TILES], g.deg[:]))
                c(dve.memset(ids[:, TILES:2 * PAIRS, :], 0))
                c.sync()
                c.step(dve.tensor_tensor(outside[:], g.const[:, C_IOTA:C_IOTA + WIN].unsqueeze(1)
                                         .broadcast_to([P, 2 * PAIRS, WIN]),
                                         spread(left[:], [P, 2 * PAIRS, WIN]), ALU.is_ge))
                dve.wait_ge(windows_in, 16 * TILES)
                c.step(dve.tensor_scalar(ids2[:], ids[:], P - 1, None, ALU.bitwise_and))
                c.step(dve.tensor_copy(lo_rows[:], ids2[:]))
                c.step(dve.tensor_scalar(ids2[:], ids[:], P.bit_length() - 1, None, ALU.arith_shift_right))
                dve.scalar_tensor_tensor(out=hi_rows[:], in0=outside[:], scalar=100.0, in1=ids2[:],
                                         op0=ALU.mult, op1=ALU.add).then_inc(rows_ready, 1)
                for q in range(PAIRS):
                    dve.wait_ge(turned, q + 1)
                    dve.tensor_copy(lo_t[:, q * P:(q + 1) * P], ps_t[:, 0, :]).then_inc(copied, 1)
                    dve.tensor_copy(hi_t[:, q * P:(q + 1) * P], ps_t[:, 1, :]).then_inc(copied, 1)
                dve.wait_ge(copied, 2 * PAIRS)

                def hot(b, halves, i, q, j):
                    dve.wait_ge(column_ready[b], i)
                    dve.wait_ge(hot_ready[b], i)
                    col = q * P + j * (2 * NODES) + b * NODES
                    for n in range(NODES):
                        dve.tensor_scalar(hot_lo[b][:, n, :], g.iota_bf[:], lo_t[:, bass.ds(col + n, 1)], None, ALU.is_equal)
                    dve.tensor_tensor(hot_hi[b][:], spread(hi_t[:, bass.ds(col, NODES)], [P, NODES, TILES]),
                                      g.iota_bf[:, 0:TILES].unsqueeze(1).broadcast_to([P, NODES, TILES]),
                                      ALU.is_equal).then_inc(hot_ready[b], 1)

                each_group(dve, hot)

            @block.tensor
            def _(pe):
                pe.wait_ge(rows_ready, 1)
                for q in range(PAIRS):
                    if q:
                        pe.wait_ge(copied, 2 * q)
                    pe.transpose(ps_t[:, 0, :], lo_rows[:, 2 * q:2 * q + 2, :].rearrange("p t w -> p (t w)"), g.eye_bf[:])
                    pe.transpose(ps_t[:, 1, :], hi_rows[:, 2 * q:2 * q + 2, :].rearrange("p t w -> p (t w)"),
                                 g.eye_bf[:]).then_inc(turned, 1)

                def products(b, halves, i, q, j):
                    pe.wait_ge(hot_ready[b], i + 1)
                    for h in halves:
                        pe.wait_ge(moved[b][h], i)
                    for n in range(NODES):
                        for h in halves:
                            mm = pe.matmul(ps[b][h][:, n * TILES:(n + 1) * TILES],
                                           hot_lo[b][h * WIN:(h + 1) * WIN, n, :],
                                           hot_hi[b][h * WIN:(h + 1) * WIN, n, :], start=True, stop=True)
                    mm.then_inc(column_ready[b], 1)

                each_group(pe, products)

            @block.scalar
            def _(act):
                def move(b, halves, i, q, j):
                    act.wait_ge(column_ready[b], i + 1)
                    for h in halves:
                        node = q * (2 * P) + j * (2 * NODES) + (b * NODES + h * P)
                        act.activation(g.A[:, :, bass.ds(node, NODES)],
                                       ps[b][h][:].rearrange("p (n s) -> p s n", n=NODES), ACT.Copy).then_inc(moved[b][h], 1)

                each_group(act, move)


def norm(dve, c, g, out, x, root_asked, root_done, asked):
    shape = [P, TILES, D]
    c.step(dve.tensor_reduce(g.mean[:], x, AX.X, ALU.add))
    c.step(dve.tensor_scalar(g.mean[:], g.mean[:], 1.0 / D, None, ALU.mult))
    c.step(dve.tensor_tensor(g.centred[:], x, spread(g.mean[:], shape), ALU.subtract))
    c.step(dve.tensor_tensor(g.squares[:], g.centred[:], g.centred[:], ALU.mult))
    c.step(dve.tensor_reduce(g.mean[:], g.squares[:], AX.X, ALU.add))
    c.step(dve.tensor_scalar(g.root_in[:], g.mean[:], 1.0 / D, LN_EPS, ALU.mult, ALU.add))
    asked[0] += 1
    dve.engine_nop().then_inc(root_asked, 1)
    dve.wait_ge(root_done, asked[0])
    c.step(dve.reciprocal(g.mean[:], g.root_in[:]))
    c.step(dve.tensor_tensor(out, g.centred[:], spread(g.mean[:], shape), ALU.mult))
    c.step(dve.tensor_scalar(out, out, 0.0, None, ALU.max))


class NodeOps:

    def __init__(self, dve, act_sem, chain):
        self.dve, self.c = dve, chain

    def tt(self, out, a, b, op):
        self.c.step(self.dve.tensor_tensor(out, a, b, op))

    def ts(self, out, a, s1, s2, op0, op1=None):
        self.c.step(self.dve.tensor_scalar(out, a, s1, s2, op0, op1) if op1 is not None
                    else self.dve.tensor_scalar(out, a, s1, None, op0))

    def reduce(self, out, a, op=ALU.add):
        self.c.step(self.dve.tensor_reduce(out, a, AX.X, op))


DENSE_TILES = 4
DENSE_STEPS = -(-TILES // DENSE_TILES)


def stage_layers01(nc, g, ins, debug=None):
    with ExitStack() as ctx:
        s = Scope(nc, ctx, "n01")
        dims = [(2 * D, 32), (64, D), (D, 32), (32, 64), (64, P), (P, 64), (64, 32), (32, D)]
        names = ["L0_gnn_b1", "L0_gnn_b2", "L1_gnn_b1", "L1_gnn_b2", "L1_gnn_b3", "L1_gnn_bl1", "L1_gnn_bl2", "L1_gnn_bl3"]
        weights = [[("L0_gnn_W1_l", 0, D), ("L0_gnn_W1_r", D, 2 * D)], [("L0_gnn_W2_l", 0, 32), ("L0_gnn_W2_r", 32, 64)],
                   [("L1_gnn_W1", 0, D)], [("L1_gnn_W2", 0, 32)], [("L1_gnn_W3", 0, 64)],
                   [("L1_gnn_Wl1", 0, P)], [("L1_gnn_Wl2", 0, 64)], [("L1_gnn_Wl3", 0, 32)]]
        widths = [D, 32, D, 32, 64]
        W = [s.sb(f"W{d}", [k, o]) for d, (k, o) in enumerate(dims)]
        bias = [s.sb(f"bias{d}", [P, o]) for d, (k, o) in enumerate(dims)]
        feat = s.sb("feat", [P, TILES, P])
        cat = s.sb("cat", [P, TILES, 64])
        rest = summed = feat[:, :, 64:P]
        parts = s.sb("parts", [P, TILES, 3, 64], BF16)
        inv_deg = s.sb("inv_deg", [P, TILES])
        dinv = s.sb("dinv", [P, TILES])
        junk = s.sb("junk", [P, NP], BF16)
        turned_sb = [s.sb(f"turned_sb{b}", [P, DENSE_TILES * P]) for b in range(2)]
        agg_ps = [s.ps(f"agg_ps{b}", [P, 512]) for b in range(2)]
        turn_ps = [s.ps(f"turn_ps{b}", [P, 512]) for b in range(2)]
        out_ps = [s.ps(f"out_ps{b}", [P, 512]) for b in range(2)]
        weights_in, dve_n, parts_ready, input_ready, turned, copied, dense_done, added = map(
            s.sem, ("weights_in", "dve_n", "parts_ready", "input_ready", "turned", "copied", "dense_done", "added"))
        agg_done = [s.sem(f"agg_done{b}") for b in range(2)]
        agg_read = [s.sem(f"agg_read{b}") for b in range(2)]
        out_done, root_asked, root_done = s.sem("out_done"), s.sem("root_asked"), s.sem("root_done")
        agg_order = {0: 0, 1: 1, 2: 2, 3: 3, 4: 4}
        even, odd = (TILES + 1) // 2, TILES // 2

        def parts_view(a):
            w = widths[a]
            return parts[:].rearrange("p t s f -> p (t s f)")[:, 0:TILES * 3 * w].rearrange("p (t k) -> p t k", t=TILES)

        def tiles_of(step):
            return range(step * DENSE_TILES, min(TILES, (step + 1) * DENSE_TILES))

        with nc.Block() as block:
            @block.sync
            def _(sp):
                n = 0
                for d, rows in enumerate(weights):
                    for name, a, b in rows:
                        sp.dma_start(W[d][a:b, :], ins[name]).then_inc(weights_in, 16)
                        n += 1
                for d, name in enumerate(names):
                    o = dims[d][1]
                    sp.dma_start(bias[d][:], ins[name].unsqueeze(0).broadcast_to([P, o])).then_inc(weights_in, 16)
                    n += 1
                sp.wait_ge(weights_in, 16 * n)
                assert n == LOADS

            @block.tensor
            def _(pe):
                pe.wait_ge(weights_in, 16 * LOADS)

                def aggregate(a):
                    w = widths[a]
                    pe.wait_ge(parts_ready, a + 1)

                    def tile(b, i, t):
                        pe.wait_ge(agg_read[b], i)
                        for shi in range(TILES):
                            mm = pe.matmul(agg_ps[b][:, 0:3 * w], g.A[:, shi, bass.ds(t * P, P)],
                                           parts_view(a)[:, shi, :], start=shi == 0, stop=shi == TILES - 1)
                        mm.then_inc(agg_done[b], 1)

                    with pe.Fori(0, TILES // 2) as i:
                        for b in range(2):
                            tile(b, i + a * (even if b == 0 else odd), i * 2 + b)
                    tile(0, TILES // 2 + a * even, TILES - 1)

                def dense(d):
                    k, o = dims[d]
                    source = cat if d < 5 else feat
                    for step in range(DENSE_STEPS):
                        n = d * DENSE_STEPS + step
                        b = n % 2
                        tiles = tiles_of(step)
                        if step == 0:
                            pe.wait_ge(input_ready, d + 1)
                        if n >= 2:
                            pe.wait_ge(copied, n - 1)
                        for t in tiles:
                            mm = pe.transpose(turn_ps[b][0:k, (t - tiles[0]) * P:(t - tiles[0] + 1) * P],
                                              source[:, t, 0:k], g.const[:, C_EYE:C_EYE + P])
                        mm.then_inc(turned, 1)
                        if step:
                            products(d, step - 1)
                    products(d, DENSE_STEPS - 1)

                def products(d, step):
                    k, o = dims[d]
                    n = d * DENSE_STEPS + step
                    b = n % 2
                    tiles = tiles_of(step)
                    pe.wait_ge(copied, n + 1)
                    if n >= 2:
                        pe.wait_ge(added, n - 1)
                    for t in tiles:
                        at = t - tiles[0]
                        mm = pe.matmul(out_ps[b][:, at * o:(at + 1) * o], turned_sb[b][0:k, at * P:(at + 1) * P],
                                       W[d][:], start=True, stop=True)
                    mm.then_inc(dense_done, 1)

                for d in range(len(dims)):
                    if d < 5:
                        aggregate(d)
                    dense(d)

            @block.scalar
            def _(act):
                def outs(d):
                    for shi in range(5 * d, 5 * d + 5):
                        if shi:
                            act.wait_ge(out_done, shi)
                        act.activation(junk[:], g.A[:, shi, :], ACT.Copy,
                                       accum_out=g.outs[:, shi:shi + 1]).then_inc(out_done, 1)

                def roots(n):
                    act.wait_ge(root_asked, n)
                    act.activation(g.root_in[:], g.root_in[:], ACT.Sqrt).then_inc(root_done, 1)

                def copies(d):
                    k = dims[d][0]
                    for step in range(DENSE_STEPS):
                        n = d * DENSE_STEPS + step
                        b, tiles = n % 2, tiles_of(step)
                        act.wait_ge(turned, n + 1)
                        if n >= 2:
                            act.wait_ge(dense_done, n - 1)
                        act.activation(turned_sb[b][0:k, 0:len(tiles) * P], turn_ps[b][0:k, 0:len(tiles) * P],
                                       ACT.Copy).then_inc(copied, 1)

                roots(1)
                for d in range(8):
                    if d == 2:
                        roots(2)
                        roots(3)
                    if d < 5:
                        outs(d)
                    copies(d)
                roots(4)
                roots(5)

            @block.vector
            def _(dve):
                c = Chain(dve, dve_n)
                ops = NodeOps(dve, None, c)
                asked = [0]

                def norm_relu(out, x):
                    norm(dve, c, g, out, x, root_asked, root_done, asked)

                def aggregate(a, source):
                    w = widths[a]
                    p3 = parts_view(a)
                    for part in range(3):
                        now = p3[:, :, part * w:(part + 1) * w]
                        cur = source if part == 0 else rest[:, :, 0:w]
                        ins_ = dve.tensor_copy(now, cur)
                        if part == 2:
                            ins_.then_inc(parts_ready, 1)
                        else:
                            c.step(ins_)
                            ops.tt(rest[:, :, 0:w], cur, now, ALU.subtract)

                    def tile(b, i, t):
                        dve.wait_ge(agg_done[b], i + 1)
                        dve.tensor_reduce(summed[:, bass.ds(t, 1), 0:w],
                                          agg_ps[b][:, 0:3 * w].rearrange("p (s f) -> p f s", f=w), AX.X,
                                          ALU.add).then_inc(agg_read[b], 1)

                    with dve.Fori(0, TILES // 2) as i:
                        for b in range(2):
                            tile(b, i + a * (even if b == 0 else odd), i * 2 + b)
                    tile(0, TILES // 2 + a * even, TILES - 1)
                    dve.wait_ge(agg_read[0], (a + 1) * even)
                    dve.wait_ge(agg_read[1], (a + 1) * odd)

                def dense(d, relu):
                    k, o = dims[d]
                    dve.engine_nop().then_inc(input_ready, 1)
                    for step in range(DENSE_STEPS):
                        n = d * DENSE_STEPS + step
                        b, tiles = n % 2, tiles_of(step)
                        dve.wait_ge(dense_done, n + 1)
                        m = len(tiles)
                        dve.tensor_tensor(feat[:, tiles[0]:tiles[0] + m, 0:o],
                                          out_ps[b][:, 0:m * o].rearrange("p (t o) -> p t o", o=o),
                                          bias[d][:].unsqueeze(1).broadcast_to([P, m, o]), ALU.add).then_inc(added, 1)
                    dve.wait_ge(added, (d + 1) * DENSE_STEPS)
                    if relu:
                        ops.ts(feat[:, :, 0:o], feat[:, :, 0:o], 0.0, None, ALU.max)

                dve.wait_ge(weights_in, 16 * LOADS)
                norm_relu(g.h[:], g.x[:])
                ops.ts(inv_deg[:], g.deg[:], 1.0, None, ALU.max)
                c.step(dve.reciprocal(inv_deg[:], inv_deg[:]))
                aggregate(0, g.h[:])
                ops.tt(cat[:, :, 0:D], summed[:, :, 0:D], spread(inv_deg[:], [P, TILES, D]), ALU.mult)
                ops.ts(cat[:, :, D:2 * D], g.h[:], 0.0, None, ALU.add)
                dense(0, True)
                aggregate(1, feat[:, :, 0:32])
                ops.tt(cat[:, :, 0:32], summed[:, :, 0:32], spread(inv_deg[:], [P, TILES, 32]), ALU.mult)
                ops.ts(cat[:, :, 32:64], feat[:, :, 0:32], 0.0, None, ALU.add)
                dense(1, False)
                ops.tt(g.x[:], g.x[:], feat[:, :, 0:D], ALU.add)
                norm_relu(g.h[:], g.x[:])
                ops.ts(g.root_in[:], g.deg[:], 1.0, None, ALU.add)
                asked[0] += 1
                dve.engine_nop().then_inc(root_asked, 1)
                dve.wait_ge(root_done, asked[0])
                c.step(dve.reciprocal(dinv[:], g.root_in[:]))
                source = g.h[:]
                for a in (2, 3, 4):
                    w = widths[a]
                    scale = spread(dinv[:], [P, TILES, w])
                    ops.tt(cat[:, :, 0:w], source, scale, ALU.mult)
                    aggregate(a, cat[:, :, 0:w])
                    ops.tt(cat[:, :, 0:w], cat[:, :, 0:w], summed[:, :, 0:w], ALU.add)
                    ops.tt(cat[:, :, 0:w], cat[:, :, 0:w], scale, ALU.mult)
                    dense(a, True)
                    source = feat[:, :, 0:dims[a][1]]
                for d in (5, 6, 7):
                    dense(d, True)
                ops.tt(g.x[:], g.x[:], feat[:, :, 0:D], ALU.add)
                norm_relu(g.h[:], g.x[:])
                dve.wait_ge(out_done, TILES)
                ops.tt(g.root_in[:], g.deg[:], g.outs[:], ALU.add)
                ops.ts(g.root_in[:], g.root_in[:], 1e-5, None, ALU.max)
                asked[0] += 1
                dve.engine_nop().then_inc(root_asked, 1)
                dve.wait_ge(root_done, asked[0])
                c.step(dve.reciprocal(g.dinv2[:], g.root_in[:]))



LOADS = 10 + 8


def stage_sheaf(nc, g, ins):
    with ExitStack() as ctx:
        s = Scope(nc, ctx, "shf")
        lanes = s.sb("lanes", [P, 2, LANE], I32)
        src_lo, src_hi = s.sb("src_lo", [P, LANE]), s.sb("src_hi", [P, LANE])
        ids2 = s.sb("ids2", [P, LANE], I32)
        table = s.sb("table", [P, TILES, 2, D])
        W1 = s.sb("W1", [P, P])
        W2 = s.sb("W2", [P, 3 * D])
        b1 = s.sb("b1", [P, 1])
        b2 = s.sb("b2", [P, 3, D])
        idx = [[s.sb(f"idx{b}{e}", [P, BATCH], I32) for e in range(2)] for b in range(2)]
        rows = [s.sb(f"rows{b}", [P, BATCH, 2, 2, D]) for b in range(2)]
        turned_sb = s.sb("turned_sb", [P, 4 * P])
        hidden = [s.sb(f"hidden{h}", [P, 4 * P]) for h in range(2)]
        v = s.sb("v", [P, BATCH, 3, D])
        vv = s.sb("vv", [P, BATCH, 3, D])
        c2 = s.sb("c2", [P, BATCH, 3])
        prod = s.sb("prod", [P, BATCH, 2, D])
        dots = s.sb("dots", [P, BATCH, 2])
        u = s.sb("u", [P, BATCH, 2, D])
        msg = [s.sb(f"msg{b}", [P, 2, BATCH, D]) for b in range(2)]
        hot_lo = [s.sb(f"hot_lo{b}", [P, BATCH, P]) for b in range(2)]
        hot_hi = s.sb("hot_hi", [P, BATCH, TILES])
        wide = [s.sb(f"wide{b}", [P, BATCH, TILES, D]) for b in range(2)]
        zeros = s.sb("zeros", [P, TILES * D])
        to_src = s.sb("to_src", [P, TILES, D])
        turn_ps = s.ps("turn_ps", [P, 4 * P])
        hid_ps = [s.ps(f"hid_ps{h}", [P, 4 * P]) for h in range(2)]
        v_ps = [s.ps(f"v_ps{b}", [P, 512]) for b in range(2)]
        sum_ps = s.ps("sum_ps", [P, 512])
        loaded, stored, chain, table_ready, table_out = map(s.sem, ("loaded", "stored", "chain", "table_ready", "table_out"))
        zeroed, turned, copied, hid_done, hid_ready, v_done = map(
            s.sem, ("zeroed", "turned", "copied", "hid_done", "hid_ready", "v_done"))
        lane_in = s.sem("lane_in")
        idx_set = [s.sem(f"idx_set{b}") for b in range(2)]
        gathered = [s.sem(f"gathered{b}") for b in range(2)]
        rows_read = [s.sem(f"rows_read{b}") for b in range(2)]
        v_read = [s.sem(f"v_read{b}") for b in range(2)]
        msg_ready = [s.sem(f"msg_ready{b}") for b in range(2)]
        msg_out = [s.sem(f"msg_out{b}") for b in range(2)]
        wide_ready = [s.sem(f"wide_ready{b}") for b in range(2)]
        wide_used = [s.sem(f"wide_used{b}") for b in range(2)]
        summed = s.sem("summed")
        msg_lanes = g.to_dst_d[:].rearrange("(p t) d -> p t d", p=P)

        with nc.Block() as block:
            @block.sync
            def _(sp):
                n = 0
                sp.wait_ge(zeroed, 4)
                w1, w2 = ins["L2_gnn_W1"].rearrange("h k -> k h"), ins["L2_gnn_W2"].rearrange("o h -> h o")
                for half in range(2):
                    o = half * 64
                    for row, col, part in ((0, 0, 0), (32, 0, 1), (32, HID, 0), (0, HID, 1)):
                        sp.dma_start(W1[o + row:o + row + D, col:col + HID], w1[part * D:(part + 1) * D, :],
                                     allow_slow_non_contiguous=True).then_inc(loaded, 16)
                        n += 1
                for row, col in ((0, 0), (HID, D), (0, 2 * D)):
                    sp.dma_start(W2[row:row + HID, col:col + D], w2, allow_slow_non_contiguous=True).then_inc(loaded, 16)
                    n += 1
                for half in range(2):
                    sp.dma_start(b1[half * HID:(half + 1) * HID, :], ins["L2_gnn_b1"].rearrange("(h o) -> h o", o=1)).then_inc(loaded, 16)
                    n += 1
                sp.dma_start(b2[:], ins["L2_gnn_b2"].unsqueeze(0).unsqueeze(0).broadcast_to([P, 3, D])).then_inc(loaded, 16)
                assert n + 1 == SHEAF_LOADS
                sp.dma_start(lanes[:, 0, :], g.src_d[:].rearrange("(p t) -> p t", p=P)).then_inc(lane_in, 16)
                sp.dma_start(lanes[:, 1, :], g.dst_d[:].rearrange("(p t) -> p t", p=P)).then_inc(lane_in, 16)
                sp.wait_ge(table_ready, 1)
                sp.dma_start(g.table_d[:].rearrange("(t p) c -> p t c", p=P),
                             table[:].rearrange("p t a d -> p t (a d)")).then_inc(table_out, 16)
                sp.wait_ge(loaded, 16 * SHEAF_LOADS)
                with sp.Fori(0, GROUPS // 2) as i:
                    for b in range(2):
                        sp.wait_ge(msg_ready[b], i + 1)
                        sp.dma_start(msg_lanes[:, bass.ds(i * (2 * BATCH) + b * BATCH, BATCH), :], msg[b][:, 0]).then_inc(msg_out[b], 16)
                for b in range(2):
                    sp.wait_ge(msg_out[b], 16 * (GROUPS // 2))

            @block.gpsimd
            def _(pool):
                pool.memset(W1[:], 0.0).then_inc(zeroed, 1)
                pool.memset(W2[:], 0.0).then_inc(zeroed, 1)
                pool.memset(zeros[:], 0.0).then_inc(zeroed, 1)
                pool.memset(b1[:], 0.0).then_inc(zeroed, 1)
                pool.wait_ge(lane_in, 32)
                pool.wait_ge(table_out, 16)
                reg = pool.alloc_register("shf_pool_carrier")
                pool.reg_mov(reg, 0)
                with pool.Fori(0, GROUPS // 2) as i:
                    for b in range(2):
                        pool.wait_ge(gathered[b], settled(pool, reg, zeroed, i * (32 * BATCH)))
                        for e in range(2):
                            pool.tensor_copy(idx[b][e][:], lanes[:, e, bass.ds(i * (2 * BATCH) + b * BATCH, BATCH)]).then_inc(idx_set[b], 1)
                        pool.wait_ge(idx_set[b], settled(pool, reg, zeroed, i * 2 + 2))
                        pool.wait_ge(rows_read[b], settled(pool, reg, zeroed, i))
                        for t in range(BATCH):
                            for e in range(2):
                                pool.indirect_dma_start(rows[b][:, t, e].rearrange("p a d -> p (a d)"), None, g.table_d[:],
                                                        bass.IndirectOffsetOnAxis(idx[b][e][:, t:t + 1], 0)).then_inc(gathered[b], 16)

            @block.tensor
            def _(pe):
                pe.wait_ge(loaded, 16 * SHEAF_LOADS)
                pe.wait_ge(zeroed, 4)
                pe.matmul(sum_ps[:, 0:TILES * D], zeros[:, 0:P], zeros[:], start=True, stop=False, skip_group_check=True)
                with pe.Fori(0, GROUPS // 2) as i:
                    for b in range(2):
                        k = i * 2 + b
                        pe.wait_ge(gathered[b], i * (32 * BATCH) + 32 * BATCH)
                        pe.wait_ge(copied, k)
                        for j in range(BATCH // 2):
                            mm = pe.transpose(turn_ps[:, j * P:(j + 1) * P],
                                              rows[b][:, 2 * j:2 * j + 2].rearrange("p t e a d -> p (t e a d)"),
                                              g.const[:, C_EYE:C_EYE + P])
                        mm.then_inc(turned, 1)
                        pe.wait_ge(copied, k + 1)
                        pe.wait_ge(hid_ready, k * 2)
                        for h in range(2):
                            pe.matmul(hid_ps[h][:], W1[64 * h:64 * h + 64, :], turned_sb[64 * h:64 * h + 64, :],
                                      start=True, stop=True).then_inc(hid_done, 1)
                        pe.wait_ge(hid_ready, k * 2 + 2)
                        pe.wait_ge(v_read[b], i)
                        for t in range(BATCH):
                            j, h = t // 2, t % 2
                            mm = pe.matmul(v_ps[b][:, t * 3 * D:(t + 1) * 3 * D], hidden[h][:, j * P:(j + 1) * P], W2[:],
                                           start=True, stop=True)
                        mm.then_inc(v_done, 1)
                    for b in range(2):
                        pe.wait_ge(wide_ready[b], i + 1)
                        for t in range(BATCH):
                            mm = pe.matmul(sum_ps[:, 0:TILES * D], hot_lo[b][:, t, :], wide[b][:, t].rearrange("p s d -> p (s d)"),
                                           start=False, stop=False, skip_group_check=True)
                        mm.then_inc(wide_used[b], 1)
                pe.matmul(sum_ps[:, 0:TILES * D], zeros[:, 0:P], zeros[:], start=False, stop=True,
                          skip_group_check=True).then_inc(summed, 1)

            @block.scalar
            def _(act):
                act.wait_ge(loaded, 16 * SHEAF_LOADS)
                with act.Fori(0, GROUPS // 2) as i:
                    for b in range(2):
                        k = i * 2 + b
                        act.wait_ge(turned, k + 1)
                        act.wait_ge(hid_done, k * 2)
                        act.activation(turned_sb[:], turn_ps[:], ACT.Copy).then_inc(copied, 1)
                        act.wait_ge(v_done, k)
                        for h in range(2):
                            act.wait_ge(hid_done, k * 2 + (h + 1))
                            act.activation(hidden[h][:], hid_ps[h][:], ACT.Relu, bias=b1[:, 0:1]).then_inc(hid_ready, 1)

            @block.vector
            def _(dve):
                c = Chain(dve, chain)
                c.step(dve.tensor_copy(table[:, :, 0, :], g.h[:]))
                c.step(dve.tensor_tensor(table[:, :, 1, :], g.h[:], spread(g.dinv2[:], [P, TILES, D]), ALU.mult))
                dve.engine_nop().then_inc(table_ready, 1)
                dve.wait_ge(lane_in, 32)
                c.step(dve.tensor_scalar(ids2[:], lanes[:, 0, :], P - 1, None, ALU.bitwise_and))
                c.step(dve.tensor_copy(src_lo[:], ids2[:]))
                c.step(dve.tensor_scalar(ids2[:], lanes[:, 0, :], P.bit_length() - 1, None, ALU.arith_shift_right))
                c.step(dve.tensor_copy(src_hi[:], ids2[:]))
                dve.wait_ge(loaded, 16 * SHEAF_LOADS)
                before = c.n
                with dve.Fori(0, GROUPS // 2) as i:
                    for b in range(2):
                        c = Chain(dve, chain, (i * 2 + b) * SHEAF_STEPS + before)
                        col = i * (2 * BATCH) + b * BATCH
                        y = rows[b][:, :, :, 1, :]
                        shape = [P, BATCH, 2, D]
                        dve.wait_ge(v_done, i * 2 + (b + 1))
                        dve.wait_ge(gathered[b], i * (32 * BATCH) + 32 * BATCH)
                        c.publish(dve.tensor_tensor(v[:], v_ps[b][:, 0:BATCH * 3 * D].rearrange("p (t a d) -> p t a d", t=BATCH, a=3),
                                                    b2[:].unsqueeze(1).broadcast_to([P, BATCH, 3, D]), ALU.add),
                                  v_read[b], i + 1)
                        c.step(dve.tensor_tensor(vv[:], v[:], v[:], ALU.mult))
                        c.step(dve.tensor_reduce(c2[:], vv[:], AX.X, ALU.add))
                        c.step(dve.tensor_scalar(c2[:], c2[:], 1e-24, 0.5, ALU.max, ALU.mult))
                        c.step(dve.reciprocal(c2[:], c2[:]))

                        def reflect(out, vec, scale, x, done):
                            c.step(dve.tensor_tensor(prod[:], vec, x, ALU.mult))
                            c.step(dve.tensor_reduce(dots[:], prod[:], AX.X, ALU.add))
                            c.step(dve.tensor_tensor(dots[:], dots[:], scale, ALU.mult))
                            c.step(dve.tensor_tensor(prod[:], vec, spread(dots[:], shape), ALU.mult))
                            c.publish(dve.tensor_tensor(out, x, prod[:], ALU.subtract), done, i + 1)

                        reflect(u[:], v[:, :, 0:2, :], c2[:, :, 0:2], y, rows_read[b])
                        dve.wait_ge(msg_out[b], i * 16)
                        dve.wait_ge(wide_used[b], i)
                        reflect(msg[b][:].rearrange("p a t d -> p t a d"), v[:, :, 1:3, :], c2[:, :, 1:3], u[:], msg_ready[b])
                        for t in range(BATCH):
                            dve.tensor_scalar(hot_lo[b][:, t, :], g.const[:, C_IOTA:C_IOTA + P], src_lo[:, bass.ds(col + t, 1)],
                                              None, ALU.is_equal)
                        c.step(dve.tensor_tensor(hot_hi[:], spread(src_hi[:, bass.ds(col, BATCH)], [P, BATCH, TILES]),
                                                 g.const[:, C_IOTA:C_IOTA + TILES].unsqueeze(1).broadcast_to([P, BATCH, TILES]),
                                                 ALU.is_equal))
                        dve.tensor_tensor(wide[b][:], spread(hot_hi[:], [P, BATCH, TILES, D]),
                                            msg[b][:, 1].unsqueeze(2).broadcast_to([P, BATCH, TILES, D]),
                                          ALU.mult).then_inc(wide_ready[b], 1)
                        assert c.n == SHEAF_STEPS, c.n
                dve.wait_ge(summed, 1)
                c = Chain(dve, chain, GROUPS * SHEAF_STEPS + before)
                c.step(dve.tensor_copy(g.messages[:], sum_ps[:, 0:TILES * D].rearrange("p (t d) -> p t d", t=TILES)))


SHEAF_LOADS = 8 + 3 + 2 + 1
SHEAF_STEPS = 4 + 4 + 4 + 1


def stage_sheaf_dst(nc, g):
    BUFS = 5
    with ExitStack() as ctx:
        s = Scope(nc, ctx, "shd")
        at_i = s.sb("at_i", [P, TILES], I32)
        inside = s.sb("inside", [P, TILES, WIN])
        window = [s.sb(f"window{b}", [P, WIN, D]) for b in range(BUFS)]
        to_dst = s.sb("to_dst", [P, TILES, D])
        chain, at_ready, root_asked, root_done, table_ready, table_out = map(
            s.sem, ("chain", "at_ready", "root_asked", "root_done", "table_ready", "table_out"))
        window_in = [s.sem(f"window_in{b}") for b in range(BUFS)]
        window_read = [s.sem(f"window_read{b}") for b in range(BUFS)]
        with nc.Block() as block:
            @block.gpsimd
            def _(pool):
                pool.wait_ge(at_ready, 1)
                for t in range(TILES):
                    b = t % BUFS
                    if t >= BUFS:
                        pool.wait_ge(window_read[b], t // BUFS)
                    pool.indirect_dma_start(window[b][:].rearrange("p w d -> p (w d)"), None, g.to_dst_d[:],
                                            bass.IndirectOffsetOnAxis(at_i[:, t:t + 1], 0)).then_inc(window_in[b], 16)

            @block.vector
            def _(dve):
                c = Chain(dve, chain)
                dve.tensor_copy(at_i[:], g.first[:]).then_inc(at_ready, 1)
                c.step(dve.tensor_tensor(inside[:], g.const[:, C_IOTA:C_IOTA + WIN].unsqueeze(1).broadcast_to([P, TILES, WIN]),
                                         spread(g.deg[:], [P, TILES, WIN]), ALU.is_lt))
                for t in range(TILES):
                    b = t % BUFS
                    dve.wait_ge(window_in[b], 16 * (t // BUFS + 1))
                    c.step(dve.tensor_tensor(window[b][:], window[b][:], spread(inside[:, t, :], [P, WIN, D]), ALU.mult))
                    dve.tensor_reduce(to_dst[:, t, :], window[b][:].rearrange("p w d -> p d w"), AX.X,
                                      ALU.add).then_inc(window_read[b], 1)
                for b in range(BUFS):
                    dve.wait_ge(window_read[b], TILES // BUFS)
                c.step(dve.tensor_tensor(g.messages[:], g.messages[:], to_dst[:], ALU.add))
                c.step(dve.tensor_tensor(g.messages[:], g.messages[:], spread(g.dinv2[:], [P, TILES, D]), ALU.mult))
                c.step(dve.tensor_tensor(g.messages[:], g.messages[:], g.h[:], ALU.add))
                c.step(dve.tensor_scalar(g.messages[:], g.messages[:], 0.0, None, ALU.max))
                c.step(dve.tensor_tensor(g.x[:], g.x[:], g.messages[:], ALU.add))
                norm(dve, c, g, g.h[:], g.x[:], root_asked, root_done, [0])
                dve.engine_nop().then_inc(table_ready, 1)

            @block.scalar
            def _(act):
                act.wait_ge(root_asked, 1)
                act.activation(g.root_in[:], g.root_in[:], ACT.Sqrt).then_inc(root_done, 1)
                act.wait_ge(table_ready, 1)
                act.dma_start(g.h_d[:].rearrange("(t p) d -> p t d", p=P), g.h[:]).then_inc(table_out, 16)
                act.wait_ge(table_out, 16)


def stage_attention(nc, g, ins, out):
    C2 = D * D
    with ExitStack() as ctx:
        s = Scope(nc, ctx, "att")
        wf = s.sb("wf", [P, 2 * C2])
        wr = s.sb("wr", [P, 2 * C2])
        wp = [s.sb(f"wp{i}", [P, 2 * C2], BF16) for i in range(3)]
        w6 = s.sb("w6", [P, 2 * C2], BF16)
        cur = s.sb("cur", [P, 1])
        at_i = s.sb("at_i", [P, 1], I32)
        ids_next = s.sb("ids_next", [P, CHUNK], I32)
        ids = [s.sb(f"ids{h}", [P, HALF], I32) for h in range(2)]
        ea = s.sb("ea", [P, CHUNK, P], BF16)
        ea_t = [s.sb(f"ea_t{h}", [P, HALF, P], BF16) for h in range(2)]
        hs = [s.sb(f"hs{h}", [P, HALF, D]) for h in range(2)]
        e12 = [s.sb(f"e12{h}", [P, HALF, 2, C2]) for h in range(2)]
        top, top_was, shift = s.sb("top", [P, C2]), s.sb("top_was", [P, C2]), s.sb("shift", [P, C2])
        decay = s.sb("decay", [P, C2])
        sums = s.sb("sums", [P, 2, C2])
        left, over = s.sb("left", [P, 1]), s.sb("over", [P, CHUNK])
        off_max, off_exp = s.sb("off_max", [P, CHUNK]), s.sb("off_exp", [P, CHUNK])
        ratio = s.sb("ratio", [P, C2])
        ft = s.sb("ft", [P, TILES + 1, D])
        zeros = s.sb("zeros", [P, 2 * C2])
        w_ps = [s.ps(f"w_ps{r}", [P, 2 * C2]) for r in range(HALF)]
        t_ps = s.ps("t_ps", [P, HALF, P], BF16)
        sum_ps = s.ps("sum_ps", [P, 2 * C2])
        w_in, zeroed, w_ready_s, chain0, chain_f, chain_l, own = map(
            s.sem, ("w_in", "zeroed", "w_ready", "chain0", "chain_f", "chain_l", "own"))
        ids_in, ea_in, shift_ready, decay_ready, sums_done, sum_added, stored = map(
            s.sem, ("ids_in", "ea_in", "shift_ready", "decay_ready", "sums_done", "sum_added", "stored"))
        hs_in, turned, ea_t_ready, w_done, w_used, sub_ready, exp_ready, num_ready, half_done = (
            [s.sem(f"{name}{h}") for h in range(2)] for name in
            ("hs_in", "turned", "ea_t_ready", "w_done", "w_used", "sub_ready", "exp_ready", "num_ready", "half_done"))

        def last_chunk(eng):
            return eng.value_load(g.loops[0:1, TILES + 1:TILES + 2], min_val=2 * TILES - 1, max_val=E)

        with nc.Block() as block:
            @block.sync
            def _(sp):
                sp.wait_ge(zeroed, 2)
                n = 0
                for col, w, bias in ((0, "L3_gnn_W_msg", "L3_gnn_b_msg"), (C2, "L3_gnn_W_attn", "L3_gnn_b_attn")):
                    for part in range(6):
                        sp.dma_start(wf[part * D:(part + 1) * D, col:col + C2], ins[w]).then_inc(w_in, 16)
                        n += 1
                    for part in range(3):
                        sp.dma_start(wf[6 * D + part:6 * D + part + 1, col:col + C2], ins[bias].rearrange("(a n) -> a n", a=1)).then_inc(w_in, 16)
                        n += 1
                assert n == 18
                sp.wait_ge(w_in, 16 * n)
                sp.wait_ge(chain0, END_STEPS)
                last = TILES - 1
                sp.dma_start(out[0:last * P, :].rearrange("(t p) d -> p t d", p=P), ft[:, 1:TILES, :]).then_inc(stored, 16)
                sp.dma_start(out[last * P:N, :], ft[0:N - last * P, TILES, :]).then_inc(stored, 16)
                sp.wait_ge(stored, 32)

            @block.gpsimd
            def _(pool):
                pool.memset(wf[:], 0.0).then_inc(zeroed, 1)
                pool.memset(zeros[:], 0.0).then_inc(zeroed, 1)
                k_reg = pool.alloc_register("att_pool_k")
                pool.reg_mov(k_reg, 0)
                reg = pool.alloc_register("att_pool_carrier")
                pool.reg_mov(reg, 0)
                edges = g.src_d[:].rearrange("(e o) -> e o", o=1)
                with pool.Fori(0, TILES) as t:
                    k = pool.snap(k_reg)
                    pool.wait_ge(ids_in, settled(pool, reg, zeroed, k * 16 + t * 16))
                    pool.wait_ge(ea_in, settled(pool, reg, zeroed, k * 16))
                    pool.wait_ge(own, settled(pool, reg, zeroed, k * 4 + t * 2))
                    pool.tensor_copy(cur[:], g.first[:, bass.ds(t, 1)]).then_inc(own, 1)
                    pool.wait_ge(own, settled(pool, reg, zeroed, k * 4 + (t * 2 + 1)))
                    pool.tensor_copy(at_i[:], cur[:]).then_inc(own, 1)
                    pool.wait_ge(own, settled(pool, reg, zeroed, k * 4 + (t * 2 + 2)))
                    pool.indirect_dma_start(ids_next[:], None, edges, bass.IndirectOffsetOnAxis(at_i[:, 0:1], 0)).then_inc(ids_in, 16)
                    chunks = pool.value_load(g.loops[0:1, bass.ds(t, 1)], min_val=2, max_val=E)
                    with pool.Fori(0, chunks):
                        k = pool.snap(k_reg)
                        base = k * 4 + (t * 2 + 2)
                        pool.wait_ge(turned[1], settled(pool, reg, zeroed, k))
                        pool.indirect_dma_start(ea[:].rearrange("p c k -> p (c k)"), None, g.ea6_d[:],
                                                bass.IndirectOffsetOnAxis(at_i[:, 0:1], 0)).then_inc(ea_in, 16)
                        pool.wait_ge(ids_in, settled(pool, reg, zeroed, k * 16 + (t * 16 + 16)))
                        for h in range(2):
                            pool.wait_ge(hs_in[h], settled(pool, reg, zeroed, k * (16 * HALF)))
                            pool.tensor_copy(ids[h][:], ids_next[:, h * HALF:(h + 1) * HALF]).then_inc(own, 1)
                            pool.wait_ge(own, settled(pool, reg, zeroed, base + (h + 1 if h == 0 else 2)))
                            if h == 1:
                                pool.wait_ge(ea_in, settled(pool, reg, zeroed, k * 16 + 16))
                                pool.tensor_scalar(cur[:], cur[:], float(CHUNK), float(E), ALU.add, ALU.min).then_inc(own, 1)
                                pool.wait_ge(own, settled(pool, reg, zeroed, base + 3))
                                pool.tensor_copy(at_i[:], cur[:]).then_inc(own, 1)
                                pool.wait_ge(own, settled(pool, reg, zeroed, base + 4))
                                pool.indirect_dma_start(ids_next[:], None, edges,
                                                        bass.IndirectOffsetOnAxis(at_i[:, 0:1], 0)).then_inc(ids_in, 16)
                            pool.wait_ge(w_used[h], settled(pool, reg, zeroed, k * HALF))
                            for r in range(HALF):
                                pool.indirect_dma_start(hs[h][:, r, :], None, g.h_d[:],
                                                        bass.IndirectOffsetOnAxis(ids[h][:, r:r + 1], 0)).then_inc(hs_in[h], 16)
                        pool.reg_add(k_reg, k_reg, 1)
                k = pool.snap(k_reg)
                pool.wait_ge(ids_in, settled(pool, reg, zeroed, k * 16 + 16 * TILES))

            @block.tensor
            def _(pe):
                def turn(k, h, waits=True):
                    if h == 0:
                        pe.wait_ge(ea_in, k * 16 + 16)
                        if waits:
                            pe.wait_ge(ea_t_ready[1], k)
                    else:
                        pe.wait_ge(ea_t_ready[0], k + 1)
                    for r in range(HALF):
                        mm = pe.transpose(t_ps[:, r, :], ea[:, h * HALF + r, :], g.eye_bf[:])
                    mm.then_inc(turned[h], 1)

                def weigh(k, h, before=None):
                    pe.wait_ge(ea_t_ready[h], k + 1)
                    for r in range(HALF):
                        if h == 1:
                            pe.wait_ge(w_used[0], k * HALF + (r + 1))
                        elif before is not None:
                            pe.wait_ge(w_used[1], before * HALF + (r + 1))
                        pe.matmul(w_ps[r][:], ea_t[h][:, r, :], w6[:], start=True, stop=True).then_inc(w_done[h], 1)

                def add(k, h):
                    if h == 0:
                        pe.wait_ge(sum_added, k + 1)
                    pe.wait_ge(num_ready[h], k + 1)
                    for r in range(HALF):
                        mm = pe.matmul(sum_ps[:], g.const[:, C_EYE:C_EYE + P], e12[h][:, r].rearrange("p a c -> p (a c)"),
                                       start=h == 0 and r == 0, stop=h == 1 and r == HALF - 1)
                    mm.then_inc(half_done[h], 1)

                pe.wait_ge(zeroed, 2)
                pe.matmul(sum_ps[:], zeros[:, 0:P], zeros[:], start=True, stop=True).then_inc(sums_done, 1)
                pe.wait_ge(w_ready_s, 1)
                turn(0, 0, waits=False)
                weigh(0, 0)
                last = last_chunk(pe)
                with pe.Fori(0, last) as k:
                    turn(k, 1)
                    weigh(k, 1)
                    add(k, 0)
                    turn(k + 1, 0)
                    weigh(k + 1, 0, before=k)
                    add(k, 1)
                k = last
                turn(k, 1)
                weigh(k, 1)
                add(k, 0)
                add(k, 1)

            @block.scalar
            def _(act):
                def copy(k, h):
                    act.wait_ge(turned[h], k + 1)
                    act.wait_ge(w_done[h], k * HALF)
                    act.activation(ea_t[h][:], t_ps[:], ACT.Copy).then_inc(ea_t_ready[h], 1)

                def exps(k):
                    act.wait_ge(shift_ready, k + 1)
                    act.activation(decay[:], shift[:], ACT.Exp).then_inc(decay_ready, 1)
                    for h in range(2):
                        act.wait_ge(sub_ready[h], k + 1)
                        for r in range(HALF):
                            e2 = e12[h][:, r, 1, :]
                            act.activation(e2, e2, ACT.Exp, bias=off_exp[:, h * HALF + r:h * HALF + r + 1]).then_inc(exp_ready[h], 1)

                copy(0, 0)
                last = last_chunk(act)
                with act.Fori(0, last) as k:
                    copy(k, 1)
                    exps(k)
                    copy(k + 1, 0)
                k = last
                copy(k, 1)
                exps(k)

            @block.vector
            def _(dve):
                c = Chain(dve, chain0)
                dve.wait_ge(w_in, 16 * 18)
                for i in range(3):
                    now = wf if i == 0 else wr
                    c.step(dve.tensor_copy(wp[i][:], now[:]))
                    if i < 2:
                        c.step(dve.tensor_tensor(wr[:], now[:], wp[i][:], ALU.subtract))
                c.step(dve.tensor_scalar(wf[:], wp[0][:], g.const[:, C_PART:C_PART + 1], None, ALU.mult))
                c.step(dve.scalar_tensor_tensor(out=wf[:], in0=wp[1][:], scalar=g.const[:, C_PART + 1:C_PART + 2], in1=wf[:],
                                                op0=ALU.mult, op1=ALU.add))
                c.step(dve.scalar_tensor_tensor(out=w6[:], in0=wp[2][:], scalar=g.const[:, C_PART + 2:C_PART + 3], in1=wf[:],
                                                op0=ALU.mult, op1=ALU.add))
                dve.engine_nop().then_inc(w_ready_s, 1)
                c.step(dve.memset(sums[:], 0.0))
                before = c.n

                def add_sums(c, k):
                    dve.wait_ge(sums_done, 1)
                    dve.wait_ge(half_done[1], k)
                    c.publish(dve.tensor_tensor(sums[:], sums[:], sum_ps[:].rearrange("p (a c) -> p a c", a=2), ALU.add),
                              sum_added, k + 1)

                def finish(c, slot):
                    c.step(dve.tensor_scalar(ratio[:], sums[:, 1, :], 1e-30, None, ALU.max))
                    c.step(dve.reciprocal(ratio[:], ratio[:]))
                    c.step(dve.tensor_tensor(ratio[:], ratio[:], sums[:, 0, :], ALU.mult))
                    c.step(dve.tensor_reduce(ft[:, slot, :], ratio[:].rearrange("p (i j) -> p j i", i=D), AX.X, ALU.add))

                def step(c, k, first, t):
                    if first:
                        c(dve.tensor_copy(left[:], g.deg[:, bass.ds(t, 1)]))
                        c(dve.memset(top_was[:], LOWEST))
                        c(dve.memset(top[:], LOWEST))
                    else:
                        c(dve.tensor_scalar(left[:], left[:], float(-CHUNK), None, ALU.add))
                        c(dve.tensor_copy(top_was[:], top[:]))
                    c.sync()
                    c.step(dve.tensor_scalar(over[:], g.const[:, C_IOTA:C_IOTA + CHUNK], left[:, 0:1], None, ALU.is_ge))
                    c(dve.tensor_scalar(off_max[:], over[:], OFF_MAX, None, ALU.mult))
                    c.step(dve.tensor_scalar(off_exp[:], over[:], OFF_EXP, None, ALU.mult))
                    for h in range(2):
                        dve.wait_ge(hs_in[h], k * (16 * HALF) + 16 * HALF)
                        dve.wait_ge(half_done[h], k)
                        for r in range(HALF):
                            dve.wait_ge(w_done[h], k * HALF + (r + 1))
                            dve.tensor_tensor(e12[h][:, r].rearrange("p a (i j) -> p a i j", i=D),
                                              w_ps[r][:].rearrange("p (a i j) -> p a i j", a=2, i=D),
                                              hs[h][:, r, :].unsqueeze(1).unsqueeze(3).broadcast_to([P, 2, D, D]),
                                              ALU.mult).then_inc(w_used[h], 1)
                        dve.wait_ge(w_used[h], k * HALF + HALF)
                        for r in range(HALF):
                            n = h * HALF + r
                            c.step(dve.scalar_tensor_tensor(out=top[:], in0=e12[h][:, r, 1, :], scalar=off_max[:, n:n + 1],
                                                            in1=top[:], op0=ALU.add, op1=ALU.max))
                    dve.wait_ge(decay_ready, k)
                    dve.tensor_tensor(shift[:], top_was[:], top[:], ALU.subtract).then_inc(shift_ready, 1)
                    for h in range(2):
                        e2 = e12[h][:, :, 1, :]
                        dve.tensor_tensor(e2, e2, top[:].unsqueeze(1).broadcast_to([P, HALF, C2]), ALU.subtract).then_inc(sub_ready[h], 1)
                    add_sums(c, k)
                    if first:
                        finish(c, bass.ds(t, 1))
                        c.step(dve.memset(sums[:], 0.0))
                        dve.wait_ge(decay_ready, k + 1)
                    else:
                        dve.wait_ge(decay_ready, k + 1)
                        c.step(dve.tensor_tensor(sums[:], sums[:], decay[:].unsqueeze(1).broadcast_to([P, 2, C2]), ALU.mult))
                    for h in range(2):
                        dve.wait_ge(exp_ready[h], k * HALF + HALF)
                        dve.tensor_tensor(e12[h][:, :, 0, :], e12[h][:, :, 0, :], e12[h][:, :, 1, :], ALU.mult).then_inc(num_ready[h], 1)

                k_reg, later_reg = dve.alloc_register("att_dve_k"), dve.alloc_register("att_dve_later")
                dve.reg_mov(k_reg, 0)
                dve.reg_mov(later_reg, 0)
                with dve.Fori(0, TILES) as t:
                    k = dve.snap(k_reg)
                    cf = Chain(dve, chain_f, t * FIRST_STEPS)
                    step(cf, k, True, t)
                    assert cf.n == FIRST_STEPS, cf.n
                    dve.reg_add(k_reg, k_reg, 1)
                    chunks = dve.value_load(g.loops[0:1, bass.ds(t, 1)], min_val=2, max_val=E)
                    with dve.Fori(1, chunks):
                        k = dve.snap(k_reg)
                        cl = Chain(dve, chain_l, dve.snap(later_reg) * LATER_STEPS)
                        step(cl, k, False, t)
                        assert cl.n == LATER_STEPS, cl.n
                        dve.reg_add(k_reg, k_reg, 1)
                        dve.reg_add(later_reg, later_reg, 1)
                c = Chain(dve, chain0, before)
                add_sums(c, dve.snap(k_reg))
                finish(c, slice(TILES, TILES + 1))
                c.step(dve.tensor_tensor(ft[:, 1:, :], ft[:, 1:, :], g.x[:], ALU.add))
                assert before + c.n == END_STEPS, before + c.n


FIRST_STEPS = 3 + 3 + 8 + 4 + 1
LATER_STEPS = 2 + 3 + 8 + 1
END_STEPS = 5 + 3 + 1 + 4 + 1


class Shared:
    pass


def build(nc, ins, out, debug=None, stages=99):
    g = Shared()
    debug = debug or {}
    with ExitStack() as ctx:
        s = Scope(nc, ctx, "all")
        g.src_d = nc.dram_tensor("src_pad", (EP,), I32).ap()
        g.dst_d = nc.dram_tensor("dst_pad", (EP,), I32).ap()
        g.first_d = nc.dram_tensor("first_pad", (NP + 1,), F32).ap()
        g.ea6_d = nc.dram_tensor("ea_parts", (EA_ROWS, P), BF16).ap()
        g.table_d = nc.dram_tensor("sheaf_table", (NP, 2 * D), F32).ap()
        g.to_dst_d = nc.dram_tensor("to_dst", (EP, D), F32).ap()
        g.h_d = nc.dram_tensor("h_table", (NP, D), F32).ap()
        g.const = s.sb("const", [P, C_END])
        g.eye_bf = s.sb("eye_bf", [P, P], BF16)
        g.iota_bf = s.sb("iota_bf", [P, P], BF16)
        g.x = s.sb("x", [P, TILES, D])
        g.h = s.sb("h", [P, TILES, D])
        g.first = s.sb("first", [P, TILES])
        g.deg = s.sb("deg", [P, TILES])
        g.outs = s.sb("outs", [P, TILES])
        g.dinv2 = s.sb("dinv2", [P, TILES])
        g.mean, g.root_in = s.sb("mean", [P, TILES]), s.sb("root_in", [P, TILES])
        g.centred, g.squares = s.sb("centred", [P, TILES, D]), s.sb("squares", [P, TILES, D])
        g.loops = s.sb("loops", [1, TILES + 2], I32)
        stage_pad(nc, g, ins)
        stage_split(nc, g, ins)
        stage_offsets(nc, g)
        with nc.sbuf_tensor("A", [P, TILES, NP], BF16) as A:
            g.A = A
            stage_adjacency(nc, g)
            if "A" in debug:
                dump(nc, [(debug["A"], A[:, :, :])])
            stage_layers01(nc, g, ins)
        if "x1" in debug:
            dump(nc, [(debug["x1"], g.x[:]), (debug["outs"], g.outs[:]), (debug["deg"], g.deg[:])])
        g.messages = s.sb("messages", [P, TILES, D])
        stage_sheaf(nc, g, ins)
        stage_sheaf_dst(nc, g)
        if "x2" in debug:
            dump(nc, [(debug["x2"], g.x[:]), (debug["h2"], g.h[:])])
        stage_attention(nc, g, ins, out)


def dump(nc, pairs):
    with nc.semaphore() as sem, nc.Block() as block:
        @block.sync
        def _(sp):
            for o, i in pairs:
                sp.dma_start(o, i).then_inc(sem, 16)
            sp.wait_ge(sem, 16 * len(pairs))


_INS = ["x", "src", "dst", "edge_attr_16", "L0_gnn_W1_l", "L0_gnn_b1", "L0_gnn_W1_r", "L0_gnn_W2_l", "L0_gnn_b2",
        "L0_gnn_W2_r", "L1_gnn_W1", "L1_gnn_b1", "L1_gnn_W2", "L1_gnn_b2", "L1_gnn_W3", "L1_gnn_b3", "L1_gnn_Wl1",
        "L1_gnn_bl1", "L1_gnn_Wl2", "L1_gnn_bl2", "L1_gnn_Wl3", "L1_gnn_bl3", "L2_gnn_W1", "L2_gnn_b1", "L2_gnn_W2",
        "L2_gnn_b2", "L3_gnn_W_msg", "L3_gnn_b_msg", "L3_gnn_W_attn", "L3_gnn_b_attn"]


def kernel(**inputs):
    import concourse.bacc as bacc
    from concourse.bass_utils import run_bass_kernel_spmd

    nc = bacc.Bacc("TRN2", target_bir_lowering=False, num_devices=1)
    arrays = {name: np.ascontiguousarray(inputs[name]) for name in _INS}
    arrays["constants"] = constants()
    ins = {name: nc.dram_tensor(f"in_{name}", a.shape, mybir.dt.from_np(a.dtype), kind="ExternalInput").ap()
           for name, a in arrays.items()}
    out = nc.dram_tensor("out", (N, D), F32, kind="ExternalOutput").ap()
    build(nc, ins, out)
    result = run_bass_kernel_spmd(nc, [{f"in_{name}": a for name, a in arrays.items()}], core_ids=[0])
    return result.results[0]["out"]
```

```python
from contextlib import ExitStack

import numpy as np

import concourse.bass as bass
from concourse import mybir

F32 = mybir.dt.float32
BF16 = mybir.dt.bfloat16
I32 = mybir.dt.int32
ALU = mybir.AluOpType
ACT = mybir.ActivationFunctionType
AX = mybir.AxisListType

P = 128
N = 3125
E = 100000
D = 16
TILES = -(-N // P)
NP = TILES * P
LANE = 784
EP = P * LANE
PADID = NP - 1
BLOCKS = EP // P
WIN = 64
PAIRS = -(-TILES // 2)
NODES = 16
CHUNK = 8
HALF = CHUNK // 2
HID = 64
BATCH = 8
GROUPS = LANE // BATCH
SPLIT_LANE = E // P
SPLIT_AT = 71
SPLIT_STEPS = SPLIT_LANE // SPLIT_AT
TAIL = E - P * SPLIT_LANE
EA_ROWS = P * SPLIT_LANE + P
LN_EPS = 1e-5
LOWEST = -3.0e38
OFF_MAX = -1.0e30
OFF_EXP = -2.0e38

C_EYE, C_IOTA, C_NODE, C_PART, C_END = 0, 128, 256, 256 + TILES, 256 + TILES + 3


def constants():
    c = np.zeros((P, C_END), np.float32)
    c[:, C_EYE:C_EYE + P] = np.eye(P)
    c[:, C_IOTA:C_IOTA + P] = np.arange(P)[None, :]
    c[:, C_NODE:C_NODE + TILES] = np.arange(TILES)[None, :] * P + np.arange(P)[:, None]
    part = [0] * 16 + [1] * 16 + [2] * 16 + [0] * 16 + [1] * 16 + [0] * 16 + [0, 1, 2]
    for row, which in enumerate(part):
        c[row, C_PART + which] = 1.0
    return c


class Chain:

    def __init__(self, eng, sem, base=0):
        self.eng, self.sem, self.base, self.n = eng, sem, base, 0

    def __call__(self, ins):
        ins.then_inc(self.sem, 1)
        self.n += 1

    def sync(self):
        self.eng.wait_ge(self.sem, self.base + self.n)

    def step(self, ins):
        self(ins)
        self.sync()

    def publish(self, ins, sem, value):
        ins.then_inc(sem, 1)
        self.eng.wait_ge(sem, value)


def settled(eng, reg, sem, value):
    eng.reg_mov(reg, value)
    value = eng.snap(reg)
    eng.wait_ge(sem, 1)
    return value


def free(eng, *sems):
    for sem in sems:
        eng.engine_nop().then_inc(sem, 1)


class Scope:

    def __init__(self, nc, ctx, tag):
        self.nc, self.ctx, self.tag = nc, ctx, tag

    def sb(self, name, shape, dt=F32):
        return self.ctx.enter_context(self.nc.sbuf_tensor(f"{self.tag}_{name}", shape, dt))

    def ps(self, name, shape, dt=F32):
        return self.ctx.enter_context(self.nc.psum_tensor(f"{self.tag}_{name}", shape, dt))

    def sem(self, name):
        return self.ctx.enter_context(self.nc.semaphore(f"{self.tag}_{name}"))


def spread(ap, shape):
    while len(ap.shape) < len(shape):
        ap = ap.unsqueeze(len(ap.shape))
    return ap.broadcast_to(shape)


def stage_pad(nc, g, ins):
    with ExitStack() as ctx:
        s = Scope(nc, ctx, "pad")
        pad_ids = s.sb("pad_ids", [32, (EP - E) // 32], I32)
        loaded, pad_set, stored = s.sem("loaded"), s.sem("pad_set"), s.sem("stored")
        with nc.Block() as block:
            @block.gpsimd
            def _(pool):
                pool.memset(pad_ids[:], PADID).then_inc(pad_set, 1)

            @block.sync
            def _(sp):
                sp.dma_start(g.const[:], ins["constants"]).then_inc(loaded, 16)
                sp.dma_start(g.x[:, 0:TILES - 1, :],
                             ins["x"][0:(TILES - 1) * P, :].rearrange("(t p) d -> p t d", p=P)).then_inc(loaded, 16)
                for real, padded in ((ins["src"], g.src_d), (ins["dst"], g.dst_d)):
                    sp.dma_start(padded[0:E].rearrange("(a b) -> a b", a=32),
                                 real.rearrange("(a b) -> a b", a=32)).then_inc(stored, 16)
                sp.wait_ge(pad_set, 1)
                for padded in (g.src_d, g.dst_d):
                    sp.dma_start(padded[E:EP].rearrange("(a b) -> a b", a=32), pad_ids[:]).then_inc(stored, 16)
                sp.wait_ge(stored, 64)
                sp.wait_ge(loaded, 32)
            x_zeroed, x_tail = s.sem("x_zeroed"), s.sem("x_tail")

            @block.vector
            def _(dve):
                dve.memset(g.x[:, TILES - 1, :], 0.0).then_inc(x_zeroed, 1)
                dve.wait_ge(loaded, 32)
                dve.tensor_copy(g.eye_bf[:], g.const[:, C_EYE:C_EYE + P]).then_inc(x_zeroed, 1)
                dve.tensor_copy(g.iota_bf[:], g.const[:, C_IOTA:C_IOTA + P]).then_inc(x_zeroed, 1)

            @block.scalar
            def _(act):
                act.wait_ge(x_zeroed, 1)
                rest = N - (TILES - 1) * P
                act.dma_start(g.x[0:rest, TILES - 1, :], ins["x"][(TILES - 1) * P:N, :]).then_inc(x_tail, 16)
                act.wait_ge(x_tail, 16)


def stage_split(nc, g, ins):
    steps = SPLIT_STEPS + 1
    with ExitStack() as ctx:
        s = Scope(nc, ctx, "split")
        ea = [s.sb(f"ea{b}", [P, SPLIT_AT, D]) for b in range(2)]
        rest1 = [s.sb(f"rest1{b}", [P, SPLIT_AT, D]) for b in range(2)]
        rest2 = [s.sb(f"rest2{b}", [P, SPLIT_AT, D]) for b in range(2)]
        out = [s.sb(f"out{b}", [P, SPLIT_AT, P], BF16) for b in range(2)]
        loaded = [s.sem(f"loaded{b}") for b in range(2)]
        stored = [s.sem(f"stored{b}") for b in range(2)]
        set_up, part1, left1, part2, left2, part3 = map(s.sem, ("set_up", "part1", "left1", "part2", "left2", "part3"))
        tail_zeroed = s.sem("tail_zeroed")
        main = ins["edge_attr_16"][0:P * SPLIT_LANE, :].rearrange("(p t) d -> p t d", p=P)
        main_out = g.ea6_d[0:P * SPLIT_LANE, :].rearrange("(p t) k -> p t k", p=P)

        with nc.Block() as block:
            @block.sync
            def _(sp):
                for k in range(steps):
                    b = k % 2
                    if k >= 2:
                        sp.wait_ge(part2, k - 1)
                    if k < SPLIT_STEPS:
                        sp.dma_start(ea[b][:], main[:, k * SPLIT_AT:(k + 1) * SPLIT_AT, :]).then_inc(loaded[b], 16)
                    else:
                        sp.wait_ge(tail_zeroed, 1)
                        sp.dma_start(ea[b][0:TAIL, 0, :], ins["edge_attr_16"][P * SPLIT_LANE:E, :]).then_inc(loaded[b], 16)

            @block.gpsimd
            def _(pool):
                for b in range(2):
                    pool.memset(out[b][:, :, 6 * D:P], 0.0).then_inc(set_up, 1)
                pool.wait_ge(set_up, 2)
                for b in range(2):
                    pool.memset(out[b][:, :, 6 * D:6 * D + 3], 1.0).then_inc(set_up, 1)
                pool.wait_ge(set_up, 4)
                for k in range(steps):
                    b = k % 2
                    pool.wait_ge(part3, k + 1)
                    if k < SPLIT_STEPS:
                        pool.dma_start(main_out[:, k * SPLIT_AT:(k + 1) * SPLIT_AT, :], out[b][:]).then_inc(stored[b], 16)
                    else:
                        pool.dma_start(g.ea6_d[P * SPLIT_LANE:EA_ROWS, :], out[b][:, 0, :]).then_inc(stored[b], 16)
                for b in range(2):
                    pool.wait_ge(stored[b], 16 * len(range(b, steps, 2)))

            @block.scalar
            def _(act):
                for k in range(steps):
                    b, n = k % 2, SPLIT_AT if k < SPLIT_STEPS else 1
                    act.wait_ge(loaded[b], 16 * (k // 2 + 1))
                    if k >= 2:
                        act.wait_ge(stored[b], 16 * (k // 2))
                    rows = out[b][:, 0:n, :]
                    act.activation(rows[:, :, 0:3 * D].rearrange("p t (c d) -> p t c d", c=3),
                                   ea[b][:, 0:n, :].unsqueeze(2).broadcast_to([P, n, 3, D]), ACT.Copy).then_inc(part1, 1)
                    act.wait_ge(left1, k + 1)
                    act.activation(rows[:, :, 3 * D:5 * D].rearrange("p t (c d) -> p t c d", c=2),
                                   rest1[b][:, 0:n, :].unsqueeze(2).broadcast_to([P, n, 2, D]), ACT.Copy).then_inc(part2, 1)
                    act.wait_ge(left2, k + 1)
                    act.activation(rows[:, :, 5 * D:6 * D], rest2[b][:, 0:n, :], ACT.Copy).then_inc(part3, 1)

            @block.vector
            def _(dve):
                for k in range(steps):
                    b, n = k % 2, SPLIT_AT if k < SPLIT_STEPS else 1
                    if k >= 2:
                        dve.wait_ge(part3, k - 1)
                    dve.wait_ge(part1, k + 1)
                    dve.tensor_tensor(rest1[b][:, 0:n, :], ea[b][:, 0:n, :], out[b][:, 0:n, 0:D],
                                      ALU.subtract).then_inc(left1, 1)
                    dve.wait_ge(part2, k + 1)
                    dve.wait_ge(left1, k + 1)
                    dve.tensor_tensor(rest2[b][:, 0:n, :], rest1[b][:, 0:n, :], out[b][:, 0:n, 3 * D:4 * D],
                                      ALU.subtract).then_inc(left2, 1)
                    if k == SPLIT_STEPS - 2:
                        dve.wait_ge(left1, k + 1)
                        dve.memset(ea[SPLIT_STEPS % 2][:, 0, :], 0.0).then_inc(tail_zeroed, 1)


def stage_offsets(nc, g):
    with ExitStack() as ctx:
        s = Scope(nc, ctx, "off")
        lasts_i = s.sb("lasts_i", [1, BLOCKS], I32)
        lasts = s.sb("lasts", [1, BLOCKS])
        ones = s.sb("ones", [1, P])
        lasts_bc = s.sb("lasts_bc", [P, BLOCKS])
        junk = s.sb("junk", [P, BLOCKS])
        below = s.sb("below", [P, TILES])
        block_at = s.sb("block_at", [P, TILES], I32)
        window_i = s.sb("window_i", [P, TILES, P], I32)
        window = s.sb("window", [P, TILES, P])
        inside = s.sb("inside", [P, TILES])
        last_row = s.sb("last_row", [1, 1])
        bc_ps = [s.ps(f"bc{b}", [P, 512]) for b in range(2)]
        lasts_in, dve_n, spread_done, windows_in, firsts_out, next_in = map(
            s.sem, ("lasts_in", "dve_n", "spread_done", "windows_in", "firsts_out", "next_in"))
        half = BLOCKS // 2

        with nc.Block() as block:
            @block.sync
            def _(sp):
                sp.dma_start(lasts_i[:], g.dst_d[:].rearrange("(b e) -> b e", e=P)[:, P - 1:P]
                             .rearrange("b e -> e b"), allow_slow_non_contiguous=True).then_inc(lasts_in, 16)
                sp.wait_ge(dve_n, SET + LASTS + COUNTED)
                sp.dma_start(g.first_d[0:NP].rearrange("(t p) -> p t", p=P), g.first[:],
                             allow_slow_non_contiguous=True).then_inc(firsts_out, 16)
                sp.dma_start(g.first_d[NP:NP + 1].rearrange("(a b) -> a b", a=1), last_row[:]).then_inc(firsts_out, 16)
                sp.wait_ge(firsts_out, 32)
                sp.dma_start(g.deg[:], g.first_d[1:NP + 1].rearrange("(t p) -> p t", p=P),
                             allow_slow_non_contiguous=True).then_inc(next_in, 16)
                sp.wait_ge(next_in, 16)

            @block.tensor
            def _(pe):
                pe.wait_ge(dve_n, SET + LASTS)
                for b in range(2):
                    pe.matmul(bc_ps[b][:, 0:half], ones[:], lasts[:, b * half:(b + 1) * half],
                              start=True, stop=True).then_inc(spread_done, 1)

            @block.gpsimd
            def _(pool):
                pool.wait_ge(dve_n, SET + LASTS + 2 + TILES + 1)
                for t in range(TILES):
                    pool.indirect_dma_start(window_i[:, t, :], None, g.dst_d[:].rearrange("(b e) -> b e", e=P),
                                            bass.IndirectOffsetOnAxis(block_at[:, t:t + 1], 0)).then_inc(windows_in, 16)
                pool.wait_ge(windows_in, 16 * TILES)

            @block.vector
            def _(dve):
                c = Chain(dve, dve_n)
                c(dve.memset(ones[:], 1.0))
                c(dve.memset(last_row[:], float(E)))
                dve.wait_ge(lasts_in, 16)
                c.step(dve.tensor_copy(lasts[:], lasts_i[:]))
                dve.wait_ge(spread_done, 2)
                for b in range(2):
                    c(dve.tensor_copy(lasts_bc[:, b * half:(b + 1) * half], bc_ps[b][:, 0:half]))
                c.sync()
                for t in range(TILES):
                    c.step(dve.tensor_scalar(junk[:], lasts_bc[:], g.const[:, C_NODE + t:C_NODE + t + 1], 0.0,
                                             ALU.is_lt, ALU.add, accum_out=below[:, t:t + 1]))
                c.step(dve.tensor_copy(block_at[:], below[:]))
                dve.wait_ge(windows_in, 16 * TILES)
                c.step(dve.tensor_copy(window[:], window_i[:]))
                for t in range(TILES):
                    c.step(dve.tensor_scalar(junk[:, 0:P], window[:, t, :], g.const[:, C_NODE + t:C_NODE + t + 1], 0.0,
                                             ALU.is_lt, ALU.add, accum_out=inside[:, t:t + 1]))
                c.step(dve.scalar_tensor_tensor(out=g.first[:], in0=below[:], scalar=float(P), in1=inside[:],
                                                op0=ALU.mult, op1=ALU.add))
                assert c.n == SET + LASTS + COUNTED
                dve.wait_ge(next_in, 16)
                c.step(dve.tensor_tensor(g.deg[:], g.deg[:], g.first[:], ALU.subtract))


SET, LASTS = 2, 1
COUNTED = 2 + TILES + 1 + 1 + TILES + 1


def stage_order(nc, g):
    with ExitStack() as ctx:
        s = Scope(nc, ctx, "ord")
        key = s.sb("key", [P, TILES])
        keys = s.sb("keys", [P, NP])
        junk = s.sb("junk", [P, NP], BF16)
        rank = s.sb("rank", [P, TILES])
        rank_i = s.sb("rank_i", [P, TILES], I32)
        part_i = s.sb("part_i", [P, 2, TILES], I32)
        info = s.sb("info", [P, TILES, 4])
        ranked = s.sb("ranked", [P, TILES, 4])
        most_t = s.sb("most_t", [TILES, 1])
        most_f = s.sb("most_f", [1, TILES])
        most_all = s.sb("most_all", [1, 2])
        counts = s.sb("counts", [1, TILES + 1], I32)
        deg_ps = s.ps("deg_ps", [TILES, P])
        row_ps = s.ps("row_ps", [1, TILES])
        dve_n, key_out, keys_in, info_out, ranked_in, pe_deg, key_set, rank_set, deg_set, most_set = map(
            s.sem, ("dve_n", "key_out", "keys_in", "info_out", "ranked_in", "pe_deg", "key_set", "rank_set",
                    "deg_set", "most_set"))

        with nc.Block() as block:
            @block.sync
            def _(sp):
                sp.wait_ge(key_set, 1)
                sp.dma_start(g.key_d[:].rearrange("(t p) -> p t", p=P), key[:],
                             allow_slow_non_contiguous=True).then_inc(key_out, 16)
                sp.wait_ge(key_out, 16)
                sp.dma_start(keys[:], g.key_d[:].unsqueeze(0).broadcast_to([P, NP])).then_inc(keys_in, 16)
                sp.wait_ge(info_out, 16 * TILES)
                sp.dma_start(ranked[:], g.info_d[:].rearrange("(t p) c -> p t c", p=P)).then_inc(ranked_in, 16)
                sp.wait_ge(ranked_in, 16)

            @block.gpsimd
            def _(pool):
                pool.wait_ge(rank_set, 1)
                for t in range(TILES):
                    pool.indirect_dma_start(g.info_d[:], bass.IndirectOffsetOnAxis(rank_i[:, t:t + 1], 0),
                                            info[:, t, :], None).then_inc(info_out, 16)
                pool.wait_ge(info_out, 16 * TILES)

            @block.tensor
            def _(pe):
                pe.wait_ge(deg_set, 1)
                pe.transpose(deg_ps[:], g.deg_s[:], g.const[:, C_EYE:C_EYE + P]).then_inc(pe_deg, 1)
                pe.wait_ge(most_set, 1)
                pe.transpose(row_ps[:], most_t[:], g.const[0:TILES, C_EYE:C_EYE + TILES]).then_inc(pe_deg, 1)

            @block.vector
            def _(dve):
                c = Chain(dve, dve_n)
                c.step(dve.tensor_scalar(key[:], g.deg[:], float(KEY_MAX), float(KEY_STEP), ALU.min, ALU.mult))
                c.publish(dve.tensor_tensor(key[:], key[:], g.const[:, C_NODE:C_NODE + TILES], ALU.subtract), key_set, 1)
                c(dve.memset(info[:], 0.0))
                c.sync()
                c(dve.tensor_copy(info[:, :, 0], g.const[:, C_NODE:C_NODE + TILES]))
                c(dve.tensor_copy(info[:, :, 1], g.first[:]))
                c(dve.tensor_copy(info[:, :, 2], g.deg[:]))
                dve.wait_ge(keys_in, 16)
                for t in range(TILES):
                    c.step(dve.tensor_scalar(junk[:], keys[:], key[:, t:t + 1], 0.0, ALU.is_gt, ALU.add,
                                             accum_out=rank[:, t:t + 1]))
                c.publish(dve.tensor_copy(rank_i[:], rank[:]), rank_set, 1)
                c(dve.tensor_scalar(part_i[:, 0, :], rank_i[:], P - 1, None, ALU.bitwise_and))
                c(dve.tensor_scalar(part_i[:, 1, :], rank_i[:], P.bit_length() - 1, None, ALU.arith_shift_right))
                c.sync()
                c.step(dve.tensor_copy(g.rank_parts[:], part_i[:].rearrange("p a t -> p t a")))
                dve.wait_ge(ranked_in, 16)
                c(dve.tensor_copy(g.node_i[:], ranked[:, :, 0]))
                c(dve.tensor_copy(g.first_s[:], ranked[:, :, 1]))
                c.publish(dve.tensor_copy(g.deg_s[:], ranked[:, :, 2]), deg_set, 1)
                dve.wait_ge(pe_deg, 1)
                c.publish(dve.tensor_reduce(most_t[:], deg_ps[:], AX.X, ALU.max), most_set, 1)
                dve.wait_ge(pe_deg, 2)
                c.step(dve.tensor_copy(most_f[:], row_ps[:]))
                c.step(dve.tensor_reduce(most_all[:, 0:1], most_f[:], AX.X, ALU.max))
                c.step(dve.tensor_scalar(most_f[:], most_f[:], float(CHUNK + 1), float(CHUNK - 1), ALU.max, ALU.add))
                c.step(dve.tensor_scalar(most_all[:, 1:2], most_all[:, 0:1], 1.0, float(WIN - 1), ALU.max, ALU.add))
                c.step(dve.tensor_copy(counts[:, 0:TILES], most_f[:]))
                c.step(dve.tensor_copy(counts[:, TILES:TILES + 1], most_all[:, 1:2]))
                c.step(dve.tensor_scalar(g.loops[:, 0:TILES], counts[:, 0:TILES], CHUNK.bit_length() - 1, None,
                                         ALU.arith_shift_right))
                c.step(dve.tensor_scalar(g.loops[:, TILES:TILES + 1], counts[:, TILES:TILES + 1],
                                         WIN.bit_length() - 1, None, ALU.arith_shift_right))
                c.step(dve.tensor_copy(most_f[:], g.loops[:, 0:TILES]))
                c.step(dve.tensor_reduce(most_all[:, 0:1], most_f[:], AX.X, ALU.add))
                c.step(dve.tensor_scalar(most_all[:, 0:1], most_all[:, 0:1], -1.0, None, ALU.add))
                c.step(dve.tensor_copy(g.loops[:, TILES + 1:TILES + 2], most_all[:, 0:1]))


KEY_MAX, KEY_STEP = 4095, 4096


def stage_adjacency(nc, g):
    with ExitStack() as ctx:
        s = Scope(nc, ctx, "adj")
        at = s.sb("at", [P, TILES])
        at_i = s.sb("at_i", [P, TILES], I32)
        left = s.sb("left", [P, 2 * PAIRS])
        ids = s.sb("ids", [P, 2 * PAIRS, WIN], I32)
        ids2 = s.sb("ids2", [P, 2 * PAIRS, WIN], I32)
        outside = s.sb("outside", [P, 2 * PAIRS, WIN], BF16)
        lo_rows = s.sb("lo_rows", [P, 2 * PAIRS, WIN], BF16)
        hi_rows = s.sb("hi_rows", [P, 2 * PAIRS, WIN], BF16)
        lo_t = s.sb("lo_t", [P, PAIRS * P], BF16)
        hi_t = s.sb("hi_t", [P, PAIRS * P], BF16)
        hot_lo = [s.sb(f"hot_lo{b}", [P, NODES, P], BF16) for b in range(2)]
        hot_hi = [s.sb(f"hot_hi{b}", [P, NODES, TILES], BF16) for b in range(2)]
        ps = [[s.ps(f"ps{b}{h}", [P, NODES * TILES]) for h in range(2)] for b in range(2)]
        ps_t = s.ps("ps_t", [P, 2, P], BF16)
        turns = P // NODES // 2

        prepared, windows_in, rows_ready, turned, copied, hot_lo_n = map(
            s.sem, ("prepared", "windows_in", "rows_ready", "turned", "copied", "hot_lo_n"))
        hot_ready = [s.sem(f"hot_ready{b}") for b in range(2)]
        column_ready = [s.sem(f"column_ready{b}") for b in range(2)]
        moved = [[s.sem(f"moved{b}{h}") for h in range(2)] for b in range(2)]

        def each_group(eng, body):
            with eng.Fori(0, TILES // 2) as q:
                with eng.Fori(0, turns) as j:
                    for b in range(2):
                        body(b, (0, 1), q * turns + j, q, j)
            q = TILES // 2
            with eng.Fori(0, turns) as j:
                for b in range(2):
                    body(b, (0,), j + q * turns, q, j)

        with nc.Block() as block:
            @block.gpsimd
            def _(pool):
                pool.wait_ge(prepared, 3)
                for t in range(TILES):
                    pool.indirect_dma_start(ids[:, t, :], None, g.src_d[:].rearrange("(e o) -> e o", o=1),
                                            bass.IndirectOffsetOnAxis(at_i[:, t:t + 1], 0)).then_inc(windows_in, 16)
                pool.wait_ge(windows_in, 16 * TILES)

            @block.vector
            def _(dve):
                free(dve, *column_ready, *moved[0], *moved[1])
                c = Chain(dve, prepared)
                c(dve.memset(left[:], 0.0))
                c(dve.tensor_copy(at[:], g.first[:]))
                c.sync()
                c.step(dve.tensor_copy(at_i[:], at[:]))
                c(dve.tensor_copy(left[:, 0:TILES], g.deg[:]))
                c(dve.memset(ids[:, TILES:2 * PAIRS, :], 0))
                c.sync()
                c.step(dve.tensor_tensor(outside[:], g.const[:, C_IOTA:C_IOTA + WIN].unsqueeze(1)
                                         .broadcast_to([P, 2 * PAIRS, WIN]),
                                         spread(left[:], [P, 2 * PAIRS, WIN]), ALU.is_ge))
                dve.wait_ge(windows_in, 16 * TILES)
                c.step(dve.tensor_scalar(ids2[:], ids[:], P - 1, None, ALU.bitwise_and))
                c.step(dve.tensor_copy(lo_rows[:], ids2[:]))
                c.step(dve.tensor_scalar(ids2[:], ids[:], P.bit_length() - 1, None, ALU.arith_shift_right))
                dve.scalar_tensor_tensor(out=hi_rows[:], in0=outside[:], scalar=100.0, in1=ids2[:],
                                         op0=ALU.mult, op1=ALU.add).then_inc(rows_ready, 1)
                for q in range(PAIRS):
                    dve.wait_ge(turned, q + 1)
                    dve.tensor_copy(lo_t[:, q * P:(q + 1) * P], ps_t[:, 0, :]).then_inc(copied, 1)
                    dve.tensor_copy(hi_t[:, q * P:(q + 1) * P], ps_t[:, 1, :]).then_inc(copied, 1)
                dve.wait_ge(copied, 2 * PAIRS)

                def hot(b, halves, i, q, j):
                    dve.wait_ge(column_ready[b], i + 1)
                    col = q * P + j * (2 * NODES) + b * NODES
                    for n in range(NODES):
                        dve.tensor_scalar(hot_lo[b][:, n, :], g.iota_bf[:], lo_t[:, bass.ds(col + n, 1)], None, ALU.is_equal)
                    dve.tensor_tensor(hot_hi[b][:], spread(hi_t[:, bass.ds(col, NODES)], [P, NODES, TILES]),
                                      g.iota_bf[:, 0:TILES].unsqueeze(1).broadcast_to([P, NODES, TILES]),
                                      ALU.is_equal).then_inc(hot_ready[b], 1)

                each_group(dve, hot)

            @block.tensor
            def _(pe):
                pe.wait_ge(rows_ready, 1)
                for q in range(PAIRS):
                    if q:
                        pe.wait_ge(copied, 2 * q)
                    pe.transpose(ps_t[:, 0, :], lo_rows[:, 2 * q:2 * q + 2, :].rearrange("p t w -> p (t w)"), g.eye_bf[:])
                    pe.transpose(ps_t[:, 1, :], hi_rows[:, 2 * q:2 * q + 2, :].rearrange("p t w -> p (t w)"),
                                 g.eye_bf[:]).then_inc(turned, 1)

                def products(b, halves, i, q, j):
                    pe.wait_ge(hot_ready[b], i + 1)
                    for h in halves:
                        pe.wait_ge(moved[b][h], i + 1)
                    for n in range(NODES):
                        for h in halves:
                            mm = pe.matmul(ps[b][h][:, n * TILES:(n + 1) * TILES],
                                           hot_lo[b][h * WIN:(h + 1) * WIN, n, :],
                                           hot_hi[b][h * WIN:(h + 1) * WIN, n, :], start=True, stop=True)
                    mm.then_inc(column_ready[b], 1)

                each_group(pe, products)

            @block.scalar
            def _(act):
                def move(b, halves, i, q, j):
                    act.wait_ge(column_ready[b], i + 2)
                    for h in halves:
                        node = q * (2 * P) + j * (2 * NODES) + (b * NODES + h * P)
                        act.activation(g.A[:, :, bass.ds(node, NODES)],
                                       ps[b][h][:].rearrange("p (n s) -> p s n", n=NODES), ACT.Copy).then_inc(moved[b][h], 1)

                each_group(act, move)


def norm(dve, c, g, out, x, root_asked, root_done, asked):
    shape = [P, TILES, D]
    c.step(dve.tensor_reduce(g.mean[:], x, AX.X, ALU.add))
    c.step(dve.tensor_scalar(g.mean[:], g.mean[:], 1.0 / D, None, ALU.mult))
    c.step(dve.tensor_tensor(g.centred[:], x, spread(g.mean[:], shape), ALU.subtract))
    c.step(dve.tensor_tensor(g.squares[:], g.centred[:], g.centred[:], ALU.mult))
    c.step(dve.tensor_reduce(g.mean[:], g.squares[:], AX.X, ALU.add))
    c.step(dve.tensor_scalar(g.root_in[:], g.mean[:], 1.0 / D, LN_EPS, ALU.mult, ALU.add))
    asked[0] += 1
    dve.engine_nop().then_inc(root_asked, 1)
    dve.wait_ge(root_done, asked[0])
    c.step(dve.reciprocal(g.mean[:], g.root_in[:]))
    c.step(dve.tensor_tensor(out, g.centred[:], spread(g.mean[:], shape), ALU.mult))
    c.step(dve.tensor_scalar(out, out, 0.0, None, ALU.max))


class NodeOps:

    def __init__(self, dve, act_sem, chain):
        self.dve, self.c = dve, chain

    def tt(self, out, a, b, op):
        self.c.step(self.dve.tensor_tensor(out, a, b, op))

    def ts(self, out, a, s1, s2, op0, op1=None):
        self.c.step(self.dve.tensor_scalar(out, a, s1, s2, op0, op1) if op1 is not None
                    else self.dve.tensor_scalar(out, a, s1, None, op0))

    def reduce(self, out, a, op=ALU.add):
        self.c.step(self.dve.tensor_reduce(out, a, AX.X, op))


DENSE_TILES = 4
DENSE_STEPS = -(-TILES // DENSE_TILES)


def stage_layers01(nc, g, ins, debug=None):
    with ExitStack() as ctx:
        s = Scope(nc, ctx, "n01")
        dims = [(2 * D, 32), (64, D), (D, 32), (32, 64), (64, P), (P, 64), (64, 32), (32, D)]
        names = ["L0_gnn_b1", "L0_gnn_b2", "L1_gnn_b1", "L1_gnn_b2", "L1_gnn_b3", "L1_gnn_bl1", "L1_gnn_bl2", "L1_gnn_bl3"]
        weights = [[("L0_gnn_W1_l", 0, D), ("L0_gnn_W1_r", D, 2 * D)], [("L0_gnn_W2_l", 0, 32), ("L0_gnn_W2_r", 32, 64)],
                   [("L1_gnn_W1", 0, D)], [("L1_gnn_W2", 0, 32)], [("L1_gnn_W3", 0, 64)],
                   [("L1_gnn_Wl1", 0, P)], [("L1_gnn_Wl2", 0, 64)], [("L1_gnn_Wl3", 0, 32)]]
        widths = [D, 32, D, 32, 64]
        W = [s.sb(f"W{d}", [k, o]) for d, (k, o) in enumerate(dims)]
        bias = [s.sb(f"bias{d}", [P, o]) for d, (k, o) in enumerate(dims)]
        feat = s.sb("feat", [P, TILES, P])
        cat = s.sb("cat", [P, TILES, 64])
        rest = summed = feat[:, :, 64:P]
        parts = s.sb("parts", [P, TILES, 3, 64], BF16)
        inv_deg = s.sb("inv_deg", [P, TILES])
        dinv = s.sb("dinv", [P, TILES])
        junk = s.sb("junk", [P, NP], BF16)
        turned_sb = [s.sb(f"turned_sb{b}", [P, DENSE_TILES * P]) for b in range(2)]
        agg_ps = [s.ps(f"agg_ps{b}", [P, 512]) for b in range(2)]
        turn_ps = [s.ps(f"turn_ps{b}", [P, 512]) for b in range(2)]
        out_ps = [s.ps(f"out_ps{b}", [P, 512]) for b in range(2)]
        weights_in, dve_n, parts_ready, input_ready, turned, copied, dense_done, added = map(
            s.sem, ("weights_in", "dve_n", "parts_ready", "input_ready", "turned", "copied", "dense_done", "added"))
        agg_done = [s.sem(f"agg_done{b}") for b in range(2)]
        agg_read = [s.sem(f"agg_read{b}") for b in range(2)]
        out_done, root_asked, root_done = s.sem("out_done"), s.sem("root_asked"), s.sem("root_done")
        agg_order = {0: 0, 1: 1, 2: 2, 3: 3, 4: 4}
        even, odd = (TILES + 1) // 2, TILES // 2

        def parts_view(a):
            w = widths[a]
            return parts[:].rearrange("p t s f -> p (t s f)")[:, 0:TILES * 3 * w].rearrange("p (t k) -> p t k", t=TILES)

        def tiles_of(step):
            return range(step * DENSE_TILES, min(TILES, (step + 1) * DENSE_TILES))

        with nc.Block() as block:
            @block.sync
            def _(sp):
                n = 0
                for d, rows in enumerate(weights):
                    for name, a, b in rows:
                        sp.dma_start(W[d][a:b, :], ins[name]).then_inc(weights_in, 16)
                        n += 1
                for d, name in enumerate(names):
                    o = dims[d][1]
                    sp.dma_start(bias[d][:], ins[name].unsqueeze(0).broadcast_to([P, o])).then_inc(weights_in, 16)
                    n += 1
                sp.wait_ge(weights_in, 16 * n)
                assert n == LOADS

            @block.tensor
            def _(pe):
                pe.wait_ge(weights_in, 16 * LOADS)

                def aggregate(a):
                    w = widths[a]
                    pe.wait_ge(parts_ready, a + 1)

                    def tile(b, i, t):
                        pe.wait_ge(agg_read[b], i + 1)
                        for shi in range(TILES):
                            mm = pe.matmul(agg_ps[b][:, 0:3 * w], g.A[:, shi, bass.ds(t * P, P)],
                                           parts_view(a)[:, shi, :], start=shi == 0, stop=shi == TILES - 1)
                        mm.then_inc(agg_done[b], 1)

                    with pe.Fori(0, TILES // 2) as i:
                        for b in range(2):
                            tile(b, i + a * (even if b == 0 else odd), i * 2 + b)
                    tile(0, TILES // 2 + a * even, TILES - 1)

                def dense(d):
                    k, o = dims[d]
                    source = cat if d < 5 else feat
                    for step in range(DENSE_STEPS):
                        n = d * DENSE_STEPS + step
                        b = n % 2
                        tiles = tiles_of(step)
                        if step == 0:
                            pe.wait_ge(input_ready, d + 1)
                        if n >= 2:
                            pe.wait_ge(copied, n - 1)
                        for t in tiles:
                            mm = pe.transpose(turn_ps[b][0:k, (t - tiles[0]) * P:(t - tiles[0] + 1) * P],
                                              source[:, t, 0:k], g.const[:, C_EYE:C_EYE + P])
                        mm.then_inc(turned, 1)
                        if step:
                            products(d, step - 1)
                    products(d, DENSE_STEPS - 1)

                def products(d, step):
                    k, o = dims[d]
                    n = d * DENSE_STEPS + step
                    b = n % 2
                    tiles = tiles_of(step)
                    pe.wait_ge(copied, n + 1)
                    if n >= 2:
                        pe.wait_ge(added, n - 1)
                    for t in tiles:
                        at = t - tiles[0]
                        mm = pe.matmul(out_ps[b][:, at * o:(at + 1) * o], turned_sb[b][0:k, at * P:(at + 1) * P],
                                       W[d][:], start=True, stop=True)
                    mm.then_inc(dense_done, 1)

                for d in range(len(dims)):
                    if d < 5:
                        aggregate(d)
                    dense(d)

            @block.scalar
            def _(act):
                def outs(d):
                    for shi in range(5 * d, 5 * d + 5):
                        if shi:
                            act.wait_ge(out_done, shi)
                        act.activation(junk[:], g.A[:, shi, :], ACT.Copy,
                                       accum_out=g.outs[:, shi:shi + 1]).then_inc(out_done, 1)

                def roots(n):
                    act.wait_ge(root_asked, n)
                    act.activation(g.root_in[:], g.root_in[:], ACT.Sqrt).then_inc(root_done, 1)

                def copies(d):
                    k = dims[d][0]
                    for step in range(DENSE_STEPS):
                        n = d * DENSE_STEPS + step
                        b, tiles = n % 2, tiles_of(step)
                        act.wait_ge(turned, n + 1)
                        if n >= 2:
                            act.wait_ge(dense_done, n - 1)
                        act.activation(turned_sb[b][0:k, 0:len(tiles) * P], turn_ps[b][0:k, 0:len(tiles) * P],
                                       ACT.Copy).then_inc(copied, 1)

                roots(1)
                for d in range(8):
                    if d == 2:
                        roots(2)
                        roots(3)
                    if d < 5:
                        outs(d)
                    copies(d)
                roots(4)
                roots(5)

            @block.vector
            def _(dve):
                c = Chain(dve, dve_n)
                ops = NodeOps(dve, None, c)
                asked = [0]
                free(dve, *agg_read)

                def norm_relu(out, x):
                    norm(dve, c, g, out, x, root_asked, root_done, asked)

                def aggregate(a, source):
                    w = widths[a]
                    p3 = parts_view(a)
                    for part in range(3):
                        now = p3[:, :, part * w:(part + 1) * w]
                        cur = source if part == 0 else rest[:, :, 0:w]
                        ins_ = dve.tensor_copy(now, cur)
                        if part == 2:
                            ins_.then_inc(parts_ready, 1)
                        else:
                            c.step(ins_)
                            ops.tt(rest[:, :, 0:w], cur, now, ALU.subtract)

                    def tile(b, i, t):
                        dve.wait_ge(agg_done[b], i + 1)
                        dve.tensor_reduce(summed[:, bass.ds(t, 1), 0:w],
                                          agg_ps[b][:, 0:3 * w].rearrange("p (s f) -> p f s", f=w), AX.X,
                                          ALU.add).then_inc(agg_read[b], 1)

                    with dve.Fori(0, TILES // 2) as i:
                        for b in range(2):
                            tile(b, i + a * (even if b == 0 else odd), i * 2 + b)
                    tile(0, TILES // 2 + a * even, TILES - 1)
                    dve.wait_ge(agg_read[0], (a + 1) * even + 1)
                    dve.wait_ge(agg_read[1], (a + 1) * odd + 1)

                def dense(d, relu):
                    k, o = dims[d]
                    dve.engine_nop().then_inc(input_ready, 1)
                    for step in range(DENSE_STEPS):
                        n = d * DENSE_STEPS + step
                        b, tiles = n % 2, tiles_of(step)
                        dve.wait_ge(dense_done, n + 1)
                        m = len(tiles)
                        dve.tensor_tensor(feat[:, tiles[0]:tiles[0] + m, 0:o],
                                          out_ps[b][:, 0:m * o].rearrange("p (t o) -> p t o", o=o),
                                          bias[d][:].unsqueeze(1).broadcast_to([P, m, o]), ALU.add).then_inc(added, 1)
                    dve.wait_ge(added, (d + 1) * DENSE_STEPS)
                    if relu:
                        ops.ts(feat[:, :, 0:o], feat[:, :, 0:o], 0.0, None, ALU.max)

                dve.wait_ge(weights_in, 16 * LOADS)
                norm_relu(g.h[:], g.x[:])
                ops.ts(inv_deg[:], g.deg[:], 1.0, None, ALU.max)
                c.step(dve.reciprocal(inv_deg[:], inv_deg[:]))
                aggregate(0, g.h[:])
                ops.tt(cat[:, :, 0:D], summed[:, :, 0:D], spread(inv_deg[:], [P, TILES, D]), ALU.mult)
                ops.ts(cat[:, :, D:2 * D], g.h[:], 0.0, None, ALU.add)
                dense(0, True)
                aggregate(1, feat[:, :, 0:32])
                ops.tt(cat[:, :, 0:32], summed[:, :, 0:32], spread(inv_deg[:], [P, TILES, 32]), ALU.mult)
                ops.ts(cat[:, :, 32:64], feat[:, :, 0:32], 0.0, None, ALU.add)
                dense(1, False)
                ops.tt(g.x[:], g.x[:], feat[:, :, 0:D], ALU.add)
                norm_relu(g.h[:], g.x[:])
                ops.ts(g.root_in[:], g.deg[:], 1.0, None, ALU.add)
                asked[0] += 1
                dve.engine_nop().then_inc(root_asked, 1)
                dve.wait_ge(root_done, asked[0])
                c.step(dve.reciprocal(dinv[:], g.root_in[:]))
                source = g.h[:]
                for a in (2, 3, 4):
                    w = widths[a]
                    scale = spread(dinv[:], [P, TILES, w])
                    ops.tt(cat[:, :, 0:w], source, scale, ALU.mult)
                    aggregate(a, cat[:, :, 0:w])
                    ops.tt(cat[:, :, 0:w], cat[:, :, 0:w], summed[:, :, 0:w], ALU.add)
                    ops.tt(cat[:, :, 0:w], cat[:, :, 0:w], scale, ALU.mult)
                    dense(a, True)
                    source = feat[:, :, 0:dims[a][1]]
                for d in (5, 6, 7):
                    dense(d, True)
                ops.tt(g.x[:], g.x[:], feat[:, :, 0:D], ALU.add)
                norm_relu(g.h[:], g.x[:])
                dve.wait_ge(out_done, TILES)
                ops.tt(g.root_in[:], g.deg[:], g.outs[:], ALU.add)
                ops.ts(g.root_in[:], g.root_in[:], 1e-5, None, ALU.max)
                asked[0] += 1
                dve.engine_nop().then_inc(root_asked, 1)
                dve.wait_ge(root_done, asked[0])
                c.step(dve.reciprocal(g.dinv2[:], g.root_in[:]))



LOADS = 10 + 8


ROW = 2 + 2 * D
OWN = ROW + D + 2


def stage_sheaf(nc, g, ins):
    with ExitStack() as ctx:
        s = Scope(nc, ctx, "shf")
        table = s.sb("table", [P, TILES, OWN])
        own = s.sb("own", [P, TILES, OWN])
        W1 = s.sb("W1", [P, P])
        W2 = s.sb("W2", [P, 3 * D])
        b1 = s.sb("b1", [P, 1])
        b2 = s.sb("b2", [P, 3, D])
        cur = s.sb("cur", [P, 1])
        at_i = s.sb("at_i", [P, 1], I32)
        ids_next = s.sb("ids_next", [P, CHUNK], I32)
        ids = [s.sb(f"ids{h}", [P, HALF], I32) for h in range(2)]
        rows = [s.sb(f"rows{h}", [P, HALF, ROW]) for h in range(2)]
        h_pair = s.sb("h_pair", [P, CHUNK, 4, D])
        y_pair = s.sb("y_pair", [P, 2, CHUNK, 2, D])
        rank_s = s.sb("rank_s", [P, 2, CHUNK, 2])
        turned_sb = s.sb("turned_sb", [P, 4 * P])
        hidden = [s.sb(f"hidden{h}", [P, 4 * P]) for h in range(2)]
        left = s.sb("left", [P, 1])
        over, keep = s.sb("over", [P, CHUNK]), s.sb("keep", [P, CHUNK])
        src_hi = s.sb("src_hi", [P, CHUNK, 1])
        v = s.sb("v", [P, CHUNK, 3, D])
        vv = s.sb("vv", [P, CHUNK, 3, D])
        c2 = s.sb("c2", [P, CHUNK, 3])
        prod = s.sb("prod", [P, CHUNK, 2, D])
        dots = s.sb("dots", [P, CHUNK, 2])
        u = s.sb("u", [P, CHUNK, 2, D])
        msg = s.sb("msg", [P, 2, CHUNK, D])
        own_sum = s.sb("own_sum", [P, CHUNK, D])
        to_dst = s.sb("to_dst", [P, TILES, D])
        hot_lo = s.sb("hot_lo", [P, CHUNK, P])
        hot_hi = s.sb("hot_hi", [P, CHUNK, TILES])
        wide = s.sb("wide", [P, CHUNK, TILES, D])
        zeros = s.sb("zeros", [P, TILES * D])
        turn_ps = s.ps("turn_ps", [P, 4 * P])
        hid_ps = [s.ps(f"hid_ps{h}", [P, 4 * P]) for h in range(2)]
        v_ps = s.ps("v_ps", [P, 512])
        sum_ps = s.ps("sum_ps", [P, 512])
        loaded, chain_a, chain_t, chain_c, table_ready, table_out, own_in, own_set = map(
            s.sem, ("loaded", "chain_a", "chain_t", "chain_c", "table_ready", "table_out", "own_in", "own_set"))
        zeroed, steps_own, ids_in, turned, copied, hid_done, hid_ready, v_done, v_read = map(
            s.sem, ("zeroed", "steps_own", "ids_in", "turned", "copied", "hid_done", "hid_ready",
                    "v_done", "v_read"))
        pair_read, wide_ready, wide_used, summed, root_asked, root_done, h_ready, h_out = map(
            s.sem, ("pair_read", "wide_ready", "wide_used", "summed", "root_asked", "root_done", "h_ready", "h_out"))
        gathered = [s.sem(f"gathered{h}") for h in range(2)]
        rows_free = [s.sem(f"rows_free{h}") for h in range(2)]

        with nc.Block() as block:
            @block.sync
            def _(sp):
                n = 0
                sp.wait_ge(zeroed, 4)
                w1, w2 = ins["L2_gnn_W1"].rearrange("h k -> k h"), ins["L2_gnn_W2"].rearrange("o h -> h o")
                for half in range(2):
                    o = half * 64
                    for row, col, part in ((0, 0, 0), (32, 0, 1), (32, HID, 0), (0, HID, 1)):
                        sp.dma_start(W1[o + row:o + row + D, col:col + HID], w1[part * D:(part + 1) * D, :],
                                     allow_slow_non_contiguous=True).then_inc(loaded, 16)
                        n += 1
                for row, col in ((0, 0), (HID, D), (0, 2 * D)):
                    sp.dma_start(W2[row:row + HID, col:col + D], w2, allow_slow_non_contiguous=True).then_inc(loaded, 16)
                    n += 1
                for half in range(2):
                    sp.dma_start(b1[half * HID:(half + 1) * HID, :],
                                 ins["L2_gnn_b1"].rearrange("(h o) -> h o", o=1)).then_inc(loaded, 16)
                    n += 1
                sp.dma_start(b2[:], ins["L2_gnn_b2"].unsqueeze(0).unsqueeze(0).broadcast_to([P, 3, D])).then_inc(loaded, 16)
                assert n + 1 == SHEAF_LOADS
                sp.wait_ge(table_ready, 1)
                sp.dma_start(g.table_d[:].rearrange("(t p) c -> p t c", p=P), table[:]).then_inc(table_out, 16)
                sp.wait_ge(table_out, 16)
                sp.wait_ge(loaded, 16 * SHEAF_LOADS)

            @block.gpsimd
            def _(pool):
                for zero in (W1, W2, zeros, b1, h_pair):
                    pool.memset(zero[:], 0.0).then_inc(zeroed, 1)
                pool.memset(at_i[:], 0).then_inc(zeroed, 1)
                free(pool, steps_own)
                pool.wait_ge(zeroed, 6)
                pool.wait_ge(table_out, 16)
                edges = g.src_d[:].rearrange("(e o) -> e o", o=1)
                spare = bass.IndirectOffsetOnAxis(at_i[:, 0:1], 0)
                pool.indirect_dma_start(ids_next[:], None, edges, spare).then_inc(ids_in, 16)
                for h in range(2):
                    pool.indirect_dma_start(rows[h][:, 0, :], None, g.table_d[:], spare).then_inc(gathered[h], 16)
                for t in range(TILES):
                    pool.indirect_dma_start(own[:, t, :], None, g.table_d[:],
                                            bass.IndirectOffsetOnAxis(g.node_i[:, t:t + 1], 0)).then_inc(own_in, 16)
                for landed in (ids_in, *gathered):
                    pool.wait_ge(landed, 16)
                k_reg, reg = pool.alloc_register("shf_pool_k"), pool.alloc_register("shf_pool_value")
                pool.reg_mov(k_reg, 0)
                pool.reg_mov(reg, 0)
                with pool.Fori(0, TILES) as t:
                    k = pool.snap(k_reg)
                    pool.wait_ge(ids_in, settled(pool, reg, zeroed, k * 16 + (t * 16 + 16)))
                    pool.wait_ge(steps_own, settled(pool, reg, zeroed, k * 4 + (t * 2 + 1)))
                    pool.tensor_copy(cur[:], g.first_s[:, bass.ds(t, 1)]).then_inc(steps_own, 1)
                    pool.wait_ge(steps_own, settled(pool, reg, zeroed, k * 4 + (t * 2 + 2)))
                    pool.tensor_copy(at_i[:], cur[:]).then_inc(steps_own, 1)
                    pool.wait_ge(steps_own, settled(pool, reg, zeroed, k * 4 + (t * 2 + 3)))
                    pool.indirect_dma_start(ids_next[:], None, edges, bass.IndirectOffsetOnAxis(at_i[:, 0:1], 0)).then_inc(ids_in, 16)
                    chunks = pool.value_load(g.loops[0:1, bass.ds(t, 1)], min_val=2, max_val=E)
                    with pool.Fori(0, chunks):
                        k = pool.snap(k_reg)
                        base = k * 4 + (t * 2 + 3)
                        pool.wait_ge(ids_in, settled(pool, reg, zeroed, k * 16 + (t * 16 + 32)))
                        for h in range(2):
                            pool.wait_ge(gathered[h], settled(pool, reg, zeroed, k * (16 * HALF) + 16))
                            pool.tensor_copy(ids[h][:], ids_next[:, h * HALF:(h + 1) * HALF]).then_inc(steps_own, 1)
                            pool.wait_ge(steps_own, settled(pool, reg, zeroed, base + (h + 1)))
                            if h == 1:
                                pool.tensor_scalar(cur[:], cur[:], float(CHUNK), float(E), ALU.add, ALU.min).then_inc(steps_own, 1)
                                pool.wait_ge(steps_own, settled(pool, reg, zeroed, base + 3))
                                pool.tensor_copy(at_i[:], cur[:]).then_inc(steps_own, 1)
                                pool.wait_ge(steps_own, settled(pool, reg, zeroed, base + 4))
                                pool.indirect_dma_start(ids_next[:], None, edges,
                                                        bass.IndirectOffsetOnAxis(at_i[:, 0:1], 0)).then_inc(ids_in, 16)
                            pool.wait_ge(rows_free[h], settled(pool, reg, zeroed, k + 1))
                            for r in range(HALF):
                                pool.indirect_dma_start(rows[h][:, r, :], None, g.table_d[:],
                                                        bass.IndirectOffsetOnAxis(ids[h][:, r:r + 1], 0)).then_inc(gathered[h], 16)
                        pool.reg_add(k_reg, k_reg, 1)
                k = pool.snap(k_reg)
                pool.wait_ge(ids_in, settled(pool, reg, zeroed, k * 16 + (16 * TILES + 16)))
                pool.wait_ge(h_ready, 1)
                for t in range(TILES):
                    pool.indirect_dma_start(g.h_d[:], bass.IndirectOffsetOnAxis(g.node_i[:, t:t + 1], 0),
                                            g.h[:, t, :], None).then_inc(h_out, 16)
                pool.wait_ge(h_out, 16 * TILES)

            @block.tensor
            def _(pe):
                def form(k):
                    pe.wait_ge(rows_free[1], k + 2)
                    pe.wait_ge(copied, k + 1)
                    for j in range(CHUNK // 2):
                        mm = pe.transpose(turn_ps[:, j * P:(j + 1) * P],
                                          h_pair[:, 2 * j:2 * j + 2].rearrange("p t a d -> p (t a d)"),
                                          g.const[:, C_EYE:C_EYE + P])
                    mm.then_inc(turned, 1)
                    pe.wait_ge(copied, k + 2)
                    pe.wait_ge(hid_ready, k * 2 + 1)
                    for h in range(2):
                        pe.matmul(hid_ps[h][:], W1[64 * h:64 * h + 64, :], turned_sb[64 * h:64 * h + 64, :],
                                  start=True, stop=True).then_inc(hid_done, 1)
                    pe.wait_ge(hid_ready, k * 2 + 3)
                    pe.wait_ge(v_read, k + 1)
                    for t in range(CHUNK):
                        j, h = t // 2, t % 2
                        mm = pe.matmul(v_ps[:, t * 3 * D:(t + 1) * 3 * D], hidden[h][:, j * P:(j + 1) * P], W2[:],
                                       start=True, stop=True)
                    mm.then_inc(v_done, 1)

                def add(k):
                    for half in range(2):
                        pe.wait_ge(wide_ready, k * 2 + (half + 1))
                        for t in range(half * HALF, (half + 1) * HALF):
                            mm = pe.matmul(sum_ps[:, 0:TILES * D], hot_lo[:, t, :], wide[:, t].rearrange("p s d -> p (s d)"),
                                           start=False, stop=False, skip_group_check=True)
                        mm.then_inc(wide_used, 1)

                pe.wait_ge(loaded, 16 * SHEAF_LOADS)
                pe.wait_ge(zeroed, 6)
                pe.matmul(sum_ps[:, 0:TILES * D], zeros[:, 0:P], zeros[:], start=True, stop=False, skip_group_check=True)
                form(0)
                last = pe.value_load(g.loops[0:1, TILES + 1:TILES + 2], min_val=2 * TILES - 1, max_val=E)
                with pe.Fori(0, last) as k:
                    form(k + 1)
                    add(k)
                add(last)
                pe.matmul(sum_ps[:, 0:TILES * D], zeros[:, 0:P], zeros[:], start=False, stop=True,
                          skip_group_check=True).then_inc(summed, 1)

            @block.scalar
            def _(act):
                act.wait_ge(loaded, 16 * SHEAF_LOADS)
                act.wait_ge(zeroed, 6)
                act.wait_ge(own_in, 16 * TILES)
                k_reg = act.alloc_register("shf_act_k")
                act.reg_mov(k_reg, 0)
                with act.Fori(0, TILES) as t:
                    chunks = act.value_load(g.loops[0:1, bass.ds(t, 1)], min_val=2, max_val=E)
                    with act.Fori(0, chunks):
                        k = act.snap(k_reg)
                        even_odd = bass.ds(k % 2, 1)
                        own_row = own[:, bass.ds(t, 1), :]
                        act.wait_ge(turned, k + 1)
                        act.wait_ge(pair_read, k + 1)
                        act.activation(h_pair[:, :, 2, :], own_row[:, :, 2:2 + D].broadcast_to([P, CHUNK, D]), ACT.Copy)
                        act.activation(y_pair[:, even_odd, :, 1, :].rearrange("p o t d -> p (o t) d"),
                                       own_row[:, :, 2 + D:ROW].broadcast_to([P, CHUNK, D]), ACT.Copy)
                        for h in range(2):
                            slots = slice(h * HALF, (h + 1) * HALF)
                            act.wait_ge(gathered[h], k * (16 * HALF) + (16 * HALF + 16))
                            act.activation(y_pair[:, even_odd, slots, 0, :].rearrange("p o t d -> p (o t) d"),
                                           rows[h][:, :, 2 + D:ROW], ACT.Copy)
                            act.activation(rank_s[:, even_odd, slots, :].rearrange("p o t d -> p (o t) d"),
                                           rows[h][:, :, 0:2], ACT.Copy)
                            done = act.activation(h_pair[:, slots, 0, :], rows[h][:, :, 2:2 + D], ACT.Copy)
                            done.then_inc(rows_free[h], 1)
                        act.wait_ge(turned, k + 2)
                        act.wait_ge(hid_done, k * 2 + 1)
                        act.activation(turned_sb[:], turn_ps[:], ACT.Copy).then_inc(copied, 1)
                        act.wait_ge(v_done, k + 1)
                        for h in range(2):
                            act.wait_ge(hid_done, k * 2 + (h + 2))
                            act.activation(hidden[h][:], hid_ps[h][:], ACT.Relu, bias=b1[:, 0:1]).then_inc(hid_ready, 1)
                        act.reg_add(k_reg, k_reg, 1)
                act.wait_ge(root_asked, 1)
                act.activation(g.root_in[:], g.root_in[:], ACT.Sqrt).then_inc(root_done, 1)

            @block.vector
            def _(dve):
                free(dve, turned, copied, hid_done, hid_ready, v_done, v_read, wide_used, pair_read, pair_read, *rows_free)
                c = Chain(dve, chain_a)
                c(dve.memset(table[:, :, OWN - 1], 0.0))
                c(dve.tensor_copy(table[:, :, 0:2], g.rank_parts[:]))
                c(dve.tensor_copy(table[:, :, 2:2 + D], g.h[:]))
                c(dve.tensor_tensor(table[:, :, 2 + D:ROW], g.h[:], spread(g.dinv2[:], [P, TILES, D]), ALU.mult))
                c(dve.tensor_copy(table[:, :, ROW:ROW + D], g.x[:]))
                c.publish(dve.tensor_copy(table[:, :, ROW + D], g.dinv2[:]), table_ready, 1)
                c.sync()
                dve.wait_ge(loaded, 16 * SHEAF_LOADS)
                before = c.n

                def step(c, k):
                    even_odd = bass.ds(k % 2, 1)
                    y = y_pair[:, even_odd].rearrange("p o t a d -> p (o t) a d")
                    rank = rank_s[:, even_odd].rearrange("p o t a -> p (o t) a")
                    shape = [P, CHUNK, 2, D]
                    iota = g.const[:, C_IOTA:C_IOTA + CHUNK]
                    c(dve.tensor_scalar(over[:], iota, left[:, 0:1], None, ALU.is_ge))
                    c(dve.tensor_scalar(keep[:], iota, left[:, 0:1], None, ALU.is_lt))
                    c.sync()
                    c(dve.tensor_scalar(left[:], left[:], float(-CHUNK), None, ALU.add))
                    dve.wait_ge(v_done, k + 2)
                    c.publish(dve.tensor_tensor(v[:], v_ps[:, 0:CHUNK * 3 * D].rearrange("p (t a d) -> p t a d", t=CHUNK, a=3),
                                                b2[:].unsqueeze(1).broadcast_to([P, CHUNK, 3, D]), ALU.add),
                              v_read, k + 2)
                    c(dve.tensor_tensor(vv[:], v[:], v[:], ALU.mult))
                    dve.wait_ge(rows_free[1], k + 2)
                    c(dve.scalar_tensor_tensor(out=src_hi[:], in0=over[:].unsqueeze(2), scalar=1000.0, in1=rank[:, :, 1:2],
                                               op0=ALU.mult, op1=ALU.add))
                    c(dve.tensor_tensor(y[:, :, 0, :], y[:, :, 0, :], spread(keep[:], [P, CHUNK, D]), ALU.mult))
                    c.sync()
                    c.step(dve.tensor_reduce(c2[:], vv[:], AX.X, ALU.add))
                    c.step(dve.tensor_scalar(c2[:], c2[:], 1e-24, 0.5, ALU.max, ALU.mult))
                    c.step(dve.reciprocal(c2[:], c2[:]))

                    def reflect(out, vec, scale, x):
                        c.step(dve.tensor_tensor(prod[:], vec, x, ALU.mult))
                        c.step(dve.tensor_reduce(dots[:], prod[:], AX.X, ALU.add))
                        c.step(dve.tensor_tensor(dots[:], dots[:], scale, ALU.mult))
                        c.step(dve.tensor_tensor(prod[:], vec, spread(dots[:], shape), ALU.mult))
                        c.step(dve.tensor_tensor(out, x, prod[:], ALU.subtract))

                    reflect(u[:], v[:, :, 0:2, :], c2[:, :, 0:2], y)
                    reflect(msg[:].rearrange("p a t d -> p t a d"), v[:, :, 1:3, :], c2[:, :, 1:3], u[:])
                    c(dve.tensor_tensor(own_sum[:], own_sum[:], msg[:, 0], ALU.add))
                    dve.wait_ge(wide_used, k * 2 + 1)
                    for t in range(CHUNK):
                        hot = dve.tensor_scalar(hot_lo[:, t, :], g.const[:, C_IOTA:C_IOTA + P], rank[:, t, 0:1],
                                                None, ALU.is_equal)
                    hot.then_inc(pair_read, 1)
                    c.step(dve.tensor_tensor(hot_hi[:], spread(src_hi[:, :, 0], [P, CHUNK, TILES]),
                                             g.const[:, C_IOTA:C_IOTA + TILES].unsqueeze(1).broadcast_to([P, CHUNK, TILES]),
                                             ALU.is_equal))
                    for half in range(2):
                        slots, shape_w = slice(half * HALF, (half + 1) * HALF), [P, HALF, TILES, D]
                        dve.tensor_tensor(wide[:, slots], spread(hot_hi[:, slots, :], shape_w),
                                          msg[:, 1, slots].unsqueeze(2).broadcast_to(shape_w), ALU.mult).then_inc(wide_ready, 1)
                    assert c.n == SHEAF_STEPS, c.n

                k_reg = dve.alloc_register("shf_dve_k")
                dve.reg_mov(k_reg, 0)
                with dve.Fori(0, TILES) as t:
                    ct = Chain(dve, chain_t, t * 3)
                    ct(dve.tensor_copy(left[:], g.deg_s[:, bass.ds(t, 1)]))
                    ct(dve.memset(own_sum[:], 0.0))
                    ct.sync()
                    chunks = dve.value_load(g.loops[0:1, bass.ds(t, 1)], min_val=2, max_val=E)
                    with dve.Fori(0, chunks):
                        k = dve.snap(k_reg)
                        step(Chain(dve, chain_c, k * SHEAF_STEPS), k)
                        dve.reg_add(k_reg, k_reg, 1)
                    dve.wait_ge(chain_c, dve.snap(k_reg) * SHEAF_STEPS)
                    ct.step(dve.tensor_reduce(to_dst[:, bass.ds(t, 1), :].rearrange("p o d -> p (o d)"),
                                              own_sum[:].rearrange("p t d -> p d t"), AX.X, ALU.add))
                dve.wait_ge(summed, 1)
                c = Chain(dve, chain_a, before)
                shape = [P, TILES, D]
                c.step(dve.tensor_tensor(to_dst[:], sum_ps[:, 0:TILES * D].rearrange("p (t d) -> p t d", t=TILES), to_dst[:], ALU.add))
                c.step(dve.tensor_tensor(to_dst[:], to_dst[:], own[:, :, ROW + D:ROW + D + 1].broadcast_to(shape), ALU.mult))
                c.step(dve.tensor_tensor(to_dst[:], to_dst[:], own[:, :, 2:2 + D], ALU.add))
                c.step(dve.tensor_scalar(to_dst[:], to_dst[:], 0.0, None, ALU.max))
                c.step(dve.tensor_tensor(g.x[:], own[:, :, ROW:ROW + D], to_dst[:], ALU.add))
                norm(dve, c, g, g.h[:], g.x[:], root_asked, root_done, [0])
                dve.engine_nop().then_inc(h_ready, 1)


SHEAF_LOADS = 8 + 3 + 2 + 1
SHEAF_STEPS = 3 + 3 + 3 + 10 + 1 + 1


def stage_attention(nc, g, ins, out):
    C2 = D * D
    with ExitStack() as ctx:
        s = Scope(nc, ctx, "att")
        wf = s.sb("wf", [P, 2 * C2])
        wr = s.sb("wr", [P, 2 * C2])
        wp = [s.sb(f"wp{i}", [P, 2 * C2], BF16) for i in range(3)]
        w6 = s.sb("w6", [P, 2 * C2], BF16)
        cur = s.sb("cur", [P, 1])
        at_i = s.sb("at_i", [P, 1], I32)
        ids_next = s.sb("ids_next", [P, CHUNK], I32)
        ids = [s.sb(f"ids{h}", [P, HALF], I32) for h in range(2)]
        ea = s.sb("ea", [P, CHUNK, P], BF16)
        ea_t = [s.sb(f"ea_t{h}", [P, HALF, P], BF16) for h in range(2)]
        hs = [s.sb(f"hs{h}", [P, HALF, D]) for h in range(2)]
        e12_all = s.sb("e12", [P, 2, 2, HALF, 2 * C2])
        top, top_was, shift = s.sb("top", [P, C2]), s.sb("top_was", [P, C2]), s.sb("shift", [P, C2])
        top_odd = s.sb("top_odd", [P, C2])
        decay = s.sb("decay", [P, C2])
        sums = s.sb("sums", [P, 2, C2])
        left, over = s.sb("left", [P, 1]), s.sb("over", [P, CHUNK])
        off_max, off_exp = s.sb("off_max", [P, CHUNK]), s.sb("off_exp", [P, CHUNK])
        ratio = s.sb("ratio", [P, C2])
        ft = s.sb("ft", [P, TILES + 1, D])
        zeros = s.sb("zeros", [P, 2 * C2])
        warm = s.sb("warm", [P, 1])
        w_ps = [s.ps(f"w_ps{r}", [P, 2 * C2]) for r in range(HALF)]
        t_ps = s.ps("t_ps", [P, HALF, P], BF16)
        sum_ps = s.ps("sum_ps", [P, 2 * C2])
        w_in, zeroed, w_ready_s, chain0, chain_f, chain_l, own = map(
            s.sem, ("w_in", "zeroed", "w_ready", "chain0", "chain_f", "chain_l", "own"))
        ids_in, ea_in, shift_ready, decay_ready, sums_done, sum_added, stored = map(
            s.sem, ("ids_in", "ea_in", "shift_ready", "decay_ready", "sums_done", "sum_added", "stored"))
        hs_in, turned, ea_t_ready, w_done, w_used, sub_ready, exp_ready, num_ready, half_done = (
            [s.sem(f"{name}{h}") for h in range(2)] for name in
            ("hs_in", "turned", "ea_t_ready", "w_done", "w_used", "sub_ready", "exp_ready", "num_ready", "half_done"))

        def e12(k, h, r=None):
            half = e12_all[:, bass.ds(k % 2, 1), h, :, :].rearrange("p o r c -> p (o r) c")
            return half if r is None else half[:, r, :]

        def last_chunk(eng):
            return eng.value_load(g.loops[0:1, TILES + 1:TILES + 2], min_val=2 * TILES - 1, max_val=E)

        with nc.Block() as block:
            @block.sync
            def _(sp):
                sp.wait_ge(zeroed, 2)
                n = 0
                for col, w, bias in ((0, "L3_gnn_W_msg", "L3_gnn_b_msg"), (C2, "L3_gnn_W_attn", "L3_gnn_b_attn")):
                    for part in range(6):
                        sp.dma_start(wf[part * D:(part + 1) * D, col:col + C2], ins[w]).then_inc(w_in, 16)
                        n += 1
                    for part in range(3):
                        sp.dma_start(wf[6 * D + part:6 * D + part + 1, col:col + C2], ins[bias].rearrange("(a n) -> a n", a=1)).then_inc(w_in, 16)
                        n += 1
                assert n == 18
                sp.wait_ge(w_in, 16 * n)

            @block.gpsimd
            def _(pool):
                pool.memset(wf[:], 0.0).then_inc(zeroed, 1)
                pool.memset(zeros[:], 0.0).then_inc(zeroed, 1)
                k_reg = pool.alloc_register("att_pool_k")
                pool.reg_mov(k_reg, 0)
                reg = pool.alloc_register("att_pool_carrier")
                pool.reg_mov(reg, 0)
                free(pool, own)
                edges = g.src_d[:].rearrange("(e o) -> e o", o=1)
                pool.memset(at_i[:], 0).then_inc(zeroed, 1)
                pool.wait_ge(zeroed, 3)
                spare = bass.IndirectOffsetOnAxis(at_i[:, 0:1], 0)
                pool.indirect_dma_start(ids_next[:], None, edges, spare).then_inc(ids_in, 16)
                pool.indirect_dma_start(ea[:].rearrange("p c k -> p (c k)"), None, g.ea6_d[:], spare).then_inc(ea_in, 16)
                for h in range(2):
                    pool.indirect_dma_start(hs[h][:, 0, :], None, g.h_d[:], spare).then_inc(hs_in[h], 16)
                for gathered in (ids_in, ea_in, *hs_in):
                    pool.wait_ge(gathered, 16)
                with pool.Fori(0, TILES) as t:
                    k = pool.snap(k_reg)
                    pool.wait_ge(ids_in, settled(pool, reg, zeroed, k * 16 + (t * 16 + 16)))
                    pool.wait_ge(ea_in, settled(pool, reg, zeroed, k * 16 + 16))
                    pool.wait_ge(own, settled(pool, reg, zeroed, k * 4 + (t * 2 + 1)))
                    pool.tensor_copy(cur[:], g.first_s[:, bass.ds(t, 1)]).then_inc(own, 1)
                    pool.wait_ge(own, settled(pool, reg, zeroed, k * 4 + (t * 2 + 2)))
                    pool.tensor_copy(at_i[:], cur[:]).then_inc(own, 1)
                    pool.wait_ge(own, settled(pool, reg, zeroed, k * 4 + (t * 2 + 3)))
                    pool.indirect_dma_start(ids_next[:], None, edges, bass.IndirectOffsetOnAxis(at_i[:, 0:1], 0)).then_inc(ids_in, 16)
                    chunks = pool.value_load(g.loops[0:1, bass.ds(t, 1)], min_val=2, max_val=E)
                    with pool.Fori(0, chunks):
                        k = pool.snap(k_reg)
                        base = k * 4 + (t * 2 + 3)
                        pool.wait_ge(turned[1], settled(pool, reg, zeroed, k + 1))
                        pool.indirect_dma_start(ea[:].rearrange("p c k -> p (c k)"), None, g.ea6_d[:],
                                                bass.IndirectOffsetOnAxis(at_i[:, 0:1], 0)).then_inc(ea_in, 16)
                        pool.wait_ge(ids_in, settled(pool, reg, zeroed, k * 16 + (t * 16 + 32)))
                        for h in range(2):
                            pool.wait_ge(hs_in[h], settled(pool, reg, zeroed, k * (16 * HALF) + 16))
                            pool.tensor_copy(ids[h][:], ids_next[:, h * HALF:(h + 1) * HALF]).then_inc(own, 1)
                            pool.wait_ge(own, settled(pool, reg, zeroed, base + (h + 1 if h == 0 else 2)))
                            if h == 1:
                                pool.wait_ge(ea_in, settled(pool, reg, zeroed, k * 16 + 32))
                                pool.tensor_scalar(cur[:], cur[:], float(CHUNK), float(E), ALU.add, ALU.min).then_inc(own, 1)
                                pool.wait_ge(own, settled(pool, reg, zeroed, base + 3))
                                pool.tensor_copy(at_i[:], cur[:]).then_inc(own, 1)
                                pool.wait_ge(own, settled(pool, reg, zeroed, base + 4))
                                pool.indirect_dma_start(ids_next[:], None, edges,
                                                        bass.IndirectOffsetOnAxis(at_i[:, 0:1], 0)).then_inc(ids_in, 16)
                            pool.wait_ge(w_used[h], settled(pool, reg, zeroed, k * HALF + 1))
                            for r in range(HALF):
                                pool.indirect_dma_start(hs[h][:, r, :], None, g.h_d[:],
                                                        bass.IndirectOffsetOnAxis(ids[h][:, r:r + 1], 0)).then_inc(hs_in[h], 16)
                        pool.reg_add(k_reg, k_reg, 1)
                k = pool.snap(k_reg)
                pool.wait_ge(ids_in, settled(pool, reg, zeroed, k * 16 + (16 * TILES + 16)))
                pool.wait_ge(chain0, END_STEPS)
                for t in range(TILES):
                    n = min(P, N - t * P)
                    pool.indirect_dma_start(out[:], bass.IndirectOffsetOnAxis(g.node_i[0:n, t:t + 1], 0),
                                            ft[0:n, t + 1, :], None).then_inc(stored, 16)
                pool.wait_ge(stored, 16 * TILES)

            @block.tensor
            def _(pe):
                def turn(k, h):
                    if h == 0:
                        pe.wait_ge(ea_in, k * 16 + 32)
                        pe.wait_ge(ea_t_ready[1], k + 1)
                    else:
                        pe.wait_ge(ea_t_ready[0], k + 2)
                    for r in range(HALF):
                        mm = pe.transpose(t_ps[:, r, :], ea[:, h * HALF + r, :], g.eye_bf[:])
                    mm.then_inc(turned[h], 1)

                def weigh(k, h, ahead=True):
                    pe.wait_ge(ea_t_ready[h], k + 2)
                    for r in range(HALF):
                        if h == 1:
                            pe.wait_ge(w_used[0], k * HALF + (r + 2))
                        else:
                            pe.wait_ge(w_used[1], k * HALF - HALF + (r + 2) if ahead else 1)
                        pe.matmul(w_ps[r][:], ea_t[h][:, r, :], w6[:], start=True, stop=True).then_inc(w_done[h], 1)

                def add(k, h):
                    if h == 0:
                        pe.wait_ge(sum_added, k + 1)
                    pe.wait_ge(num_ready[h], k + 1)
                    for r in range(HALF):
                        mm = pe.matmul(sum_ps[:], g.const[:, C_EYE:C_EYE + P], e12(k, h, r),
                                       start=h == 0 and r == 0, stop=h == 1 and r == HALF - 1)
                    mm.then_inc(half_done[h], 1)

                pe.wait_ge(zeroed, 2)
                pe.matmul(sum_ps[:], zeros[:, 0:P], zeros[:], start=True, stop=True).then_inc(sums_done, 1)
                pe.wait_ge(w_ready_s, 1)
                turn(0, 0)
                turn(0, 1)
                weigh(0, 0, ahead=False)
                last = last_chunk(pe)
                weigh(0, 1)
                turn(1, 0)
                turn(1, 1)
                weigh(1, 0)
                with pe.Fori(1, last) as k:
                    add(k - 1, 0)
                    weigh(k, 1)
                    turn(k + 1, 0)
                    turn(k + 1, 1)
                    add(k - 1, 1)
                    weigh(k + 1, 0)
                add(last - 1, 0)
                weigh(last, 1)
                add(last - 1, 1)
                add(last, 0)
                add(last, 1)

            @block.scalar
            def _(act):
                def copy(k, h):
                    act.wait_ge(turned[h], k + 2)
                    act.wait_ge(w_done[h], k * HALF + 1)
                    act.activation(ea_t[h][:], t_ps[:], ACT.Copy).then_inc(ea_t_ready[h], 1)

                def exps(k):
                    act.wait_ge(shift_ready, k + 1)
                    act.activation(decay[:], shift[:], ACT.Exp).then_inc(decay_ready, 1)
                    for h in range(2):
                        act.wait_ge(sub_ready[h], k + 1)
                        for r in range(HALF):
                            e2 = e12(k, h, r)[:, C2:2 * C2]
                            act.activation(e2, e2, ACT.Exp, bias=off_exp[:, h * HALF + r:h * HALF + r + 1]).then_inc(exp_ready[h], 1)

                act.wait_ge(zeroed, 2)
                act.activation(warm[:], zeros[:, 0:1], ACT.Exp)
                copy(0, 0)
                copy(0, 1)
                last = last_chunk(act)
                with act.Fori(0, last) as k:
                    copy(k + 1, 0)
                    copy(k + 1, 1)
                    exps(k)
                exps(last)

            @block.vector
            def _(dve):
                free(dve, *w_used, *turned, *w_done, *half_done, *half_done, *ea_t_ready, decay_ready)
                c = Chain(dve, chain0)
                dve.wait_ge(w_in, 16 * 18)
                for i in range(3):
                    now = wf if i == 0 else wr
                    c.step(dve.tensor_copy(wp[i][:], now[:]))
                    if i < 2:
                        c.step(dve.tensor_tensor(wr[:], now[:], wp[i][:], ALU.subtract))
                c.step(dve.tensor_scalar(wf[:], wp[0][:], g.const[:, C_PART:C_PART + 1], None, ALU.mult))
                c.step(dve.scalar_tensor_tensor(out=wf[:], in0=wp[1][:], scalar=g.const[:, C_PART + 1:C_PART + 2], in1=wf[:],
                                                op0=ALU.mult, op1=ALU.add))
                c.step(dve.scalar_tensor_tensor(out=w6[:], in0=wp[2][:], scalar=g.const[:, C_PART + 2:C_PART + 3], in1=wf[:],
                                                op0=ALU.mult, op1=ALU.add))
                dve.engine_nop().then_inc(w_ready_s, 1)
                c.step(dve.memset(sums[:], 0.0))
                before = c.n

                def add_sums(c, k):
                    dve.wait_ge(sums_done, 1)
                    dve.wait_ge(half_done[1], k + 2)
                    c.publish(dve.tensor_tensor(sums[:], sums[:], sum_ps[:].rearrange("p (a c) -> p a c", a=2), ALU.add),
                              sum_added, k + 1)

                def finish(c, slot):
                    c.step(dve.tensor_scalar(ratio[:], sums[:, 1, :], 1e-30, None, ALU.max))
                    c.step(dve.reciprocal(ratio[:], ratio[:]))
                    c.step(dve.tensor_tensor(ratio[:], ratio[:], sums[:, 0, :], ALU.mult))
                    c.step(dve.tensor_reduce(ft[:, slot, :], ratio[:].rearrange("p (i j) -> p j i", i=D), AX.X, ALU.add))

                def weighted(k, h):
                    dve.wait_ge(exp_ready[h], k * HALF + HALF)
                    e1, e2 = e12(k, h)[:, :, 0:C2], e12(k, h)[:, :, C2:2 * C2]
                    dve.tensor_tensor(e1, e1, e2, ALU.mult).then_inc(num_ready[h], 1)

                def step(c, k, first, t):
                    if first:
                        c(dve.tensor_copy(left[:], g.deg_s[:, bass.ds(t, 1)]))
                        c(dve.memset(top_was[:], LOWEST))
                        c(dve.memset(top[:], LOWEST))
                        c(dve.memset(top_odd[:], LOWEST))
                    else:
                        c(dve.tensor_scalar(left[:], left[:], float(-CHUNK), None, ALU.add))
                        c(dve.tensor_copy(top_was[:], top[:]))
                    c.sync()
                    c.step(dve.tensor_scalar(over[:], g.const[:, C_IOTA:C_IOTA + CHUNK], left[:, 0:1], None, ALU.is_ge))
                    c(dve.tensor_scalar(off_max[:], over[:], OFF_MAX, None, ALU.mult))
                    c.step(dve.tensor_scalar(off_exp[:], over[:], OFF_EXP, None, ALU.mult))
                    for h in range(2):
                        dve.wait_ge(hs_in[h], k * (16 * HALF) + (16 * HALF + 16))
                        dve.wait_ge(half_done[h], k + 1)
                        for r in range(HALF):
                            dve.wait_ge(w_done[h], k * HALF + (r + 2))
                            dve.tensor_tensor(e12(k, h, r).rearrange("p (a i j) -> p a i j", a=2, i=D),
                                              w_ps[r][:].rearrange("p (a i j) -> p a i j", a=2, i=D),
                                              hs[h][:, r, :].unsqueeze(1).unsqueeze(3).broadcast_to([P, 2, D, D]),
                                              ALU.mult).then_inc(w_used[h], 1)
                        dve.wait_ge(w_used[h], k * HALF + (HALF + 1))
                        for r in range(HALF):
                            n = h * HALF + r
                            m = top if r % 2 == 0 else top_odd
                            if r >= 2 or h:
                                dve.wait_ge(c.sem, c.base + (c.n - 1))
                            c(dve.scalar_tensor_tensor(out=m[:], in0=e12(k, h, r)[:, C2:2 * C2], scalar=off_max[:, n:n + 1],
                                                       in1=m[:], op0=ALU.add, op1=ALU.max))
                    c.sync()
                    c.step(dve.tensor_tensor(top[:], top[:], top_odd[:], ALU.max))
                    dve.wait_ge(decay_ready, k + 1)
                    dve.tensor_tensor(shift[:], top_was[:], top[:], ALU.subtract).then_inc(shift_ready, 1)
                    for h in range(2):
                        e2 = e12(k, h)[:, :, C2:2 * C2]
                        dve.tensor_tensor(e2, e2, top[:].unsqueeze(1).broadcast_to([P, HALF, C2]), ALU.subtract).then_inc(sub_ready[h], 1)
                    add_sums(c, k)
                    weighted(k, 0)
                    if first:
                        finish(c, bass.ds(t, 1))
                        c.step(dve.memset(sums[:], 0.0))
                        dve.wait_ge(decay_ready, k + 2)
                    else:
                        dve.wait_ge(decay_ready, k + 2)
                        c.step(dve.tensor_tensor(sums[:], sums[:], decay[:].unsqueeze(1).broadcast_to([P, 2, C2]), ALU.mult))
                    weighted(k, 1)

                k_reg, later_reg = dve.alloc_register("att_dve_k"), dve.alloc_register("att_dve_later")
                dve.reg_mov(k_reg, 0)
                dve.reg_mov(later_reg, 0)
                with dve.Fori(0, TILES) as t:
                    k = dve.snap(k_reg)
                    cf = Chain(dve, chain_f, t * FIRST_STEPS)
                    step(cf, k, True, t)
                    assert cf.n == FIRST_STEPS, cf.n
                    dve.reg_add(k_reg, k_reg, 1)
                    chunks = dve.value_load(g.loops[0:1, bass.ds(t, 1)], min_val=2, max_val=E)
                    with dve.Fori(1, chunks):
                        k = dve.snap(k_reg)
                        cl = Chain(dve, chain_l, dve.snap(later_reg) * LATER_STEPS)
                        step(cl, k, False, t)
                        assert cl.n == LATER_STEPS, cl.n
                        dve.reg_add(k_reg, k_reg, 1)
                        dve.reg_add(later_reg, later_reg, 1)
                c = Chain(dve, chain0, before)
                add_sums(c, dve.snap(k_reg))
                finish(c, slice(TILES, TILES + 1))
                c.step(dve.tensor_tensor(ft[:, 1:, :], ft[:, 1:, :], g.x[:], ALU.add))
                assert before + c.n == END_STEPS, before + c.n


FIRST_STEPS = 4 + 3 + 9 + 4 + 1
LATER_STEPS = 2 + 3 + 9 + 1
END_STEPS = 5 + 3 + 1 + 4 + 1


class Shared:
    pass


def build(nc, ins, out, debug=None, stages=99):
    g = Shared()
    debug = debug or {}
    with ExitStack() as ctx:
        s = Scope(nc, ctx, "all")
        g.src_d = nc.dram_tensor("src_pad", (EP,), I32).ap()
        g.dst_d = nc.dram_tensor("dst_pad", (EP,), I32).ap()
        g.first_d = nc.dram_tensor("first_pad", (NP + 1,), F32).ap()
        g.ea6_d = nc.dram_tensor("ea_parts", (EA_ROWS, P), BF16).ap()
        g.key_d = nc.dram_tensor("rank_keys", (NP,), F32).ap()
        g.info_d = nc.dram_tensor("rank_info", (NP, 4), F32).ap()
        g.table_d = nc.dram_tensor("sheaf_table", (NP, OWN), F32).ap()
        g.h_d = nc.dram_tensor("h_table", (NP, D), F32).ap()
        g.const = s.sb("const", [P, C_END])
        g.eye_bf = s.sb("eye_bf", [P, P], BF16)
        g.iota_bf = s.sb("iota_bf", [P, P], BF16)
        g.x = s.sb("x", [P, TILES, D])
        g.h = s.sb("h", [P, TILES, D])
        g.first = s.sb("first", [P, TILES])
        g.deg = s.sb("deg", [P, TILES])
        g.first_s, g.deg_s = s.sb("first_s", [P, TILES]), s.sb("deg_s", [P, TILES])
        g.node_i = s.sb("node_i", [P, TILES], I32)
        g.rank_parts = s.sb("rank_parts", [P, TILES, 2])
        g.outs = s.sb("outs", [P, TILES])
        g.dinv2 = s.sb("dinv2", [P, TILES])
        g.mean, g.root_in = s.sb("mean", [P, TILES]), s.sb("root_in", [P, TILES])
        g.centred, g.squares = s.sb("centred", [P, TILES, D]), s.sb("squares", [P, TILES, D])
        g.loops = s.sb("loops", [1, TILES + 2], I32)
        stage_pad(nc, g, ins)
        stage_split(nc, g, ins)
        stage_offsets(nc, g)
        stage_order(nc, g)
        with nc.sbuf_tensor("A", [P, TILES, NP], BF16) as A:
            g.A = A
            stage_adjacency(nc, g)
            if "A" in debug:
                dump(nc, [(debug["A"], A[:, :, :])])
            stage_layers01(nc, g, ins)
        if "x1" in debug:
            dump(nc, [(debug["x1"], g.x[:]), (debug["outs"], g.outs[:]), (debug["deg"], g.deg[:])])
        stage_sheaf(nc, g, ins)
        if "x2" in debug:
            dump(nc, [(debug["x2"], g.x[:]), (debug["h2"], g.h[:])])
        stage_attention(nc, g, ins, out)


def dump(nc, pairs):
    with nc.semaphore() as sem, nc.Block() as block:
        @block.sync
        def _(sp):
            for o, i in pairs:
                sp.dma_start(o, i).then_inc(sem, 16)
            sp.wait_ge(sem, 16 * len(pairs))


_INS = ["x", "src", "dst", "edge_attr_16", "L0_gnn_W1_l", "L0_gnn_b1", "L0_gnn_W1_r", "L0_gnn_W2_l", "L0_gnn_b2",
        "L0_gnn_W2_r", "L1_gnn_W1", "L1_gnn_b1", "L1_gnn_W2", "L1_gnn_b2", "L1_gnn_W3", "L1_gnn_b3", "L1_gnn_Wl1",
        "L1_gnn_bl1", "L1_gnn_Wl2", "L1_gnn_bl2", "L1_gnn_Wl3", "L1_gnn_bl3", "L2_gnn_W1", "L2_gnn_b1", "L2_gnn_W2",
        "L2_gnn_b2", "L3_gnn_W_msg", "L3_gnn_b_msg", "L3_gnn_W_attn", "L3_gnn_b_attn"]


def kernel(**inputs):
    import concourse.bacc as bacc
    from concourse.bass_utils import run_bass_kernel_spmd

    nc = bacc.Bacc("TRN2", target_bir_lowering=False, num_devices=1)
    arrays = {name: np.ascontiguousarray(inputs[name]) for name in _INS}
    arrays["constants"] = constants()
    ins = {name: nc.dram_tensor(f"in_{name}", a.shape, mybir.dt.from_np(a.dtype), kind="ExternalInput").ap()
           for name, a in arrays.items()}
    out = nc.dram_tensor("out", (N, D), F32, kind="ExternalOutput").ap()
    build(nc, ins, out)
    result = run_bass_kernel_spmd(nc, [{f"in_{name}": a for name, a in arrays.items()}], core_ids=[0])
    return result.results[0]["out"]
```

```python
from contextlib import ExitStack

import numpy as np

import concourse.bass as bass
from concourse import mybir

F32 = mybir.dt.float32
BF16 = mybir.dt.bfloat16
I32 = mybir.dt.int32
ALU = mybir.AluOpType
ACT = mybir.ActivationFunctionType
AX = mybir.AxisListType

P = 128
N = 3125
E = 100000
D = 16
TILES = -(-N // P)
NP = TILES * P
LANE = 784
EP = P * LANE
PADID = NP - 1
BLOCKS = EP // P
WIN = 64
PAIRS = -(-TILES // 2)
NODES = 16
CHUNK = 8
HALF = CHUNK // 2
HID = 64
BATCH = 8
GROUPS = LANE // BATCH
EA_ROWS = E + CHUNK
LN_EPS = 1e-5
LOWEST = -3.0e38
OFF_MAX = -1.0e30
OFF_EXP = -2.0e38

C_EYE, C_IOTA, C_NODE, C_PART, C_END = 0, 128, 256, 256 + TILES, 256 + TILES + 3


def constants():
    c = np.zeros((P, C_END), np.float32)
    c[:, C_EYE:C_EYE + P] = np.eye(P)
    c[:, C_IOTA:C_IOTA + P] = np.arange(P)[None, :]
    c[:, C_NODE:C_NODE + TILES] = np.arange(TILES)[None, :] * P + np.arange(P)[:, None]
    part = [0] * 16 + [1] * 16 + [2] * 16 + [0] * 16 + [1] * 16 + [0] * 16 + [0, 1, 2]
    for row, which in enumerate(part):
        c[row, C_PART + which] = 1.0
    return c


class Chain:

    def __init__(self, eng, sem, base=0):
        self.eng, self.sem, self.base, self.n = eng, sem, base, 0

    def __call__(self, ins):
        ins.then_inc(self.sem, 1)
        self.n += 1

    def sync(self):
        self.eng.wait_ge(self.sem, self.base + self.n)

    def step(self, ins):
        self(ins)
        self.sync()

    def publish(self, ins, sem, value):
        ins.then_inc(sem, 1)
        self.eng.wait_ge(sem, value)


def settled(eng, reg, sem, value):
    eng.reg_mov(reg, value)
    value = eng.snap(reg)
    eng.wait_ge(sem, 1)
    return value


def free(eng, *sems):
    for sem in sems:
        eng.engine_nop().then_inc(sem, 1)


class Scope:

    def __init__(self, nc, ctx, tag):
        self.nc, self.ctx, self.tag = nc, ctx, tag

    def sb(self, name, shape, dt=F32):
        return self.ctx.enter_context(self.nc.sbuf_tensor(f"{self.tag}_{name}", shape, dt))

    def ps(self, name, shape, dt=F32):
        return self.ctx.enter_context(self.nc.psum_tensor(f"{self.tag}_{name}", shape, dt))

    def sem(self, name):
        return self.ctx.enter_context(self.nc.semaphore(f"{self.tag}_{name}"))


def spread(ap, shape):
    while len(ap.shape) < len(shape):
        ap = ap.unsqueeze(len(ap.shape))
    return ap.broadcast_to(shape)


def stage_pad(nc, g, ins):
    with ExitStack() as ctx:
        s = Scope(nc, ctx, "pad")
        pad_ids = s.sb("pad_ids", [32, (EP - E) // 32], I32)
        loaded, pad_set, stored = s.sem("loaded"), s.sem("pad_set"), s.sem("stored")
        with nc.Block() as block:
            @block.gpsimd
            def _(pool):
                pool.memset(pad_ids[:], PADID).then_inc(pad_set, 1)

            @block.sync
            def _(sp):
                sp.dma_start(g.const[:], ins["constants"]).then_inc(loaded, 16)
                sp.dma_start(g.x[:, 0:TILES - 1, :],
                             ins["x"][0:(TILES - 1) * P, :].rearrange("(t p) d -> p t d", p=P)).then_inc(loaded, 16)
                for real, padded in ((ins["src"], g.src_d), (ins["dst"], g.dst_d)):
                    sp.dma_start(padded[0:E].rearrange("(a b) -> a b", a=32),
                                 real.rearrange("(a b) -> a b", a=32)).then_inc(stored, 16)
                sp.wait_ge(pad_set, 1)
                for padded in (g.src_d, g.dst_d):
                    sp.dma_start(padded[E:EP].rearrange("(a b) -> a b", a=32), pad_ids[:]).then_inc(stored, 16)
                sp.wait_ge(stored, 64)
                sp.wait_ge(loaded, 32)
            x_zeroed, x_tail = s.sem("x_zeroed"), s.sem("x_tail")

            @block.vector
            def _(dve):
                dve.memset(g.x[:, TILES - 1, :], 0.0).then_inc(x_zeroed, 1)
                dve.wait_ge(loaded, 32)
                dve.tensor_copy(g.eye_bf[:], g.const[:, C_EYE:C_EYE + P]).then_inc(x_zeroed, 1)
                dve.tensor_copy(g.iota_bf[:], g.const[:, C_IOTA:C_IOTA + P]).then_inc(x_zeroed, 1)

            @block.scalar
            def _(act):
                act.wait_ge(x_zeroed, 1)
                rest = N - (TILES - 1) * P
                act.dma_start(g.x[0:rest, TILES - 1, :], ins["x"][(TILES - 1) * P:N, :]).then_inc(x_tail, 16)
                act.wait_ge(x_tail, 16)


def stage_offsets(nc, g):
    with ExitStack() as ctx:
        s = Scope(nc, ctx, "off")
        lasts_i = s.sb("lasts_i", [1, BLOCKS], I32)
        lasts = s.sb("lasts", [1, BLOCKS])
        ones = s.sb("ones", [1, P])
        lasts_bc = s.sb("lasts_bc", [P, BLOCKS])
        junk = s.sb("junk", [P, BLOCKS])
        below = s.sb("below", [P, TILES])
        block_at = s.sb("block_at", [P, TILES], I32)
        window_i = s.sb("window_i", [P, TILES, P], I32)
        window = s.sb("window", [P, TILES, P])
        inside = s.sb("inside", [P, TILES])
        last_row = s.sb("last_row", [1, 1])
        bc_ps = [s.ps(f"bc{b}", [P, 512]) for b in range(2)]
        lasts_in, dve_n, spread_done, windows_in, firsts_out, next_in = map(
            s.sem, ("lasts_in", "dve_n", "spread_done", "windows_in", "firsts_out", "next_in"))
        half = BLOCKS // 2

        with nc.Block() as block:
            @block.sync
            def _(sp):
                sp.dma_start(lasts_i[:], g.dst_d[:].rearrange("(b e) -> b e", e=P)[:, P - 1:P]
                             .rearrange("b e -> e b"), allow_slow_non_contiguous=True).then_inc(lasts_in, 16)
                sp.wait_ge(dve_n, SET + LASTS + COUNTED)
                sp.dma_start(g.first_d[0:NP].rearrange("(t p) -> p t", p=P), g.first[:],
                             allow_slow_non_contiguous=True).then_inc(firsts_out, 16)
                sp.dma_start(g.first_d[NP:NP + 1].rearrange("(a b) -> a b", a=1), last_row[:]).then_inc(firsts_out, 16)
                sp.wait_ge(firsts_out, 32)
                sp.dma_start(g.deg[:], g.first_d[1:NP + 1].rearrange("(t p) -> p t", p=P),
                             allow_slow_non_contiguous=True).then_inc(next_in, 16)
                sp.wait_ge(next_in, 16)

            @block.tensor
            def _(pe):
                pe.wait_ge(dve_n, SET + LASTS)
                for b in range(2):
                    pe.matmul(bc_ps[b][:, 0:half], ones[:], lasts[:, b * half:(b + 1) * half],
                              start=True, stop=True).then_inc(spread_done, 1)

            @block.gpsimd
            def _(pool):
                pool.wait_ge(dve_n, SET + LASTS + 2 + TILES + 1)
                for t in range(TILES):
                    pool.indirect_dma_start(window_i[:, t, :], None, g.dst_d[:].rearrange("(b e) -> b e", e=P),
                                            bass.IndirectOffsetOnAxis(block_at[:, t:t + 1], 0)).then_inc(windows_in, 16)
                pool.wait_ge(windows_in, 16 * TILES)

            @block.vector
            def _(dve):
                c = Chain(dve, dve_n)
                c(dve.memset(ones[:], 1.0))
                c(dve.memset(last_row[:], float(E)))
                dve.wait_ge(lasts_in, 16)
                c.step(dve.tensor_copy(lasts[:], lasts_i[:]))
                dve.wait_ge(spread_done, 2)
                for b in range(2):
                    c(dve.tensor_copy(lasts_bc[:, b * half:(b + 1) * half], bc_ps[b][:, 0:half]))
                c.sync()
                for t in range(TILES):
                    c.step(dve.tensor_scalar(junk[:], lasts_bc[:], g.const[:, C_NODE + t:C_NODE + t + 1], 0.0,
                                             ALU.is_lt, ALU.add, accum_out=below[:, t:t + 1]))
                c.step(dve.tensor_copy(block_at[:], below[:]))
                dve.wait_ge(windows_in, 16 * TILES)
                c.step(dve.tensor_copy(window[:], window_i[:]))
                for t in range(TILES):
                    c.step(dve.tensor_scalar(junk[:, 0:P], window[:, t, :], g.const[:, C_NODE + t:C_NODE + t + 1], 0.0,
                                             ALU.is_lt, ALU.add, accum_out=inside[:, t:t + 1]))
                c.step(dve.scalar_tensor_tensor(out=g.first[:], in0=below[:], scalar=float(P), in1=inside[:],
                                                op0=ALU.mult, op1=ALU.add))
                assert c.n == SET + LASTS + COUNTED
                dve.wait_ge(next_in, 16)
                c.step(dve.tensor_tensor(g.deg[:], g.deg[:], g.first[:], ALU.subtract))


SET, LASTS = 2, 1
COUNTED = 2 + TILES + 1 + 1 + TILES + 1


def stage_order(nc, g):
    with ExitStack() as ctx:
        s = Scope(nc, ctx, "ord")
        key = s.sb("key", [P, TILES])
        keys = s.sb("keys", [P, NP])
        junk = s.sb("junk", [P, NP], BF16)
        signs = s.sb("signs", [P, NP], BF16)
        minus_key = s.sb("minus_key", [P, TILES])
        minus_set, signs_done = s.sem("minus_set"), s.sem("signs_done")
        rank = s.sb("rank", [P, TILES])
        rank_i = s.sb("rank_i", [P, TILES], I32)
        part_i = s.sb("part_i", [P, 2, TILES], I32)
        info = s.sb("info", [P, TILES, 4])
        ranked = s.sb("ranked", [P, TILES, 4])
        most_t = s.sb("most_t", [TILES, 1])
        most_f = s.sb("most_f", [1, TILES])
        most_all = s.sb("most_all", [1, 2])
        counts = s.sb("counts", [1, TILES + 1], I32)
        deg_ps = s.ps("deg_ps", [TILES, P])
        row_ps = s.ps("row_ps", [1, TILES])
        dve_n, key_out, keys_in, info_out, ranked_in, pe_deg, key_set, rank_set, deg_set, most_set = map(
            s.sem, ("dve_n", "key_out", "keys_in", "info_out", "ranked_in", "pe_deg", "key_set", "rank_set",
                    "deg_set", "most_set"))

        with nc.Block() as block:
            @block.sync
            def _(sp):
                sp.wait_ge(key_set, 1)
                sp.dma_start(g.key_d[:].rearrange("(t p) -> p t", p=P), key[:],
                             allow_slow_non_contiguous=True).then_inc(key_out, 16)
                sp.wait_ge(key_out, 16)
                sp.dma_start(keys[:], g.key_d[:].unsqueeze(0).broadcast_to([P, NP])).then_inc(keys_in, 16)
                sp.wait_ge(info_out, 16 * TILES)
                sp.dma_start(ranked[:], g.info_d[:].rearrange("(t p) c -> p t c", p=P)).then_inc(ranked_in, 16)
                sp.wait_ge(ranked_in, 16)

            @block.gpsimd
            def _(pool):
                pool.wait_ge(rank_set, 1)
                for t in range(TILES):
                    pool.indirect_dma_start(g.info_d[:], bass.IndirectOffsetOnAxis(rank_i[:, t:t + 1], 0),
                                            info[:, t, :], None).then_inc(info_out, 16)
                pool.wait_ge(info_out, 16 * TILES)

            @block.tensor
            def _(pe):
                pe.wait_ge(deg_set, 1)
                pe.transpose(deg_ps[:], g.deg_s[:], g.const[:, C_EYE:C_EYE + P]).then_inc(pe_deg, 1)
                pe.wait_ge(most_set, 1)
                pe.transpose(row_ps[:], most_t[:], g.const[0:TILES, C_EYE:C_EYE + TILES]).then_inc(pe_deg, 1)

            @block.scalar
            def _(act):
                act.wait_ge(minus_set, 1)
                act.wait_ge(keys_in, 16)
                for t in range(ACT_FROM, TILES):
                    if t > ACT_FROM:
                        act.wait_ge(signs_done, t - ACT_FROM)
                    act.activation(signs[:], keys[:], ACT.Sign, bias=minus_key[:, t:t + 1],
                                   accum_out=rank[:, t:t + 1]).then_inc(signs_done, 1)

            @block.vector
            def _(dve):
                c = Chain(dve, dve_n)
                c.step(dve.tensor_scalar(key[:], g.deg[:], float(KEY_MAX), float(KEY_STEP), ALU.min, ALU.mult))
                c.publish(dve.tensor_tensor(key[:], key[:], g.const[:, C_NODE:C_NODE + TILES], ALU.subtract), key_set, 1)
                dve.tensor_scalar(minus_key[:], key[:], -1.0, None, ALU.mult).then_inc(minus_set, 1)
                c(dve.memset(info[:], 0.0))
                c.sync()
                c(dve.tensor_copy(info[:, :, 0], g.const[:, C_NODE:C_NODE + TILES]))
                c(dve.tensor_copy(info[:, :, 1], g.first[:]))
                c(dve.tensor_copy(info[:, :, 2], g.deg[:]))
                dve.wait_ge(keys_in, 16)
                for t in range(0, ACT_FROM):
                    c.step(dve.tensor_scalar(junk[:], keys[:], key[:, t:t + 1], 0.0, ALU.is_gt, ALU.add,
                                             accum_out=rank[:, t:t + 1]))
                dve.wait_ge(signs_done, TILES - ACT_FROM)
                c.step(dve.tensor_scalar(rank[:, ACT_FROM:TILES], rank[:, ACT_FROM:TILES], float(NP - 1), 0.5, ALU.add, ALU.mult))
                c.publish(dve.tensor_copy(rank_i[:], rank[:]), rank_set, 1)
                c(dve.tensor_scalar(part_i[:, 0, :], rank_i[:], P - 1, None, ALU.bitwise_and))
                c(dve.tensor_scalar(part_i[:, 1, :], rank_i[:], P.bit_length() - 1, None, ALU.arith_shift_right))
                c.sync()
                c.step(dve.tensor_copy(g.rank_parts[:], part_i[:].rearrange("p a t -> p t a")))
                dve.wait_ge(ranked_in, 16)
                c(dve.tensor_copy(g.node_i[:], ranked[:, :, 0]))
                c(dve.tensor_copy(g.first_s[:], ranked[:, :, 1]))
                c.publish(dve.tensor_copy(g.deg_s[:], ranked[:, :, 2]), deg_set, 1)
                dve.wait_ge(pe_deg, 1)
                c.publish(dve.tensor_reduce(most_t[:], deg_ps[:], AX.X, ALU.max), most_set, 1)
                dve.wait_ge(pe_deg, 2)
                c.step(dve.tensor_copy(most_f[:], row_ps[:]))
                c.step(dve.tensor_reduce(most_all[:, 0:1], most_f[:], AX.X, ALU.max))
                c.step(dve.tensor_scalar(most_f[:], most_f[:], float(CHUNK + 1), float(CHUNK - 1), ALU.max, ALU.add))
                c.step(dve.tensor_scalar(most_all[:, 1:2], most_all[:, 0:1], 1.0, float(WIN - 1), ALU.max, ALU.add))
                c.step(dve.tensor_copy(counts[:, 0:TILES], most_f[:]))
                c.step(dve.tensor_copy(counts[:, TILES:TILES + 1], most_all[:, 1:2]))
                c.step(dve.tensor_scalar(g.loops[:, 0:TILES], counts[:, 0:TILES], CHUNK.bit_length() - 1, None,
                                         ALU.arith_shift_right))
                c.step(dve.tensor_scalar(g.loops[:, TILES:TILES + 1], counts[:, TILES:TILES + 1],
                                         WIN.bit_length() - 1, None, ALU.arith_shift_right))
                c.step(dve.tensor_copy(most_f[:], g.loops[:, 0:TILES]))
                c.step(dve.tensor_reduce(most_all[:, 0:1], most_f[:], AX.X, ALU.add))
                c.step(dve.tensor_scalar(most_all[:, 0:1], most_all[:, 0:1], -1.0, None, ALU.add))
                c.step(dve.tensor_copy(g.loops[:, TILES + 1:TILES + 2], most_all[:, 0:1]))


KEY_MAX, KEY_STEP = 4095, 4096
ACT_FROM = TILES // 2


def stage_adjacency(nc, g, ins):
    with ExitStack() as ctx:
        s = Scope(nc, ctx, "adj")
        at = s.sb("at", [P, TILES])
        at_i = s.sb("at_i", [P, TILES], I32)
        left = s.sb("left", [P, 2 * PAIRS])
        ids = s.sb("ids", [P, 2 * PAIRS, WIN], I32)
        ids2 = s.sb("ids2", [P, 2 * PAIRS, WIN], I32)
        outside = s.sb("outside", [P, 2 * PAIRS, WIN], BF16)
        lo_rows = s.sb("lo_rows", [P, 2 * PAIRS, WIN], BF16)
        hi_rows = s.sb("hi_rows", [P, 2 * PAIRS, WIN], BF16)
        lo_t = s.sb("lo_t", [P, PAIRS * P], BF16)
        hi_t = s.sb("hi_t", [P, PAIRS * P], BF16)
        hot_lo = [s.sb(f"hot_lo{b}", [P, NODES, P], BF16) for b in range(2)]
        hot_hi = [s.sb(f"hot_hi{b}", [P, NODES, TILES], BF16) for b in range(2)]
        ps = [[s.ps(f"ps{b}{h}", [P, NODES * TILES]) for h in range(2)] for b in range(2)]
        ps_t = s.ps("ps_t", [P, 2, P], BF16)
        turns = P // NODES // 2

        prepared, windows_in, rows_ready, turned, copied, hot_lo_n = map(
            s.sem, ("prepared", "windows_in", "rows_ready", "turned", "copied", "hot_lo_n"))
        hot_ready = [s.sem(f"hot_ready{b}") for b in range(2)]
        column_ready = [s.sem(f"column_ready{b}") for b in range(2)]
        moved = [[s.sem(f"moved{b}{h}") for h in range(2)] for b in range(2)]

        def each_group(eng, body):
            with eng.Fori(0, TILES // 2) as q:
                with eng.Fori(0, turns) as j:
                    for b in range(2):
                        body(b, (0, 1), q * turns + j, q, j)
            q = TILES // 2
            with eng.Fori(0, turns) as j:
                for b in range(2):
                    body(b, (0,), j + q * turns, q, j)

        ea_zeros, zeros_set, ea_out = s.sb("ea_zeros", [CHUNK, D]), s.sem("zeros_set"), s.sem("ea_out")

        with nc.Block() as block:
            @block.sync
            def _(sp):
                sp.dma_start(g.ea_d[0:E, :].rearrange("(a b) d -> a (b d)", a=32),
                             ins["edge_attr_16"].rearrange("(a b) d -> a (b d)", a=32)).then_inc(ea_out, 16)
                sp.wait_ge(zeros_set, 1)
                sp.dma_start(g.ea_d[E:EA_ROWS, :], ea_zeros[:]).then_inc(ea_out, 16)
                sp.wait_ge(ea_out, 32)

            @block.gpsimd
            def _(pool):
                pool.memset(ea_zeros[:], 0.0).then_inc(zeros_set, 1)
                pool.wait_ge(prepared, 3)
                for t in range(TILES):
                    pool.indirect_dma_start(ids[:, t, :], None, g.src_d[:].rearrange("(e o) -> e o", o=1),
                                            bass.IndirectOffsetOnAxis(at_i[:, t:t + 1], 0)).then_inc(windows_in, 16)
                pool.wait_ge(windows_in, 16 * TILES)

            @block.vector
            def _(dve):
                free(dve, *column_ready, *moved[0], *moved[1])
                c = Chain(dve, prepared)
                c(dve.memset(left[:], 0.0))
                c(dve.tensor_copy(at[:], g.first[:]))
                c.sync()
                c.step(dve.tensor_copy(at_i[:], at[:]))
                c(dve.tensor_copy(left[:, 0:TILES], g.deg[:]))
                c(dve.memset(ids[:, TILES:2 * PAIRS, :], 0))
                c.sync()
                c.step(dve.tensor_tensor(outside[:], g.const[:, C_IOTA:C_IOTA + WIN].unsqueeze(1)
                                         .broadcast_to([P, 2 * PAIRS, WIN]),
                                         spread(left[:], [P, 2 * PAIRS, WIN]), ALU.is_ge))
                dve.wait_ge(windows_in, 16 * TILES)
                c.step(dve.tensor_scalar(ids2[:], ids[:], P - 1, None, ALU.bitwise_and))
                c.step(dve.tensor_copy(lo_rows[:], ids2[:]))
                c.step(dve.tensor_scalar(ids2[:], ids[:], P.bit_length() - 1, None, ALU.arith_shift_right))
                dve.scalar_tensor_tensor(out=hi_rows[:], in0=outside[:], scalar=100.0, in1=ids2[:],
                                         op0=ALU.mult, op1=ALU.add).then_inc(rows_ready, 1)
                for q in range(PAIRS):
                    dve.wait_ge(turned, q + 1)
                    dve.tensor_copy(lo_t[:, q * P:(q + 1) * P], ps_t[:, 0, :]).then_inc(copied, 1)
                    dve.tensor_copy(hi_t[:, q * P:(q + 1) * P], ps_t[:, 1, :]).then_inc(copied, 1)
                dve.wait_ge(copied, 2 * PAIRS)

                def hot(b, halves, i, q, j):
                    dve.wait_ge(column_ready[b], i + 1)
                    col = q * P + j * (2 * NODES) + b * NODES
                    for n in range(NODES):
                        dve.tensor_scalar(hot_lo[b][:, n, :], g.iota_bf[:], lo_t[:, bass.ds(col + n, 1)], None, ALU.is_equal)
                    dve.tensor_tensor(hot_hi[b][:], spread(hi_t[:, bass.ds(col, NODES)], [P, NODES, TILES]),
                                      g.iota_bf[:, 0:TILES].unsqueeze(1).broadcast_to([P, NODES, TILES]),
                                      ALU.is_equal).then_inc(hot_ready[b], 1)

                each_group(dve, hot)

            @block.tensor
            def _(pe):
                pe.wait_ge(rows_ready, 1)
                for q in range(PAIRS):
                    if q:
                        pe.wait_ge(copied, 2 * q)
                    pe.transpose(ps_t[:, 0, :], lo_rows[:, 2 * q:2 * q + 2, :].rearrange("p t w -> p (t w)"), g.eye_bf[:])
                    pe.transpose(ps_t[:, 1, :], hi_rows[:, 2 * q:2 * q + 2, :].rearrange("p t w -> p (t w)"),
                                 g.eye_bf[:]).then_inc(turned, 1)

                def products(b, halves, i, q, j):
                    pe.wait_ge(hot_ready[b], i + 1)
                    for h in halves:
                        pe.wait_ge(moved[b][h], i + 1)
                    for n in range(NODES):
                        for h in halves:
                            mm = pe.matmul(ps[b][h][:, n * TILES:(n + 1) * TILES],
                                           hot_lo[b][h * WIN:(h + 1) * WIN, n, :],
                                           hot_hi[b][h * WIN:(h + 1) * WIN, n, :], start=True, stop=True)
                    mm.then_inc(column_ready[b], 1)

                each_group(pe, products)

            @block.scalar
            def _(act):
                def move(b, halves, i, q, j):
                    act.wait_ge(column_ready[b], i + 2)
                    for h in halves:
                        node = q * (2 * P) + j * (2 * NODES) + (b * NODES + h * P)
                        act.activation(g.A[:, :, bass.ds(node, NODES)],
                                       ps[b][h][:].rearrange("p (n s) -> p s n", n=NODES), ACT.Copy).then_inc(moved[b][h], 1)

                each_group(act, move)


def stage_more_windows(nc, g):
    with ExitStack() as ctx:
        s = Scope(nc, ctx, "more")
        at = s.sb("at", [P, TILES])
        at_i = s.sb("at_i", [P, TILES], I32)
        left = s.sb("left", [P, 2 * PAIRS])
        ids = s.sb("ids", [P, 2 * PAIRS, WIN], I32)
        ids2 = s.sb("ids2", [P, 2 * PAIRS, WIN], I32)
        outside = s.sb("outside", [P, 2 * PAIRS, WIN], BF16)
        lo_rows = s.sb("lo_rows", [P, 2 * PAIRS, WIN], BF16)
        hi_rows = s.sb("hi_rows", [P, 2 * PAIRS, WIN], BF16)
        lo_t = s.sb("lo_t", [P, PAIRS * P], BF16)
        hi_t = s.sb("hi_t", [P, PAIRS * P], BF16)
        hot_lo = s.sb("hot_lo", [P, NODES, P], BF16)
        hot_hi = s.sb("hot_hi", [P, NODES, TILES], BF16)
        ps = [s.ps(f"ps{h}", [P, NODES * TILES]) for h in range(2)]
        ps_t = s.ps("ps_t", [P, 2, P], BF16)
        set_up, chain, windows_in, at_ready, rows_ready, turned, copied, hot_ready, column_ready, added = map(
            s.sem, ("set_up", "chain", "windows_in", "at_ready", "rows_ready", "turned", "copied", "hot_ready",
                    "column_ready", "added"))
        turns = P // NODES
        groups = PAIRS * turns

        def rounds(eng):
            return eng.value_load(g.loops[0:1, TILES:TILES + 1], min_val=1, max_val=-(-E // WIN))

        def each_group(eng, n, body):
            with eng.Fori(0, TILES // 2) as q:
                with eng.Fori(0, turns) as j:
                    body((0, 1), n * groups + q * turns + j, q, j)
            q = TILES // 2
            with eng.Fori(0, turns) as j:
                body((0,), n * groups + j + q * turns, q, j)

        with nc.Block() as block:
            @block.gpsimd
            def _(pool):
                reg = pool.alloc_register("more_pool_value")
                pool.reg_mov(reg, 0)
                pool.memset(at_i[:], 0).then_inc(set_up, 1)
                pool.memset(ids[:], 0).then_inc(set_up, 1)
                pool.wait_ge(set_up, 2)
                count = rounds(pool)
                with pool.If(count - 1), pool.Fori(1, count) as r:
                    pool.wait_ge(at_ready, settled(pool, reg, set_up, r + 0))
                    for t in range(TILES):
                        pool.indirect_dma_start(ids[:, t, :], None, g.src_d[:].rearrange("(e o) -> e o", o=1),
                                                bass.IndirectOffsetOnAxis(at_i[:, t:t + 1], 0)).then_inc(windows_in, 16)
                    pool.wait_ge(windows_in, r * (16 * TILES))

            @block.tensor
            def _(pe):
                count = rounds(pe)
                with pe.If(count - 1), pe.Fori(1, count) as r:
                    pe.wait_ge(rows_ready, r + 0)
                    for q in range(PAIRS):
                        if q:
                            pe.wait_ge(copied, (r - 1) * (2 * PAIRS) + 2 * q)
                        pe.transpose(ps_t[:, 0, :], lo_rows[:, 2 * q:2 * q + 2, :].rearrange("p t w -> p (t w)"), g.eye_bf[:])
                        pe.transpose(ps_t[:, 1, :], hi_rows[:, 2 * q:2 * q + 2, :].rearrange("p t w -> p (t w)"),
                                     g.eye_bf[:]).then_inc(turned, 1)

                    def products(halves, i, q, j):
                        pe.wait_ge(hot_ready, i + 1)
                        for n in range(NODES):
                            for h in halves:
                                mm = pe.matmul(ps[h][:, n * TILES:(n + 1) * TILES],
                                               hot_lo[h * WIN:(h + 1) * WIN, n, :],
                                               hot_hi[h * WIN:(h + 1) * WIN, n, :], start=True, stop=True)
                        mm.then_inc(column_ready, 1)

                    each_group(pe, r - 1, products)

            @block.vector
            def _(dve):
                free(dve, added, added)
                dve.wait_ge(set_up, 2)
                c = Chain(dve, chain)
                c(dve.memset(left[:], 0.0))
                c(dve.tensor_copy(at[:], g.first[:]))
                c.sync()
                c.step(dve.tensor_scalar(left[:, 0:TILES], g.deg[:], float(-WIN), None, ALU.add))
                before = c.n
                count = rounds(dve)
                with dve.If(count - 1), dve.Fori(1, count) as r:
                    c = Chain(dve, chain, (r - 1) * MORE_STEPS + before)
                    c.step(dve.tensor_scalar(at[:], at[:], float(WIN), float(E), ALU.add, ALU.min))
                    c.publish(dve.tensor_copy(at_i[:], at[:]), at_ready, r + 0)
                    c.step(dve.tensor_tensor(outside[:], g.const[:, C_IOTA:C_IOTA + WIN].unsqueeze(1)
                                             .broadcast_to([P, 2 * PAIRS, WIN]),
                                             spread(left[:], [P, 2 * PAIRS, WIN]), ALU.is_ge))
                    dve.wait_ge(windows_in, r * (16 * TILES))
                    c.step(dve.tensor_scalar(ids2[:], ids[:], P - 1, None, ALU.bitwise_and))
                    c.step(dve.tensor_copy(lo_rows[:], ids2[:]))
                    c.step(dve.tensor_scalar(ids2[:], ids[:], P.bit_length() - 1, None, ALU.arith_shift_right))
                    c.publish(dve.scalar_tensor_tensor(out=hi_rows[:], in0=outside[:], scalar=100.0, in1=ids2[:],
                                                       op0=ALU.mult, op1=ALU.add), rows_ready, r + 0)
                    for q in range(PAIRS):
                        dve.wait_ge(turned, (r - 1) * PAIRS + (q + 1))
                        dve.tensor_copy(lo_t[:, q * P:(q + 1) * P], ps_t[:, 0, :]).then_inc(copied, 1)
                        dve.tensor_copy(hi_t[:, q * P:(q + 1) * P], ps_t[:, 1, :]).then_inc(copied, 1)
                    dve.wait_ge(copied, r * (2 * PAIRS))
                    c(dve.tensor_scalar(left[:], left[:], float(-WIN), None, ALU.add))

                    def group(halves, i, q, j):
                        col = q * P + j * NODES
                        dve.wait_ge(added, i * 2 + 2)
                        for n in range(NODES):
                            dve.tensor_scalar(hot_lo[:, n, :], g.iota_bf[:], lo_t[:, bass.ds(col + n, 1)], None, ALU.is_equal)
                        dve.tensor_tensor(hot_hi[:], spread(hi_t[:, bass.ds(col, NODES)], [P, NODES, TILES]),
                                          g.iota_bf[:, 0:TILES].unsqueeze(1).broadcast_to([P, NODES, TILES]),
                                          ALU.is_equal).then_inc(hot_ready, 1)
                        dve.wait_ge(column_ready, i + 1)
                        for h in range(2):
                            if h in halves:
                                column = g.A[:, :, bass.ds(q * (2 * P) + j * NODES + h * P, NODES)]
                                dve.tensor_tensor(column, column, ps[h][:].rearrange("p (n s) -> p s n", n=NODES),
                                                  ALU.add).then_inc(added, 1)
                            else:
                                dve.engine_nop().then_inc(added, 1)

                    each_group(dve, r - 1, group)
                    assert c.n == MORE_STEPS, c.n


MORE_STEPS = 2 + 1 + 3


def norm(dve, c, g, out, x, root_asked, root_done, asked):
    shape = [P, TILES, D]
    c.step(dve.tensor_reduce(g.mean[:], x, AX.X, ALU.add))
    c.step(dve.tensor_scalar(g.mean[:], g.mean[:], 1.0 / D, None, ALU.mult))
    c.step(dve.tensor_tensor(g.centred[:], x, spread(g.mean[:], shape), ALU.subtract))
    c.step(dve.tensor_tensor(g.squares[:], g.centred[:], g.centred[:], ALU.mult))
    c.step(dve.tensor_reduce(g.mean[:], g.squares[:], AX.X, ALU.add))
    c.step(dve.tensor_scalar(g.root_in[:], g.mean[:], 1.0 / D, LN_EPS, ALU.mult, ALU.add))
    asked[0] += 1
    dve.engine_nop().then_inc(root_asked, 1)
    dve.wait_ge(root_done, asked[0])
    c.step(dve.reciprocal(g.mean[:], g.root_in[:]))
    c.step(dve.tensor_tensor(out, g.centred[:], spread(g.mean[:], shape), ALU.mult))
    c.step(dve.tensor_scalar(out, out, 0.0, None, ALU.max))


class NodeOps:

    def __init__(self, dve, chain):
        self.dve, self.c = dve, chain

    def tt(self, out, a, b, op):
        self.c.step(self.dve.tensor_tensor(out, a, b, op))

    def ts(self, out, a, s1, s2, op0, op1=None):
        self.c.step(self.dve.tensor_scalar(out, a, s1, s2, op0, op1) if op1 is not None
                    else self.dve.tensor_scalar(out, a, s1, None, op0))

    def reduce(self, out, a, op=ALU.add):
        self.c.step(self.dve.tensor_reduce(out, a, AX.X, op))


DENSE_TILES = 4
DENSE_STEPS = -(-TILES // DENSE_TILES)


def stage_layers01(nc, g, ins, debug=None):
    with ExitStack() as ctx:
        s = Scope(nc, ctx, "n01")
        dims = [(2 * D, 32), (64, D), (D, 32), (32, 64), (64, P), (P, 64), (64, 32), (32, D)]
        names = ["L0_gnn_b1", "L0_gnn_b2", "L1_gnn_b1", "L1_gnn_b2", "L1_gnn_b3", "L1_gnn_bl1", "L1_gnn_bl2", "L1_gnn_bl3"]
        weights = [[("L0_gnn_W1_l", 0, D), ("L0_gnn_W1_r", D, 2 * D)], [("L0_gnn_W2_l", 0, 32), ("L0_gnn_W2_r", 32, 64)],
                   [("L1_gnn_W1", 0, D)], [("L1_gnn_W2", 0, 32)], [("L1_gnn_W3", 0, 64)],
                   [("L1_gnn_Wl1", 0, P)], [("L1_gnn_Wl2", 0, 64)], [("L1_gnn_Wl3", 0, 32)]]
        widths = [D, 32, D, 32, 64]
        W = [s.sb(f"W{d}", [k, o]) for d, (k, o) in enumerate(dims)]
        bias = [s.sb(f"bias{d}", [P, o]) for d, (k, o) in enumerate(dims)]
        feat = s.sb("feat", [P, TILES, P])
        cat = s.sb("cat", [P, TILES, 64])
        rest = summed = feat[:, :, 64:P]
        parts = s.sb("parts", [P, TILES, 3, 64], BF16)
        inv_deg = s.sb("inv_deg", [P, TILES])
        dinv = s.sb("dinv", [P, TILES])
        junk = s.sb("junk", [P, NP], BF16)
        turned_sb = [s.sb(f"turned_sb{b}", [P, DENSE_TILES * P]) for b in range(2)]
        agg_ps = [s.ps(f"agg_ps{b}", [P, 512]) for b in range(2)]
        turn_ps = [s.ps(f"turn_ps{b}", [P, 512]) for b in range(2)]
        out_ps = [s.ps(f"out_ps{b}", [P, 512]) for b in range(2)]
        weights_in, dve_n, parts_ready, input_ready, turned, copied, dense_done, added = map(
            s.sem, ("weights_in", "dve_n", "parts_ready", "input_ready", "turned", "copied", "dense_done", "added"))
        agg_done = [s.sem(f"agg_done{b}") for b in range(2)]
        agg_read = [s.sem(f"agg_read{b}") for b in range(2)]
        out_done, root_asked, root_done = s.sem("out_done"), s.sem("root_asked"), s.sem("root_done")
        even, odd = (TILES + 1) // 2, TILES // 2

        def parts_view(a):
            w = widths[a]
            return parts[:].rearrange("p t s f -> p (t s f)")[:, 0:TILES * 3 * w].rearrange("p (t k) -> p t k", t=TILES)

        def tiles_of(step):
            return range(step * DENSE_TILES, min(TILES, (step + 1) * DENSE_TILES))

        with nc.Block() as block:
            @block.sync
            def _(sp):
                n = 0
                for d, rows in enumerate(weights):
                    for name, a, b in rows:
                        sp.dma_start(W[d][a:b, :], ins[name]).then_inc(weights_in, 16)
                        n += 1
                for d, name in enumerate(names):
                    o = dims[d][1]
                    sp.dma_start(bias[d][:], ins[name].unsqueeze(0).broadcast_to([P, o])).then_inc(weights_in, 16)
                    n += 1
                sp.wait_ge(weights_in, 16 * n)
                assert n == LOADS

            @block.tensor
            def _(pe):
                pe.wait_ge(weights_in, 16 * LOADS)

                def aggregate(a):
                    w = widths[a]
                    pe.wait_ge(parts_ready, a + 1)

                    def tile(b, i, t):
                        pe.wait_ge(agg_read[b], i + 1)
                        for shi in range(TILES):
                            mm = pe.matmul(agg_ps[b][:, 0:3 * w], g.A[:, shi, t * P:(t + 1) * P],
                                           parts_view(a)[:, shi, :], start=shi == 0, stop=shi == TILES - 1)
                        mm.then_inc(agg_done[b], 1)

                    for t in range(TILES):
                        tile(t % 2, t // 2 + a * (even if t % 2 == 0 else odd), t)

                def dense(d):
                    k, o = dims[d]
                    source = cat if d < 5 else feat
                    for step in range(DENSE_STEPS):
                        n = d * DENSE_STEPS + step
                        b = n % 2
                        tiles = tiles_of(step)
                        if step == 0:
                            pe.wait_ge(input_ready, d + 1)
                        if n >= 2:
                            pe.wait_ge(copied, n - 1)
                        for t in tiles:
                            mm = pe.transpose(turn_ps[b][0:k, (t - tiles[0]) * P:(t - tiles[0] + 1) * P],
                                              source[:, t, 0:k], g.const[:, C_EYE:C_EYE + P])
                        mm.then_inc(turned, 1)
                        if step:
                            products(d, step - 1)
                    products(d, DENSE_STEPS - 1)

                def products(d, step):
                    k, o = dims[d]
                    n = d * DENSE_STEPS + step
                    b = n % 2
                    tiles = tiles_of(step)
                    pe.wait_ge(copied, n + 1)
                    if n >= 2:
                        pe.wait_ge(added, n - 1)
                    for t in tiles:
                        at = t - tiles[0]
                        mm = pe.matmul(out_ps[b][:, at * o:(at + 1) * o], turned_sb[b][0:k, at * P:(at + 1) * P],
                                       W[d][:], start=True, stop=True)
                    mm.then_inc(dense_done, 1)

                for d in range(len(dims)):
                    if d < 5:
                        aggregate(d)
                    dense(d)

            @block.scalar
            def _(act):
                def outs(d):
                    for shi in range(5 * d, 5 * d + 5):
                        if shi:
                            act.wait_ge(out_done, shi)
                        act.activation(junk[:], g.A[:, shi, :], ACT.Copy,
                                       accum_out=g.outs[:, shi:shi + 1]).then_inc(out_done, 1)

                def roots(n):
                    act.wait_ge(root_asked, n)
                    act.activation(g.root_in[:], g.root_in[:], ACT.Sqrt).then_inc(root_done, 1)

                def copies(d):
                    k = dims[d][0]
                    for step in range(DENSE_STEPS):
                        n = d * DENSE_STEPS + step
                        b, tiles = n % 2, tiles_of(step)
                        act.wait_ge(turned, n + 1)
                        if n >= 2:
                            act.wait_ge(dense_done, n - 1)
                        act.activation(turned_sb[b][0:k, 0:len(tiles) * P], turn_ps[b][0:k, 0:len(tiles) * P],
                                       ACT.Copy).then_inc(copied, 1)

                roots(1)
                for d in range(8):
                    if d == 2:
                        roots(2)
                        roots(3)
                    if d < 5:
                        outs(d)
                    copies(d)
                roots(4)
                roots(5)

            @block.vector
            def _(dve):
                c = Chain(dve, dve_n)
                ops = NodeOps(dve, c)
                asked = [0]
                free(dve, *agg_read)

                def norm_relu(out, x):
                    norm(dve, c, g, out, x, root_asked, root_done, asked)

                def aggregate(a, source):
                    w = widths[a]
                    p3 = parts_view(a)
                    for part in range(3):
                        now = p3[:, :, part * w:(part + 1) * w]
                        cur = source if part == 0 else rest[:, :, 0:w]
                        ins_ = dve.tensor_copy(now, cur)
                        if part == 2:
                            ins_.then_inc(parts_ready, 1)
                        else:
                            c.step(ins_)
                            ops.tt(rest[:, :, 0:w], cur, now, ALU.subtract)

                    def tile(b, i, t):
                        dve.wait_ge(agg_done[b], i + 1)
                        dve.tensor_reduce(summed[:, bass.ds(t, 1), 0:w],
                                          agg_ps[b][:, 0:3 * w].rearrange("p (s f) -> p f s", f=w), AX.X,
                                          ALU.add).then_inc(agg_read[b], 1)

                    with dve.Fori(0, TILES // 2) as i:
                        for b in range(2):
                            tile(b, i + a * (even if b == 0 else odd), i * 2 + b)
                    tile(0, TILES // 2 + a * even, TILES - 1)
                    dve.wait_ge(agg_read[0], (a + 1) * even + 1)
                    dve.wait_ge(agg_read[1], (a + 1) * odd + 1)

                def dense(d, relu):
                    k, o = dims[d]
                    dve.engine_nop().then_inc(input_ready, 1)
                    for step in range(DENSE_STEPS):
                        n = d * DENSE_STEPS + step
                        b, tiles = n % 2, tiles_of(step)
                        dve.wait_ge(dense_done, n + 1)
                        m = len(tiles)
                        dve.tensor_tensor(feat[:, tiles[0]:tiles[0] + m, 0:o],
                                          out_ps[b][:, 0:m * o].rearrange("p (t o) -> p t o", o=o),
                                          bias[d][:].unsqueeze(1).broadcast_to([P, m, o]), ALU.add).then_inc(added, 1)
                    dve.wait_ge(added, (d + 1) * DENSE_STEPS)
                    if relu:
                        ops.ts(feat[:, :, 0:o], feat[:, :, 0:o], 0.0, None, ALU.max)

                dve.wait_ge(weights_in, 16 * LOADS)
                norm_relu(g.h[:], g.x[:])
                ops.ts(inv_deg[:], g.deg[:], 1.0, None, ALU.max)
                c.step(dve.reciprocal(inv_deg[:], inv_deg[:]))
                aggregate(0, g.h[:])
                ops.tt(cat[:, :, 0:D], summed[:, :, 0:D], spread(inv_deg[:], [P, TILES, D]), ALU.mult)
                ops.ts(cat[:, :, D:2 * D], g.h[:], 0.0, None, ALU.add)
                dense(0, True)
                aggregate(1, feat[:, :, 0:32])
                ops.tt(cat[:, :, 0:32], summed[:, :, 0:32], spread(inv_deg[:], [P, TILES, 32]), ALU.mult)
                ops.ts(cat[:, :, 32:64], feat[:, :, 0:32], 0.0, None, ALU.add)
                dense(1, False)
                ops.tt(g.x[:], g.x[:], feat[:, :, 0:D], ALU.add)
                norm_relu(g.h[:], g.x[:])
                ops.ts(g.root_in[:], g.deg[:], 1.0, None, ALU.add)
                asked[0] += 1
                dve.engine_nop().then_inc(root_asked, 1)
                dve.wait_ge(root_done, asked[0])
                c.step(dve.reciprocal(dinv[:], g.root_in[:]))
                source = g.h[:]
                for a in (2, 3, 4):
                    w = widths[a]
                    scale = spread(dinv[:], [P, TILES, w])
                    ops.tt(cat[:, :, 0:w], source, scale, ALU.mult)
                    aggregate(a, cat[:, :, 0:w])
                    ops.tt(cat[:, :, 0:w], cat[:, :, 0:w], summed[:, :, 0:w], ALU.add)
                    ops.tt(cat[:, :, 0:w], cat[:, :, 0:w], scale, ALU.mult)
                    dense(a, True)
                    source = feat[:, :, 0:dims[a][1]]
                for d in (5, 6, 7):
                    dense(d, True)
                ops.tt(g.x[:], g.x[:], feat[:, :, 0:D], ALU.add)
                norm_relu(g.h[:], g.x[:])
                dve.wait_ge(out_done, TILES)
                ops.tt(g.root_in[:], g.deg[:], g.outs[:], ALU.add)
                ops.ts(g.root_in[:], g.root_in[:], 1e-5, None, ALU.max)
                asked[0] += 1
                dve.engine_nop().then_inc(root_asked, 1)
                dve.wait_ge(root_done, asked[0])
                c.step(dve.reciprocal(g.dinv2[:], g.root_in[:]))


LOADS = 10 + 8


ROW = 2 + 2 * D
OWN = ROW + D + 2


def stage_sheaf(nc, g, ins):
    with ExitStack() as ctx:
        s = Scope(nc, ctx, "shf")
        table = s.sb("table", [P, TILES, OWN])
        own = s.sb("own", [P, TILES, OWN])
        W1 = s.sb("W1", [P, P])
        W2 = s.sb("W2", [P, 3 * D])
        b1 = s.sb("b1", [P, 1])
        b2 = s.sb("b2", [P, 3, D])
        cur = s.sb("cur", [P, 1])
        at_i = s.sb("at_i", [P, 1], I32)
        ids_next = s.sb("ids_next", [P, CHUNK], I32)
        ids = [s.sb(f"ids{h}", [P, HALF], I32) for h in range(2)]
        rows = [s.sb(f"rows{h}", [P, HALF, ROW]) for h in range(2)]
        h_pair = s.sb("h_pair", [P, CHUNK, 4, D])
        y_pair = s.sb("y_pair", [P, 2, CHUNK, 2, D])
        rank_s = s.sb("rank_s", [P, 4, CHUNK, 2])
        turned_sb = s.sb("turned_sb", [P, 4 * P])
        hidden = [s.sb(f"hidden{h}", [P, 4 * P]) for h in range(2)]
        left = s.sb("left", [P, 1])
        over, keep = s.sb("over", [P, CHUNK]), s.sb("keep", [P, CHUNK])
        src_hi = s.sb("src_hi", [P, CHUNK, 1])
        v = s.sb("v", [P, CHUNK, 3, D])
        vv = s.sb("vv", [P, CHUNK, 3, D])
        c2 = s.sb("c2", [P, CHUNK, 3])
        prod = s.sb("prod", [P, CHUNK, 2, D])
        dots = s.sb("dots", [P, CHUNK, 2])
        u = s.sb("u", [P, CHUNK, 2, D])
        msg = s.sb("msg", [P, 2, CHUNK, D])
        own_sum = s.sb("own_sum", [P, CHUNK, D])
        to_dst = s.sb("to_dst", [P, TILES, D])
        hot_lo = s.sb("hot_lo", [P, CHUNK, P])
        hot_hi = s.sb("hot_hi", [P, CHUNK, TILES])
        wide = s.sb("wide", [P, CHUNK, TILES, D])
        zeros = s.sb("zeros", [P, TILES * D])
        one = s.sb("one", [P, 1])
        turn_ps = s.ps("turn_ps", [P, 4 * P])
        hid_ps = [s.ps(f"hid_ps{h}", [P, 4 * P]) for h in range(2)]
        v_ps = s.ps("v_ps", [P, 512])
        sum_ps = s.ps("sum_ps", [P, 512])
        loaded, chain_a, chain_t, chain_c, table_ready, table_out, own_in, own_set = map(
            s.sem, ("loaded", "chain_a", "chain_t", "chain_c", "table_ready", "table_out", "own_in", "own_set"))
        zeroed, steps_own, ids_in, turned, copied, hid_done, hid_ready, v_done, v_read = map(
            s.sem, ("zeroed", "steps_own", "ids_in", "turned", "copied", "hid_done", "hid_ready",
                    "v_done", "v_read"))
        pair_read, wide_ready, wide_used, summed, root_asked, root_done, h_ready, h_out = map(
            s.sem, ("pair_read", "wide_ready", "wide_used", "summed", "root_asked", "root_done", "h_ready", "h_out"))
        hot_squared, hot_ready = s.sem("hot_squared"), s.sem("hot_ready")
        gathered = [s.sem(f"gathered{h}") for h in range(2)]
        rows_free = [s.sem(f"rows_free{h}") for h in range(2)]

        with nc.Block() as block:
            @block.sync
            def _(sp):
                n = 0
                sp.wait_ge(zeroed, 4)
                w1, w2 = ins["L2_gnn_W1"].rearrange("h k -> k h"), ins["L2_gnn_W2"].rearrange("o h -> h o")
                for half in range(2):
                    o = half * 64
                    for row, col, part in ((0, 0, 0), (32, 0, 1), (32, HID, 0), (0, HID, 1)):
                        sp.dma_start(W1[o + row:o + row + D, col:col + HID], w1[part * D:(part + 1) * D, :],
                                     allow_slow_non_contiguous=True).then_inc(loaded, 16)
                        n += 1
                for row, col in ((0, 0), (HID, D), (0, 2 * D)):
                    sp.dma_start(W2[row:row + HID, col:col + D], w2, allow_slow_non_contiguous=True).then_inc(loaded, 16)
                    n += 1
                for half in range(2):
                    sp.dma_start(b1[half * HID:(half + 1) * HID, :],
                                 ins["L2_gnn_b1"].rearrange("(h o) -> h o", o=1)).then_inc(loaded, 16)
                    n += 1
                sp.dma_start(b2[:], ins["L2_gnn_b2"].unsqueeze(0).unsqueeze(0).broadcast_to([P, 3, D])).then_inc(loaded, 16)
                assert n + 1 == SHEAF_LOADS
                sp.wait_ge(table_ready, 1)
                sp.dma_start(g.table_d[:].rearrange("(t p) c -> p t c", p=P), table[:]).then_inc(table_out, 16)
                sp.wait_ge(table_out, 16)
                sp.wait_ge(loaded, 16 * SHEAF_LOADS)

            @block.gpsimd
            def _(pool):
                for zero in (W1, W2, zeros, b1, h_pair):
                    pool.memset(zero[:], 0.0).then_inc(zeroed, 1)
                pool.memset(at_i[:], 0).then_inc(zeroed, 1)
                pool.memset(rank_s[:], 0.0).then_inc(zeroed, 1)
                pool.memset(one[:], 1.0).then_inc(zeroed, 1)
                free(pool, steps_own)
                pool.wait_ge(zeroed, 8)
                pool.wait_ge(table_out, 16)
                edges = g.src_d[:].rearrange("(e o) -> e o", o=1)
                spare = bass.IndirectOffsetOnAxis(at_i[:, 0:1], 0)
                pool.indirect_dma_start(ids_next[:], None, edges, spare).then_inc(ids_in, 16)
                for h in range(2):
                    pool.indirect_dma_start(rows[h][:, 0, :], None, g.table_d[:], spare).then_inc(gathered[h], 16)
                for t in range(TILES):
                    pool.indirect_dma_start(own[:, t, :], None, g.table_d[:],
                                            bass.IndirectOffsetOnAxis(g.node_i[:, t:t + 1], 0)).then_inc(own_in, 16)
                for landed in (ids_in, *gathered):
                    pool.wait_ge(landed, 16)
                k_reg, reg = pool.alloc_register("shf_pool_k"), pool.alloc_register("shf_pool_value")
                pool.reg_mov(k_reg, 0)
                pool.reg_mov(reg, 0)
                with pool.Fori(0, TILES) as t:
                    k = pool.snap(k_reg)
                    pool.wait_ge(ids_in, settled(pool, reg, zeroed, k * 16 + (t * 16 + 16)))
                    pool.wait_ge(steps_own, settled(pool, reg, zeroed, k * 4 + (t * 2 + 1)))
                    pool.tensor_copy(cur[:], g.first_s[:, bass.ds(t, 1)]).then_inc(steps_own, 1)
                    pool.wait_ge(steps_own, settled(pool, reg, zeroed, k * 4 + (t * 2 + 2)))
                    pool.tensor_copy(at_i[:], cur[:]).then_inc(steps_own, 1)
                    pool.wait_ge(steps_own, settled(pool, reg, zeroed, k * 4 + (t * 2 + 3)))
                    pool.indirect_dma_start(ids_next[:], None, edges, bass.IndirectOffsetOnAxis(at_i[:, 0:1], 0)).then_inc(ids_in, 16)
                    chunks = pool.value_load(g.loops[0:1, bass.ds(t, 1)], min_val=2, max_val=E)
                    with pool.Fori(0, chunks):
                        k = pool.snap(k_reg)
                        base = k * 4 + (t * 2 + 3)
                        pool.wait_ge(ids_in, settled(pool, reg, zeroed, k * 16 + (t * 16 + 32)))
                        for h in range(2):
                            pool.wait_ge(gathered[h], settled(pool, reg, zeroed, k * (16 * HALF) + 16))
                            pool.tensor_copy(ids[h][:], ids_next[:, h * HALF:(h + 1) * HALF]).then_inc(steps_own, 1)
                            pool.wait_ge(steps_own, settled(pool, reg, zeroed, base + (h + 1)))
                            if h == 1:
                                pool.tensor_scalar(cur[:], cur[:], float(CHUNK), float(E), ALU.add, ALU.min).then_inc(steps_own, 1)
                                pool.wait_ge(steps_own, settled(pool, reg, zeroed, base + 3))
                                pool.tensor_copy(at_i[:], cur[:]).then_inc(steps_own, 1)
                                pool.wait_ge(steps_own, settled(pool, reg, zeroed, base + 4))
                                pool.indirect_dma_start(ids_next[:], None, edges,
                                                        bass.IndirectOffsetOnAxis(at_i[:, 0:1], 0)).then_inc(ids_in, 16)
                            pool.wait_ge(rows_free[h], settled(pool, reg, zeroed, k + 1))
                            for r in range(HALF):
                                pool.indirect_dma_start(rows[h][:, r, :], None, g.table_d[:],
                                                        bass.IndirectOffsetOnAxis(ids[h][:, r:r + 1], 0)).then_inc(gathered[h], 16)
                        pool.reg_add(k_reg, k_reg, 1)
                k = pool.snap(k_reg)
                pool.wait_ge(ids_in, settled(pool, reg, zeroed, k * 16 + (16 * TILES + 16)))
                pool.wait_ge(h_ready, 1)
                for t in range(TILES):
                    pool.indirect_dma_start(g.h_d[:], bass.IndirectOffsetOnAxis(g.node_i[:, t:t + 1], 0),
                                            g.h[:, t, :], None).then_inc(h_out, 16)
                pool.wait_ge(h_out, 16 * TILES)

            @block.tensor
            def _(pe):
                def turn(k):
                    pe.wait_ge(rows_free[1], k + 2)
                    pe.wait_ge(copied, k + 1)
                    for j in range(CHUNK // 2):
                        mm = pe.transpose(turn_ps[:, j * P:(j + 1) * P],
                                          h_pair[:, 2 * j:2 * j + 2].rearrange("p t a d -> p (t a d)"),
                                          g.const[:, C_EYE:C_EYE + P])
                    mm.then_inc(turned, 1)

                def hide(k):
                    pe.wait_ge(copied, k + 2)
                    pe.wait_ge(hid_ready, k * 2 + 1)
                    for h in range(2):
                        pe.matmul(hid_ps[h][:], W1[64 * h:64 * h + 64, :], turned_sb[64 * h:64 * h + 64, :],
                                  start=True, stop=True).then_inc(hid_done, 1)

                def form(k):
                    pe.wait_ge(hid_ready, k * 2 + 3)
                    pe.wait_ge(v_read, k + 1)
                    for t in range(CHUNK):
                        j, h = t // 2, t % 2
                        mm = pe.matmul(v_ps[:, t * 3 * D:(t + 1) * 3 * D], hidden[h][:, j * P:(j + 1) * P], W2[:],
                                       start=True, stop=True)
                    mm.then_inc(v_done, 1)

                def add(k, half):
                    pe.wait_ge(wide_ready, k * 2 + (half + 3))
                    if half == 0:
                        pe.wait_ge(hot_ready, k + 3)
                    for t in range(half * HALF, (half + 1) * HALF):
                        mm = pe.matmul(sum_ps[:, 0:TILES * D], hot_lo[:, t, :], wide[:, t].rearrange("p s d -> p (s d)"),
                                       start=False, stop=False, skip_group_check=True)
                    mm.then_inc(wide_used, 1)

                pe.wait_ge(loaded, 16 * SHEAF_LOADS)
                pe.wait_ge(zeroed, 8)
                pe.matmul(sum_ps[:, 0:TILES * D], zeros[:, 0:P], zeros[:], start=True, stop=False, skip_group_check=True)
                for k in range(2):
                    turn(k)
                    hide(k)
                    form(k)
                last = pe.value_load(g.loops[0:1, TILES + 1:TILES + 2], min_val=2 * TILES - 1, max_val=E)
                with pe.Fori(0, last - 1) as k:
                    turn(k + 2)
                    add(k, 0)
                    hide(k + 2)
                    add(k, 1)
                    form(k + 2)
                for k in (last - 1, last):
                    add(k, 0)
                    add(k, 1)
                pe.matmul(sum_ps[:, 0:TILES * D], zeros[:, 0:P], zeros[:], start=False, stop=True,
                          skip_group_check=True).then_inc(summed, 1)

            @block.scalar
            def _(act):
                act.wait_ge(loaded, 16 * SHEAF_LOADS)
                act.wait_ge(zeroed, 8)
                act.wait_ge(own_in, 16 * TILES)

                def hot_rows(k):
                    act.wait_ge(wide_used, k * 2 + 1)
                    for t in range(CHUNK):
                        squares = act.activation(hot_lo[:, t, :], g.const[:, C_IOTA:C_IOTA + P], ACT.Square,
                                                 bias=rank_s[:, bass.ds((k + 2) % 4, 1), t, 0:1].rearrange("p o a -> p (o a)"))
                    squares.then_inc(hot_squared, 1)
                    act.wait_ge(hot_squared, k + 1)
                    act.activation(hot_lo[:], hot_lo[:], ACT.Relu, scale=-1.0, bias=one[:, 0:1]).then_inc(hot_ready, 1)

                k_reg = act.alloc_register("shf_act_k")
                act.reg_mov(k_reg, 0)
                with act.Fori(0, TILES) as t:
                    chunks = act.value_load(g.loops[0:1, bass.ds(t, 1)], min_val=2, max_val=E)
                    with act.Fori(0, chunks):
                        k = act.snap(k_reg)
                        even_odd = bass.ds(k % 2, 1)
                        own_row = own[:, bass.ds(t, 1), :]
                        act.wait_ge(turned, k + 1)
                        act.wait_ge(pair_read, k + 1)
                        act.activation(h_pair[:, :, 2, :], own_row[:, :, 2:2 + D].broadcast_to([P, CHUNK, D]), ACT.Copy)
                        act.activation(y_pair[:, even_odd, :, 1, :].rearrange("p o t d -> p (o t) d"),
                                       own_row[:, :, 2 + D:ROW].broadcast_to([P, CHUNK, D]), ACT.Copy)
                        for h in range(2):
                            slots = slice(h * HALF, (h + 1) * HALF)
                            act.wait_ge(gathered[h], k * (16 * HALF) + (16 * HALF + 16))
                            act.activation(y_pair[:, even_odd, slots, 0, :].rearrange("p o t d -> p (o t) d"),
                                           rows[h][:, :, 2 + D:ROW], ACT.Copy)
                            act.activation(rank_s[:, bass.ds(k % 4, 1), slots, :].rearrange("p o t d -> p (o t) d"),
                                           rows[h][:, :, 0:2], ACT.Copy)
                            done = act.activation(h_pair[:, slots, 0, :], rows[h][:, :, 2:2 + D], ACT.Copy)
                            done.then_inc(rows_free[h], 1)
                        hot_rows(k)
                        act.wait_ge(turned, k + 2)
                        act.wait_ge(hid_done, k * 2 + 1)
                        act.activation(turned_sb[:], turn_ps[:], ACT.Copy).then_inc(copied, 1)
                        act.wait_ge(v_done, k + 1)
                        for h in range(2):
                            act.wait_ge(hid_done, k * 2 + (h + 2))
                            act.activation(hidden[h][:], hid_ps[h][:], ACT.Relu, bias=b1[:, 0:1]).then_inc(hid_ready, 1)
                        act.reg_add(k_reg, k_reg, 1)
                k = act.snap(k_reg)
                hot_rows(k)
                hot_rows(k + 1)
                act.wait_ge(root_asked, 1)
                act.activation(g.root_in[:], g.root_in[:], ACT.Sqrt).then_inc(root_done, 1)

            @block.vector
            def _(dve):
                free(dve, turned, copied, hid_done, hid_ready, v_done, v_read, pair_read, pair_read, *rows_free, *[wide_used] * 5, *[wide_ready] * 2)
                c = Chain(dve, chain_a)
                c(dve.memset(table[:, :, OWN - 1], 0.0))
                c(dve.tensor_scalar(table[:, :, 0:1], g.rank_parts[:, :, 0:1], -1.0, None, ALU.mult))
                c(dve.tensor_copy(table[:, :, 1:2], g.rank_parts[:, :, 1:2]))
                c(dve.tensor_copy(table[:, :, 2:2 + D], g.h[:]))
                c(dve.tensor_tensor(table[:, :, 2 + D:ROW], g.h[:], spread(g.dinv2[:], [P, TILES, D]), ALU.mult))
                c(dve.tensor_copy(table[:, :, ROW:ROW + D], g.x[:]))
                c.publish(dve.tensor_copy(table[:, :, ROW + D], g.dinv2[:]), table_ready, 1)
                c.sync()
                dve.wait_ge(loaded, 16 * SHEAF_LOADS)
                before = c.n

                def step(c, k):
                    even_odd = bass.ds(k % 2, 1)
                    y = y_pair[:, even_odd].rearrange("p o t a d -> p (o t) a d")
                    rank = rank_s[:, bass.ds(k % 4, 1)].rearrange("p o t a -> p (o t) a")
                    shape = [P, CHUNK, 2, D]
                    iota = g.const[:, C_IOTA:C_IOTA + CHUNK]
                    c(dve.tensor_scalar(over[:], iota, left[:, 0:1], None, ALU.is_ge))
                    c(dve.tensor_scalar(keep[:], iota, left[:, 0:1], None, ALU.is_lt))
                    c.sync()
                    c(dve.tensor_scalar(left[:], left[:], float(-CHUNK), None, ALU.add))
                    dve.wait_ge(v_done, k + 2)
                    c.publish(dve.tensor_tensor(v[:], v_ps[:, 0:CHUNK * 3 * D].rearrange("p (t a d) -> p t a d", t=CHUNK, a=3),
                                                b2[:].unsqueeze(1).broadcast_to([P, CHUNK, 3, D]), ALU.add),
                              v_read, k + 2)
                    c(dve.tensor_tensor(vv[:], v[:], v[:], ALU.mult))
                    dve.wait_ge(rows_free[1], k + 2)
                    c(dve.scalar_tensor_tensor(out=src_hi[:], in0=over[:].unsqueeze(2), scalar=1000.0, in1=rank[:, :, 1:2],
                                               op0=ALU.mult, op1=ALU.add))
                    c(dve.tensor_tensor(y[:, :, 0, :], y[:, :, 0, :], spread(keep[:], [P, CHUNK, D]), ALU.mult))
                    c.sync()
                    c.step(dve.tensor_reduce(c2[:], vv[:], AX.X, ALU.add))
                    c.step(dve.tensor_scalar(c2[:], c2[:], 1e-24, 0.5, ALU.max, ALU.mult))
                    c.step(dve.reciprocal(c2[:], c2[:]))

                    def reflect(out, vec, scale, x, last_read=None):
                        c.step(dve.tensor_tensor(prod[:], vec, x, ALU.mult))
                        c.step(dve.tensor_reduce(dots[:], prod[:], AX.X, ALU.add))
                        c.step(dve.tensor_tensor(dots[:], dots[:], scale, ALU.mult))
                        c.step(dve.tensor_tensor(prod[:], vec, spread(dots[:], shape), ALU.mult))
                        done = dve.tensor_tensor(out, x, prod[:], ALU.subtract)
                        if last_read is None:
                            c.step(done)
                        else:
                            c.publish(done, *last_read)

                    reflect(u[:], v[:, :, 0:2, :], c2[:, :, 0:2], y, (pair_read, k + 3))
                    reflect(msg[:].rearrange("p a t d -> p t a d"), v[:, :, 1:3, :], c2[:, :, 1:3], u[:])
                    c(dve.tensor_tensor(own_sum[:], own_sum[:], msg[:, 0], ALU.add))
                    dve.wait_ge(wide_used, k * 2 + 5)
                    c.step(dve.tensor_tensor(hot_hi[:], spread(src_hi[:, :, 0], [P, CHUNK, TILES]),
                                             g.const[:, C_IOTA:C_IOTA + TILES].unsqueeze(1).broadcast_to([P, CHUNK, TILES]),
                                             ALU.is_equal))
                    for half in range(2):
                        slots, shape_w = slice(half * HALF, (half + 1) * HALF), [P, HALF, TILES, D]
                        dve.tensor_tensor(wide[:, slots], spread(hot_hi[:, slots, :], shape_w),
                                          msg[:, 1, slots].unsqueeze(2).broadcast_to(shape_w), ALU.mult).then_inc(wide_ready, 1)
                    assert c.n == SHEAF_STEPS, c.n

                k_reg = dve.alloc_register("shf_dve_k")
                dve.reg_mov(k_reg, 0)
                with dve.Fori(0, TILES) as t:
                    ct = Chain(dve, chain_t, t * 3)
                    ct(dve.tensor_copy(left[:], g.deg_s[:, bass.ds(t, 1)]))
                    ct(dve.memset(own_sum[:], 0.0))
                    ct.sync()
                    chunks = dve.value_load(g.loops[0:1, bass.ds(t, 1)], min_val=2, max_val=E)
                    with dve.Fori(0, chunks):
                        k = dve.snap(k_reg)
                        step(Chain(dve, chain_c, k * SHEAF_STEPS), k)
                        dve.reg_add(k_reg, k_reg, 1)
                    dve.wait_ge(chain_c, dve.snap(k_reg) * SHEAF_STEPS)
                    ct.step(dve.tensor_reduce(to_dst[:, bass.ds(t, 1), :].rearrange("p o d -> p (o d)"),
                                              own_sum[:].rearrange("p t d -> p d t"), AX.X, ALU.add))
                dve.wait_ge(summed, 1)
                c = Chain(dve, chain_a, before)
                shape = [P, TILES, D]
                c.step(dve.tensor_tensor(to_dst[:], sum_ps[:, 0:TILES * D].rearrange("p (t d) -> p t d", t=TILES), to_dst[:], ALU.add))
                c.step(dve.tensor_tensor(to_dst[:], to_dst[:], own[:, :, ROW + D:ROW + D + 1].broadcast_to(shape), ALU.mult))
                c.step(dve.tensor_tensor(to_dst[:], to_dst[:], own[:, :, 2:2 + D], ALU.add))
                c.step(dve.tensor_scalar(to_dst[:], to_dst[:], 0.0, None, ALU.max))
                c.step(dve.tensor_tensor(g.x[:], own[:, :, ROW:ROW + D], to_dst[:], ALU.add))
                norm(dve, c, g, g.h[:], g.x[:], root_asked, root_done, [0])
                dve.engine_nop().then_inc(h_ready, 1)


SHEAF_LOADS = 8 + 3 + 2 + 1
SHEAF_STEPS = 3 + 3 + 3 + 9 + 1 + 1


def stage_attention(nc, g, ins, out):
    C2 = D * D
    with ExitStack() as ctx:
        s = Scope(nc, ctx, "att")
        wf = s.sb("wf", [P, 2 * C2])
        wr = s.sb("wr", [P, 2 * C2])
        wp = [s.sb(f"wp{i}", [P, 2 * C2], BF16) for i in range(3)]
        w6 = s.sb("w6", [P, 2 * C2], BF16)
        cur = s.sb("cur", [P, 1])
        at_i = s.sb("at_i", [P, 1], I32)
        ids_next = s.sb("ids_next", [P, CHUNK], I32)
        ids = [s.sb(f"ids{h}", [P, HALF], I32) for h in range(2)]
        ea = s.sb("ea", [P, CHUNK, D])
        ea_rest = s.sb("ea_rest", [P, CHUNK, D])
        ea_parts = s.sb("ea_parts", [P, CHUNK, P], BF16)
        ea_t = [s.sb(f"ea_t{h}", [P, HALF, P], BF16) for h in range(2)]
        hs = [s.sb(f"hs{h}", [P, HALF, D]) for h in range(2)]
        e12_all = s.sb("e12", [P, 2, 2, HALF, 2 * C2])
        top, top_was, shift = s.sb("top", [P, C2]), s.sb("top_was", [P, C2]), s.sb("shift", [P, C2])
        top_odd = s.sb("top_odd", [P, C2])
        decay = s.sb("decay", [P, C2])
        sums = s.sb("sums", [P, 2, C2])
        left, over = s.sb("left", [P, 1]), s.sb("over", [P, CHUNK])
        off_max, off_exp = s.sb("off_max", [P, CHUNK]), s.sb("off_exp", [P, CHUNK])
        ratio = s.sb("ratio", [P, C2])
        ft = s.sb("ft", [P, TILES + 1, D])
        zeros = s.sb("zeros", [P, 2 * C2])
        warm = s.sb("warm", [P, 1])
        w_ps = [s.ps(f"w_ps{r}", [P, 2 * C2]) for r in range(HALF)]
        t_ps = s.ps("t_ps", [P, HALF, P], BF16)
        sum_ps = s.ps("sum_ps", [P, 2 * C2])
        w_in, zeroed, w_ready_s, chain0, chain_f, chain_l, own = map(
            s.sem, ("w_in", "zeroed", "w_ready", "chain0", "chain_f", "chain_l", "own"))
        part1, left1, part2, part3 = map(s.sem, ("part1", "left1", "part2", "part3"))
        ids_in, ea_in, shift_ready, decay_ready, sums_done, sum_added, stored = map(
            s.sem, ("ids_in", "ea_in", "shift_ready", "decay_ready", "sums_done", "sum_added", "stored"))
        hs_in, turned, ea_t_ready, w_done, w_used, sub_ready, exp_ready, num_ready, half_done = (
            [s.sem(f"{name}{h}") for h in range(2)] for name in
            ("hs_in", "turned", "ea_t_ready", "w_done", "w_used", "sub_ready", "exp_ready", "num_ready", "half_done"))

        def e12(k, h, r=None):
            half = e12_all[:, bass.ds(k % 2, 1), h, :, :].rearrange("p o r c -> p (o r) c")
            return half if r is None else half[:, r, :]

        def last_chunk(eng):
            return eng.value_load(g.loops[0:1, TILES + 1:TILES + 2], min_val=2 * TILES - 1, max_val=E)

        with nc.Block() as block:
            @block.sync
            def _(sp):
                sp.wait_ge(zeroed, 2)
                n = 0
                for col, w, bias in ((0, "L3_gnn_W_msg", "L3_gnn_b_msg"), (C2, "L3_gnn_W_attn", "L3_gnn_b_attn")):
                    for part in range(6):
                        sp.dma_start(wf[part * D:(part + 1) * D, col:col + C2], ins[w]).then_inc(w_in, 16)
                        n += 1
                    for part in range(3):
                        sp.dma_start(wf[6 * D + part:6 * D + part + 1, col:col + C2], ins[bias].rearrange("(a n) -> a n", a=1)).then_inc(w_in, 16)
                        n += 1
                assert n == 18
                sp.wait_ge(w_in, 16 * n)

            @block.gpsimd
            def _(pool):
                pool.memset(wf[:], 0.0).then_inc(zeroed, 1)
                pool.memset(zeros[:], 0.0).then_inc(zeroed, 1)
                pool.memset(ea_parts[:, :, 6 * D:P], 0.0).then_inc(zeroed, 1)
                for parity in range(2):
                    pool.memset(e12_all[:, parity, 1], 0.0).then_inc(zeroed, 1)
                pool.wait_ge(zeroed, 5)
                pool.memset(ea_parts[:, :, 6 * D:6 * D + 3], 1.0).then_inc(zeroed, 1)
                k_reg = pool.alloc_register("att_pool_k")
                pool.reg_mov(k_reg, 0)
                reg = pool.alloc_register("att_pool_carrier")
                pool.reg_mov(reg, 0)
                free(pool, own)

                def weighted(k):
                    e1, e2 = e12(k, 1)[:, :, 0:C2], e12(k, 1)[:, :, C2:2 * C2]
                    pool.wait_ge(exp_ready[1], settled(pool, reg, zeroed, k * HALF + 1))
                    pool.tensor_tensor(e1, e1, e2, ALU.mult).then_inc(num_ready[1], 1)

                edges = g.src_d[:].rearrange("(e o) -> e o", o=1)
                pool.memset(at_i[:], 0).then_inc(zeroed, 1)
                pool.wait_ge(zeroed, 7)
                spare = bass.IndirectOffsetOnAxis(at_i[:, 0:1], 0)
                pool.indirect_dma_start(ids_next[:], None, edges, spare).then_inc(ids_in, 16)
                pool.indirect_dma_start(ea[:].rearrange("p c k -> p (c k)"), None, g.ea_d[:], spare).then_inc(ea_in, 16)
                for h in range(2):
                    pool.indirect_dma_start(hs[h][:, 0, :], None, g.h_d[:], spare).then_inc(hs_in[h], 16)
                for gathered in (ids_in, ea_in, *hs_in):
                    pool.wait_ge(gathered, 16)
                with pool.Fori(0, TILES) as t:
                    k = pool.snap(k_reg)
                    pool.wait_ge(ids_in, settled(pool, reg, zeroed, k * 16 + (t * 16 + 16)))
                    pool.wait_ge(ea_in, settled(pool, reg, zeroed, k * 16 + 16))
                    pool.wait_ge(own, settled(pool, reg, zeroed, k * 4 + (t * 2 + 1)))
                    pool.tensor_copy(cur[:], g.first_s[:, bass.ds(t, 1)]).then_inc(own, 1)
                    pool.wait_ge(own, settled(pool, reg, zeroed, k * 4 + (t * 2 + 2)))
                    pool.tensor_copy(at_i[:], cur[:]).then_inc(own, 1)
                    pool.wait_ge(own, settled(pool, reg, zeroed, k * 4 + (t * 2 + 3)))
                    pool.indirect_dma_start(ids_next[:], None, edges, bass.IndirectOffsetOnAxis(at_i[:, 0:1], 0)).then_inc(ids_in, 16)
                    chunks = pool.value_load(g.loops[0:1, bass.ds(t, 1)], min_val=2, max_val=E)
                    with pool.Fori(0, chunks):
                        k = pool.snap(k_reg)
                        base = k * 4 + (t * 2 + 3)
                        pool.wait_ge(left1, settled(pool, reg, zeroed, k + 1))
                        pool.indirect_dma_start(ea[:].rearrange("p c k -> p (c k)"), None, g.ea_d[:],
                                                bass.IndirectOffsetOnAxis(at_i[:, 0:1], 0)).then_inc(ea_in, 16)
                        weighted(k)
                        pool.wait_ge(ids_in, settled(pool, reg, zeroed, k * 16 + (t * 16 + 32)))
                        for h in range(2):
                            pool.wait_ge(hs_in[h], settled(pool, reg, zeroed, k * (16 * HALF) + 16))
                            pool.tensor_copy(ids[h][:], ids_next[:, h * HALF:(h + 1) * HALF]).then_inc(own, 1)
                            pool.wait_ge(own, settled(pool, reg, zeroed, base + (h + 1 if h == 0 else 2)))
                            if h == 1:
                                pool.wait_ge(ea_in, settled(pool, reg, zeroed, k * 16 + 32))
                                pool.tensor_scalar(cur[:], cur[:], float(CHUNK), float(E), ALU.add, ALU.min).then_inc(own, 1)
                                pool.wait_ge(own, settled(pool, reg, zeroed, base + 3))
                                pool.tensor_copy(at_i[:], cur[:]).then_inc(own, 1)
                                pool.wait_ge(own, settled(pool, reg, zeroed, base + 4))
                                pool.indirect_dma_start(ids_next[:], None, edges,
                                                        bass.IndirectOffsetOnAxis(at_i[:, 0:1], 0)).then_inc(ids_in, 16)
                            pool.wait_ge(w_used[h], settled(pool, reg, zeroed, k * HALF + 1))
                            for r in range(HALF):
                                pool.indirect_dma_start(hs[h][:, r, :], None, g.h_d[:],
                                                        bass.IndirectOffsetOnAxis(ids[h][:, r:r + 1], 0)).then_inc(hs_in[h], 16)
                        pool.reg_add(k_reg, k_reg, 1)
                k = pool.snap(k_reg)
                pool.wait_ge(ids_in, settled(pool, reg, zeroed, k * 16 + (16 * TILES + 16)))
                pool.wait_ge(left1, settled(pool, reg, zeroed, k + 1))
                pool.indirect_dma_start(ea[:].rearrange("p c k -> p (c k)"), None, g.ea_d[:],
                                        bass.IndirectOffsetOnAxis(at_i[:, 0:1], 0)).then_inc(ea_in, 16)
                pool.wait_ge(ea_in, settled(pool, reg, zeroed, k * 16 + 32))
                weighted(k)
                weighted(k + 1)
                pool.wait_ge(chain0, END_STEPS)
                for t in range(TILES):
                    n = min(P, N - t * P)
                    pool.indirect_dma_start(out[:], bass.IndirectOffsetOnAxis(g.node_i[0:n, t:t + 1], 0),
                                            ft[0:n, t + 1, :], None).then_inc(stored, 16)
                pool.wait_ge(stored, 16 * TILES)

            @block.tensor
            def _(pe):
                def turn(k, h):
                    if h == 0:
                        pe.wait_ge(part3, k + 1)
                        pe.wait_ge(ea_t_ready[1], k + 1)
                    else:
                        pe.wait_ge(ea_t_ready[0], k + 2)
                    for r in range(HALF):
                        mm = pe.transpose(t_ps[:, r, :], ea_parts[:, h * HALF + r, :], g.eye_bf[:])
                    mm.then_inc(turned[h], 1)

                def weigh(k, h, ahead=True):
                    pe.wait_ge(ea_t_ready[h], k + 2)
                    for r in range(HALF):
                        if h == 1:
                            pe.wait_ge(w_used[0], k * HALF + (r + 2))
                        else:
                            pe.wait_ge(w_used[1], k * HALF - HALF + (r + 2) if ahead else 1)
                        pe.matmul(w_ps[r][:], ea_t[h][:, r, :], w6[:], start=True, stop=True).then_inc(w_done[h], 1)

                def add(k, h, slots=range(HALF)):
                    if h == 0 and slots[0] == 0:
                        pe.wait_ge(sum_added, k + 1)
                    if slots[0] == 0:
                        pe.wait_ge(num_ready[h], k + (1 + 2 * h))
                    for r in slots:
                        mm = pe.matmul(sum_ps[:], g.const[:, C_EYE:C_EYE + P], e12(k, h, r),
                                       start=h == 0 and r == 0, stop=h == 1 and r == HALF - 1)
                    if slots[-1] == HALF - 1:
                        mm.then_inc(half_done[h], 1)

                pe.wait_ge(zeroed, 2)
                pe.matmul(sum_ps[:], zeros[:, 0:P], zeros[:], start=True, stop=True).then_inc(sums_done, 1)
                pe.wait_ge(w_ready_s, 1)
                turn(0, 0)
                turn(0, 1)
                weigh(0, 0, ahead=False)
                last = last_chunk(pe)
                weigh(0, 1)
                turn(1, 0)
                turn(1, 1)
                weigh(1, 0)
                with pe.Fori(1, last) as k:
                    add(k - 1, 0, range(0, HALF // 2))
                    weigh(k, 1)
                    add(k - 1, 0, range(HALF // 2, HALF))
                    add(k - 1, 1)
                    turn(k + 1, 0)
                    turn(k + 1, 1)
                    weigh(k + 1, 0)
                add(last - 1, 0)
                weigh(last, 1)
                add(last - 1, 1)
                add(last, 0)
                add(last, 1)

            @block.scalar
            def _(act):
                def copy(k, h):
                    act.wait_ge(turned[h], k + 2)
                    act.wait_ge(w_done[h], k * HALF + 1)
                    act.activation(ea_t[h][:], t_ps[:], ACT.Copy).then_inc(ea_t_ready[h], 1)

                def part(k):
                    act.wait_ge(ea_in, k * 16 + 32)
                    act.wait_ge(turned[1], k + 1)
                    act.activation(ea_parts[:, :, 0:3 * D].rearrange("p t (c d) -> p t c d", c=3),
                                   ea[:].unsqueeze(2).broadcast_to([P, CHUNK, 3, D]), ACT.Copy).then_inc(part1, 1)
                    act.wait_ge(left1, k + 2)
                    act.activation(ea_parts[:, :, 3 * D:5 * D].rearrange("p t (c d) -> p t c d", c=2),
                                   ea_rest[:].unsqueeze(2).broadcast_to([P, CHUNK, 2, D]), ACT.Copy).then_inc(part2, 1)

                def exps(k):
                    act.wait_ge(shift_ready, k + 1)
                    act.activation(decay[:], shift[:], ACT.Exp).then_inc(decay_ready, 1)
                    for h in range(2):
                        act.wait_ge(sub_ready[h], k + 1)
                        for r in range(HALF):
                            e2 = e12(k, h, r)[:, C2:2 * C2]
                            act.activation(e2, e2, ACT.Exp, bias=off_exp[:, h * HALF + r:h * HALF + r + 1]).then_inc(exp_ready[h], 1)

                act.wait_ge(zeroed, 2)
                act.activation(warm[:], zeros[:, 0:1], ACT.Exp)
                act.wait_ge(zeroed, 7)
                part(0)
                copy(0, 0)
                copy(0, 1)
                last = last_chunk(act)
                with act.Fori(0, last) as k:
                    part(k + 1)
                    copy(k + 1, 0)
                    copy(k + 1, 1)
                    exps(k)
                part(last + 1)
                exps(last)

            @block.vector
            def _(dve):
                free(dve, *w_used, *turned, *w_done, *half_done, *half_done, *ea_t_ready, decay_ready, left1, *[exp_ready[1]] * (HALF + 1))
                c = Chain(dve, chain0)
                dve.wait_ge(w_in, 16 * 18)
                for i in range(3):
                    now = wf if i == 0 else wr
                    c.step(dve.tensor_copy(wp[i][:], now[:]))
                    if i < 2:
                        c.step(dve.tensor_tensor(wr[:], now[:], wp[i][:], ALU.subtract))
                c.step(dve.tensor_scalar(wf[:], wp[0][:], g.const[:, C_PART:C_PART + 1], None, ALU.mult))
                c.step(dve.scalar_tensor_tensor(out=wf[:], in0=wp[1][:], scalar=g.const[:, C_PART + 1:C_PART + 2], in1=wf[:],
                                                op0=ALU.mult, op1=ALU.add))
                c.step(dve.scalar_tensor_tensor(out=w6[:], in0=wp[2][:], scalar=g.const[:, C_PART + 2:C_PART + 3], in1=wf[:],
                                                op0=ALU.mult, op1=ALU.add))
                dve.engine_nop().then_inc(w_ready_s, 1)
                c.step(dve.memset(sums[:], 0.0))
                before = c.n

                def add_sums(c, k):
                    dve.wait_ge(sums_done, 1)
                    dve.wait_ge(half_done[1], k + 2)
                    c.publish(dve.tensor_tensor(sums[:], sums[:], sum_ps[:].rearrange("p (a c) -> p a c", a=2), ALU.add),
                              sum_added, k + 1)

                def finish(c, slot):
                    c.step(dve.tensor_scalar(ratio[:], sums[:, 1, :], 1e-30, None, ALU.max))
                    c.step(dve.reciprocal(ratio[:], ratio[:]))
                    c.step(dve.tensor_tensor(ratio[:], ratio[:], sums[:, 0, :], ALU.mult))
                    c.step(dve.tensor_reduce(ft[:, slot, :], ratio[:].rearrange("p (i j) -> p j i", i=D), AX.X, ALU.add))

                def rest1(k):
                    dve.wait_ge(part1, k + 1)
                    dve.tensor_tensor(ea_rest[:], ea[:], ea_parts[:, :, 0:D], ALU.subtract).then_inc(left1, 1)

                def rest2(k):
                    dve.wait_ge(part2, k + 1)
                    dve.wait_ge(left1, k + 2)
                    dve.tensor_tensor(ea_parts[:, :, 5 * D:6 * D], ea_rest[:], ea_parts[:, :, 3 * D:4 * D],
                                      ALU.subtract).then_inc(part3, 1)

                def weighted(k):
                    dve.wait_ge(exp_ready[0], k * HALF + HALF)
                    e1, e2 = e12(k, 0)[:, :, 0:C2], e12(k, 0)[:, :, C2:2 * C2]
                    dve.tensor_tensor(e1, e1, e2, ALU.mult).then_inc(num_ready[0], 1)

                def step(c, k, first, t):
                    if first:
                        c(dve.tensor_copy(left[:], g.deg_s[:, bass.ds(t, 1)]))
                        c(dve.memset(top_was[:], LOWEST))
                        c(dve.memset(top[:], LOWEST))
                        c(dve.memset(top_odd[:], LOWEST))
                    else:
                        c(dve.tensor_scalar(left[:], left[:], float(-CHUNK), None, ALU.add))
                        c(dve.tensor_copy(top_was[:], top[:]))

                    def mask(r):
                        if r == 0:
                            c.sync()
                            c(dve.tensor_scalar(over[:], g.const[:, C_IOTA:C_IOTA + CHUNK], left[:, 0:1], None, ALU.is_ge))
                        elif r == 1:
                            c.sync()
                            c(dve.tensor_scalar(off_max[:], over[:], OFF_MAX, None, ALU.mult))
                            dve.wait_ge(exp_ready[1], k * HALF + (HALF + 1))
                            c(dve.tensor_scalar(off_exp[:], over[:], OFF_EXP, None, ALU.mult))

                    for h in range(2):
                        dve.wait_ge(hs_in[h], k * (16 * HALF) + (16 * HALF + 16))
                        dve.wait_ge(half_done[h], k + 1)
                        if h == 1:
                            dve.wait_ge(num_ready[1], k + 1)
                        for r in range(HALF):
                            dve.wait_ge(w_done[h], k * HALF + (r + 2))
                            dve.tensor_tensor(e12(k, h, r).rearrange("p (a i j) -> p a i j", a=2, i=D),
                                              w_ps[r][:].rearrange("p (a i j) -> p a i j", a=2, i=D),
                                              hs[h][:, r, :].unsqueeze(1).unsqueeze(3).broadcast_to([P, 2, D, D]),
                                              ALU.mult).then_inc(w_used[h], 1)
                            if h == 0:
                                mask(r)
                        dve.wait_ge(w_used[h], k * HALF + (HALF + 1))
                        if h == 1:
                            rest2(k + 1)
                        for r in range(HALF):
                            n = h * HALF + r
                            m = top if r % 2 == 0 else top_odd
                            if r >= 2 or h:
                                dve.wait_ge(c.sem, c.base + (c.n - 1))
                            c(dve.scalar_tensor_tensor(out=m[:], in0=e12(k, h, r)[:, C2:2 * C2], scalar=off_max[:, n:n + 1],
                                                       in1=m[:], op0=ALU.add, op1=ALU.max))
                        if h == 0:
                            dve.wait_ge(part3, k + 1)
                            rest1(k + 1)
                    c.sync()
                    c.step(dve.tensor_tensor(top[:], top[:], top_odd[:], ALU.max))
                    dve.wait_ge(decay_ready, k + 1)
                    dve.tensor_tensor(shift[:], top_was[:], top[:], ALU.subtract).then_inc(shift_ready, 1)
                    for h in range(2):
                        e2 = e12(k, h)[:, :, C2:2 * C2]
                        dve.tensor_tensor(e2, e2, top[:].unsqueeze(1).broadcast_to([P, HALF, C2]), ALU.subtract).then_inc(sub_ready[h], 1)
                    add_sums(c, k)
                    if first:
                        finish(c, bass.ds(t, 1))
                        c.step(dve.memset(sums[:], 0.0))
                        dve.wait_ge(decay_ready, k + 2)
                    else:
                        dve.wait_ge(decay_ready, k + 2)
                        c.step(dve.tensor_tensor(sums[:], sums[:], decay[:].unsqueeze(1).broadcast_to([P, 2, C2]), ALU.mult))
                    weighted(k)

                k_reg, later_reg = dve.alloc_register("att_dve_k"), dve.alloc_register("att_dve_later")
                dve.reg_mov(k_reg, 0)
                rest1(0)
                rest2(0)
                dve.reg_mov(later_reg, 0)
                with dve.Fori(0, TILES) as t:
                    k = dve.snap(k_reg)
                    cf = Chain(dve, chain_f, t * FIRST_STEPS)
                    step(cf, k, True, t)
                    assert cf.n == FIRST_STEPS, cf.n
                    dve.reg_add(k_reg, k_reg, 1)
                    chunks = dve.value_load(g.loops[0:1, bass.ds(t, 1)], min_val=2, max_val=E)
                    with dve.Fori(1, chunks):
                        k = dve.snap(k_reg)
                        cl = Chain(dve, chain_l, dve.snap(later_reg) * LATER_STEPS)
                        step(cl, k, False, t)
                        assert cl.n == LATER_STEPS, cl.n
                        dve.reg_add(k_reg, k_reg, 1)
                        dve.reg_add(later_reg, later_reg, 1)
                c = Chain(dve, chain0, before)
                add_sums(c, dve.snap(k_reg))
                finish(c, slice(TILES, TILES + 1))
                c.step(dve.tensor_tensor(ft[:, 1:, :], ft[:, 1:, :], g.x[:], ALU.add))
                assert before + c.n == END_STEPS, before + c.n


FIRST_STEPS = 4 + 3 + 9 + 4 + 1
LATER_STEPS = 2 + 3 + 9 + 1
END_STEPS = 5 + 3 + 1 + 4 + 1


class Shared:
    pass


def build(nc, ins, out, debug=None, stages=99):
    g = Shared()
    debug = debug or {}
    with ExitStack() as ctx:
        s = Scope(nc, ctx, "all")
        g.src_d = nc.dram_tensor("src_pad", (EP,), I32).ap()
        g.dst_d = nc.dram_tensor("dst_pad", (EP,), I32).ap()
        g.first_d = nc.dram_tensor("first_pad", (NP + 1,), F32).ap()
        g.ea_d = nc.dram_tensor("ea_pad", (EA_ROWS, D), F32).ap()
        g.key_d = nc.dram_tensor("rank_keys", (NP,), F32).ap()
        g.info_d = nc.dram_tensor("rank_info", (NP, 4), F32).ap()
        g.table_d = nc.dram_tensor("sheaf_table", (NP, OWN), F32).ap()
        g.h_d = nc.dram_tensor("h_table", (NP, D), F32).ap()
        g.const = s.sb("const", [P, C_END])
        g.eye_bf = s.sb("eye_bf", [P, P], BF16)
        g.iota_bf = s.sb("iota_bf", [P, P], BF16)
        g.x = s.sb("x", [P, TILES, D])
        g.h = s.sb("h", [P, TILES, D])
        g.first = s.sb("first", [P, TILES])
        g.deg = s.sb("deg", [P, TILES])
        g.first_s, g.deg_s = s.sb("first_s", [P, TILES]), s.sb("deg_s", [P, TILES])
        g.node_i = s.sb("node_i", [P, TILES], I32)
        g.rank_parts = s.sb("rank_parts", [P, TILES, 2])
        g.outs = s.sb("outs", [P, TILES])
        g.dinv2 = s.sb("dinv2", [P, TILES])
        g.mean, g.root_in = s.sb("mean", [P, TILES]), s.sb("root_in", [P, TILES])
        g.centred, g.squares = s.sb("centred", [P, TILES, D]), s.sb("squares", [P, TILES, D])
        g.loops = s.sb("loops", [1, TILES + 2], I32)
        stage_pad(nc, g, ins)
        stage_offsets(nc, g)
        stage_order(nc, g)
        with nc.sbuf_tensor("A", [P, TILES, NP], BF16) as A:
            g.A = A
            stage_adjacency(nc, g, ins)
            stage_more_windows(nc, g)
            if "A" in debug:
                dump(nc, [(debug["A"], A[:, :, :])])
            stage_layers01(nc, g, ins)
        if "x1" in debug:
            dump(nc, [(debug["x1"], g.x[:]), (debug["outs"], g.outs[:]), (debug["deg"], g.deg[:])])
        stage_sheaf(nc, g, ins)
        if "x2" in debug:
            dump(nc, [(debug["x2"], g.x[:]), (debug["h2"], g.h[:])])
        stage_attention(nc, g, ins, out)


def dump(nc, pairs):
    with nc.semaphore() as sem, nc.Block() as block:
        @block.sync
        def _(sp):
            for o, i in pairs:
                sp.dma_start(o, i).then_inc(sem, 16)
            sp.wait_ge(sem, 16 * len(pairs))


_INS = ["x", "src", "dst", "edge_attr_16", "L0_gnn_W1_l", "L0_gnn_b1", "L0_gnn_W1_r", "L0_gnn_W2_l", "L0_gnn_b2",
        "L0_gnn_W2_r", "L1_gnn_W1", "L1_gnn_b1", "L1_gnn_W2", "L1_gnn_b2", "L1_gnn_W3", "L1_gnn_b3", "L1_gnn_Wl1",
        "L1_gnn_bl1", "L1_gnn_Wl2", "L1_gnn_bl2", "L1_gnn_Wl3", "L1_gnn_bl3", "L2_gnn_W1", "L2_gnn_b1", "L2_gnn_W2",
        "L2_gnn_b2", "L3_gnn_W_msg", "L3_gnn_b_msg", "L3_gnn_W_attn", "L3_gnn_b_attn"]


def kernel(**inputs):
    import concourse.bacc as bacc
    from concourse.bass_utils import run_bass_kernel_spmd

    nc = bacc.Bacc("TRN2", target_bir_lowering=False, num_devices=1)
    arrays = {name: np.ascontiguousarray(inputs[name]) for name in _INS}
    arrays["constants"] = constants()
    ins = {name: nc.dram_tensor(f"in_{name}", a.shape, mybir.dt.from_np(a.dtype), kind="ExternalInput").ap()
           for name, a in arrays.items()}
    out = nc.dram_tensor("out", (N, D), F32, kind="ExternalOutput").ap()
    build(nc, ins, out)
    result = run_bass_kernel_spmd(nc, [{f"in_{name}": a for name, a in arrays.items()}], core_ids=[0])
    return result.results[0]["out"]
```
